# Optimizing a Trainium2 kernel written in Bass

```python
import numpy as np
import jax
import jax.numpy as jnp

def _softmax(x, axis=-1):
    return jax.nn.softmax(x, axis=axis)

def _gelu(x):
    return jax.nn.gelu(x, approximate=True)

def _silu(x):
    return jax.nn.silu(x)

def _sigmoid(x):
    return jax.nn.sigmoid(x)

def _layernorm(x, axis=-1, eps=1e-05):
    m = jnp.mean(x, axis=axis, keepdims=True)
    v = jnp.var(x, axis=axis, keepdims=True)
    return (x - m) / jnp.sqrt(v + eps)

def _scatter_add(tgt, idx, src, axis=0):
    return tgt.at[idx].add(src)

def _segment_sum(src, seg, n):
    return jax.ops.segment_sum(src, seg, n)
kernel_name = 'mk_prb_d4_jaxref_r8_6595e9'

def setup_inputs(seed: int=0):
    np.random.seed(seed)
    _w = jnp.asarray

    def _L0_attn_setup():
        import jax, jax.numpy as jnp
        import numpy as np
        N_HEAD = 16
        D_K = 64
        D_V = 64
        EMBED = 128
        BATCH = 4
        SEQ = 256
        key = jax.random.key(seed)
        ks = jax.random.split(key, 12)
        s = lambda d: 1.0 / np.sqrt(d)
        u = lambda k, shape, d: jax.random.uniform(k, shape, jnp.float32, -s(d), s(d))
        return {'z': jax.random.normal(ks[0], (BATCH, SEQ, EMBED), jnp.float32), 'wq': u(ks[1], (EMBED, D_K), D_K), 'wk': u(ks[2], (EMBED, D_K), D_K), 'wv': u(ks[3], (EMBED, D_V), D_V), 'fcq_w': u(ks[4], (D_K, N_HEAD * D_K), D_K), 'fcq_b': u(ks[5], (N_HEAD * D_K,), N_HEAD * D_K), 'fck_w': u(ks[6], (D_K, N_HEAD * D_K), D_K), 'fck_b': u(ks[7], (N_HEAD * D_K,), N_HEAD * D_K), 'fcv_w': u(ks[8], (D_V, N_HEAD * D_V), D_V), 'fcv_b': u(ks[9], (N_HEAD * D_V,), N_HEAD * D_V), 'fco_w': u(ks[10], (N_HEAD * D_V, EMBED), EMBED), 'fco_b': u(ks[11], (EMBED,), EMBED)}
    _L0_attn_in = _L0_attn_setup()

    def _L0_ffn_setup():
        import jax, jax.numpy as jnp
        import numpy as np
        DIM = 128
        HEADS = 8
        DH = 64
        HDH = HEADS * DH
        SEQ = 1024
        BATCH = 2
        WIN = 64
        N_ITERS = 50
        EPS = 1.0
        NQ = 128
        NKV = 256
        FETCH_K = 9.0 / 8.0

        def rmsnorm(x, g):
            n = jnp.maximum(jnp.sqrt(jnp.sum(x * x, axis=-1, keepdims=True)), 1e-12)
            return x / n * DIM ** 0.5 * g

        def layernorm(x, g, b):
            m = jnp.mean(x, axis=-1, keepdims=True)
            v = jnp.mean((x - m) ** 2, axis=-1, keepdims=True)
            return (x - m) / jnp.sqrt(v + 1e-05) * g + b

        def coor_descent(s, k_eff):
            logk = jnp.log(jnp.float32(k_eff))

            def body(carry, _):
                a, b = carry
                sb = (s + b) / EPS
                a = EPS * (logk - jax.nn.logsumexp(sb, axis=-1, keepdims=True))
                b = -jax.nn.relu(s + a)
                return ((a, b), None)
            init = (jnp.zeros_like(s[..., :1]), -s)
            (a, b), _ = jax.lax.scan(body, init, None, length=N_ITERS)
            return jnp.exp((s + a + b) / EPS)

        def route(x, routing_token, num_tokens, k_eff):
            s = jnp.einsum('bnd,rd->brn', x, routing_token)[:, 0]
            scores = coor_descent(s, k_eff)
            sel_scores, sel_idx = jax.lax.top_k(scores, num_tokens)
            sel_scores = sel_scores + jax.lax.stop_gradient(1.0 - sel_scores)
            return (sel_scores, sel_idx)

        def light_attn(x, ln_g, ln_b, w_qkv, w_out):
            b, n, _ = x.shape
            xn = layernorm(x, ln_g, ln_b)
            q, k, v = jnp.split(xn @ w_qkv, 3, axis=-1)

            def towin(t):
                return t.reshape(b, n // WIN, WIN, HEADS, DH).transpose(0, 3, 1, 2, 4)
            q, k, v = (towin(q), towin(k), towin(v))

            def around(t):
                pad = jnp.pad(t, ((0, 0), (0, 0), (1, 1), (0, 0), (0, 0)))
                return jnp.concatenate([pad[:, :, :-2], pad[:, :, 1:-1], pad[:, :, 2:]], axis=3)
            kk, vv = (around(k), around(v))
            nw = n // WIN
            wvalid = jnp.pad(jnp.ones((nw,), bool), (1, 1))
            kmask = jnp.concatenate([jnp.repeat(wvalid[:-2, None], WIN, 1), jnp.repeat(wvalid[1:-1, None], WIN, 1), jnp.repeat(wvalid[2:, None], WIN, 1)], axis=1)
            sim = jnp.einsum('bhnwd,bhnWd->bhnwW', q * DH ** (-0.5), kk)
            sim = jnp.where(kmask[None, None, :, None, :], sim, -jnp.finfo(sim.dtype).max)
            attn = jax.nn.softmax(sim, axis=-1)
            o = jnp.einsum('bhnwW,bhnWd->bhnwd', attn, vv)
            o = o.transpose(0, 2, 3, 1, 4).reshape(b, n, HDH)
            return o @ w_out

        def heavy_attn(xq, ctx, scores_kv, rms_g, w_q, w_kv, null_kv, w_out):
            b = xq.shape[0]
            xq = rmsnorm(xq, rms_g)
            ctx = rmsnorm(ctx, rms_g)
            q = (xq @ w_q).reshape(b, -1, HEADS, DH).transpose(0, 2, 1, 3)
            kv = jnp.einsum('bni,ihd->bhnd', ctx, w_kv)
            k, v = (kv[..., :DH], kv[..., DH:])
            v = v * scores_kv[:, None, :, None]
            nk = jnp.broadcast_to(null_kv[0][None, :, None, :], (b, HEADS, 1, DH))
            nv = jnp.broadcast_to(null_kv[1][None, :, None, :], (b, HEADS, 1, DH))
            k = jnp.concatenate([nk, k], axis=2)
            v = jnp.concatenate([nv, v], axis=2)
            sim = jnp.einsum('bhqd,bhkd->bhqk', q * DH ** (-0.5), k)
            attn = jax.nn.softmax(sim, axis=-1)
            o = jnp.einsum('bhqk,bhkd->bhqd', attn, v)
            o = o.transpose(0, 2, 1, 3).reshape(b, -1, HDH)
            return o @ w_out

        def forward(x, ln_g, ln_b, w_qkv_l, w_out_l, null_q, rt_q, rt_kv, rms_g, w_q_h, w_kv_h, null_kv, w_out_h):
            light = light_attn(x, ln_g, ln_b, w_qkv_l, w_out_l)
            sq, iq = route(x, rt_q, NQ, min(NQ * FETCH_K, SEQ))
            skv, ikv = route(x, rt_kv, NKV, min(NKV * FETCH_K, SEQ))
            batch_idx = jnp.arange(x.shape[0])[:, None]
            xq = x[batch_idx, iq]
            xkv = x[batch_idx, ikv]
            routed_out = heavy_attn(xq, xkv, skv, rms_g, w_q_h, w_kv_h, null_kv, w_out_h)
            routed_out = routed_out * sq[..., None]
            out = jnp.broadcast_to(null_q, x.shape)
            out = out.at[batch_idx, iq].set(routed_out)
            return light + out
        key = jax.random.key(seed)
        ks = jax.random.split(key, 10)
        p = lambda i, shape: jax.random.normal(ks[i], shape, jnp.float32) * 0.02
        return dict(x=jax.random.normal(ks[0], (BATCH, SEQ, DIM), jnp.float32), ln_g=jnp.ones((DIM,), jnp.float32), ln_b=jnp.zeros((DIM,), jnp.float32), w_qkv_l=p(1, (DIM, 3 * HDH)), w_out_l=p(2, (HDH, DIM)), null_q=jax.random.normal(ks[3], (DIM,), jnp.float32), rt_q=jax.random.normal(ks[4], (1, DIM), jnp.float32), rt_kv=jax.random.normal(ks[5], (1, DIM), jnp.float32), rms_g=jnp.ones((DIM,), jnp.float32), w_q_h=p(6, (DIM, HDH)), w_kv_h=p(7, (DIM, HEADS, 2 * DH)), null_kv=jax.random.normal(ks[8], (2, HEADS, DH), jnp.float32), w_out_h=p(9, (HDH, DIM)))
    _L0_ffn_in = _L0_ffn_setup()

    def _L1_attn_setup():
        import jax, jax.numpy as jnp
        import numpy as np
        B, N, D = (2, 256, 128)
        H, FD, HD = (16, 16, 64)
        ENC = 64
        EPS = 1e-12
        RD = 4.0
        RRD = 2.0
        R2 = float(np.sqrt(2.0))

        def taylor_exp(x):
            x2 = (x[..., :, None] * x[..., None, :]).reshape(*x.shape[:-1], FD * FD) / R2
            return jnp.concatenate([jnp.ones_like(x[..., :1]), x / RRD, x2 / RD], axis=-1)
        key = jax.random.key(seed)
        ks = jax.random.split(key, 7)
        s = 1.0 / np.sqrt(D)
        x = jax.random.normal(ks[0], (B, N, D), dtype=jnp.float32)
        Wq = jax.random.normal(ks[1], (H * FD, D), dtype=jnp.float32) * s
        Wk = jax.random.normal(ks[2], (H * FD, D), dtype=jnp.float32) * s
        Wv = jax.random.normal(ks[3], (H * HD, D), dtype=jnp.float32) * s
        Wk_enc = jax.random.normal(ks[4], (H * FD, D), dtype=jnp.float32) * s
        Wv_enc = jax.random.normal(ks[5], (H * HD, D), dtype=jnp.float32) * s
        Wout = jax.random.normal(ks[6], (D, H * HD), dtype=jnp.float32) * s
        return {'x': x, 'Wq': Wq, 'Wk': Wk, 'Wv': Wv, 'Wk_enc': Wk_enc, 'Wv_enc': Wv_enc, 'Wout': Wout}
    _L1_attn_in = _L1_attn_setup()

    def _L1_ffn_setup():
        import jax, jax.numpy as jnp
        import numpy as np
        B, S, D = (4, 256, 128)
        E, K = (8, 2)
        H = 176
        key = jax.random.key(seed)
        kx, kr, k1, k2, k3 = jax.random.split(key, 5)
        s = 0.02
        return {'x': jax.random.normal(kx, (B, S, D), dtype=jnp.float32), 'w_router': jax.random.normal(kr, (E, D), dtype=jnp.float32) * s, 'w1': jax.random.normal(k1, (E, D, H), dtype=jnp.float32) * s, 'w2': jax.random.normal(k2, (E, H, D), dtype=jnp.float32) * s, 'w3': jax.random.normal(k3, (E, D, H), dtype=jnp.float32) * s}
    _L1_ffn_in = _L1_ffn_setup()

    def _L2_attn_setup():
        import jax, jax.numpy as jnp
        import numpy as np
        NUM_HEADS = 16

        def _rope_cos_sin(n, head_dim, dtype):
            inv_freq = 1.0 / 10000.0 ** (jnp.arange(0, head_dim, 2, dtype=jnp.float32) / head_dim)
            t = jnp.arange(n, dtype=jnp.float32)
            freqs = t[:, None] * inv_freq[None, :]
            return (jnp.cos(freqs).astype(dtype), jnp.sin(freqs).astype(dtype))

        def _apply_rope(x, cos, sin):
            x1, x2 = (x[..., ::2], x[..., 1::2])
            return jnp.concatenate([x1 * cos - x2 * sin, x2 * cos + x1 * sin], axis=-1)
        key = jax.random.key(seed)
        k1, k2, k3 = jax.random.split(key, 3)
        B, N, C = (2, 256, 128)
        x = jax.random.normal(k1, (B, N, C), dtype=jnp.float32)
        w_qkv = jax.random.normal(k2, (3 * C, C), dtype=jnp.float32) * C ** (-0.5)
        w_proj = jax.random.normal(k3, (C, C), dtype=jnp.float32) * C ** (-0.5)
        b_proj = jnp.zeros((C,), dtype=jnp.float32)
        return {'x': x, 'w_qkv': w_qkv, 'w_proj': w_proj, 'b_proj': b_proj}
    _L2_attn_in = _L2_attn_setup()

    def _L2_ffn_setup():
        import jax, jax.numpy as jnp
        import numpy as np
        B, S, H, E, F = (2, 256, 128, 8, 512)
        key = jax.random.key(seed)
        k1, k2, k3, k4 = jax.random.split(key, 4)
        h = jax.random.normal(k1, (B, S, H), dtype=jnp.float32)
        Wr = jax.random.normal(k2, (H, E), dtype=jnp.float32) / np.sqrt(H)
        W1 = jax.random.normal(k3, (E, H, F), dtype=jnp.float32) / np.sqrt(H)
        W2 = jax.random.normal(k4, (E, F, H), dtype=jnp.float32) / np.sqrt(F)
        return {'h': h, 'Wr': Wr, 'W1': W1, 'W2': W2}
    _L2_ffn_in = _L2_ffn_setup()

    def _L3_attn_setup():
        import jax, jax.numpy as jnp
        import numpy as np
        D_MODEL = 128
        D_STATE = 16
        D_CONV = 4
        EXPAND = 2
        D_INNER = D_MODEL * EXPAND

        def _forward(x, W_in, conv_w, conv_b, W_x, A_log, D_param, W_dt, b_dt, W_out):
            B, L, _ = x.shape
            xz = x @ W_in.T
            x_ssm, z = jnp.split(xz, 2, axis=-1)
            xc = jnp.transpose(x_ssm, (0, 2, 1))
            xc = jax.lax.conv_general_dilated(xc, conv_w, window_strides=(1,), padding=[(D_CONV - 1, 0)], feature_group_count=D_INNER, dimension_numbers=('NCH', 'OIH', 'NCH'))
            xc = xc + conv_b[None, :, None]
            x_ssm = jax.nn.silu(jnp.transpose(xc, (0, 2, 1)))
            proj = x_ssm @ W_x.T
            B_ssm = proj[..., :D_STATE]
            C_ssm = proj[..., D_STATE:2 * D_STATE]
            dt = jax.nn.softplus(proj[..., -1:] * W_dt[:, 0] + b_dt)
            A = -jnp.exp(A_log)

            def step(h, inp):
                dt_t, Bt, Ct, xt = inp
                dA = jnp.exp(dt_t[..., None] * A)
                h = dA * h + (xt * dt_t)[..., None] * Bt[:, None, :]
                y = jnp.einsum('bdn,bn->bd', h, Ct)
                return (h, y)
            h0 = jnp.zeros((B, D_INNER, D_STATE), x.dtype)
            inputs = (jnp.transpose(dt, (1, 0, 2)), jnp.transpose(B_ssm, (1, 0, 2)), jnp.transpose(C_ssm, (1, 0, 2)), jnp.transpose(x_ssm, (1, 0, 2)))
            _, ys = jax.lax.scan(step, h0, inputs)
            y = jnp.transpose(ys, (1, 0, 2)) + x_ssm * D_param
            y = y * jax.nn.silu(z)
            return y @ W_out.T
        key = jax.random.key(seed)
        ks = jax.random.split(key, 10)
        B, L = (2, 256)
        x = jax.random.normal(ks[0], (B, L, D_MODEL), jnp.float32)
        W_in = jax.random.normal(ks[1], (2 * D_INNER, D_MODEL), jnp.float32) * (1.0 / np.sqrt(D_MODEL))
        conv_w = jax.random.normal(ks[2], (D_INNER, 1, D_CONV), jnp.float32) * (1.0 / np.sqrt(D_CONV))
        conv_b = jax.random.normal(ks[3], (D_INNER,), jnp.float32) * 0.1
        W_x = jax.random.normal(ks[4], (2 * D_STATE + 1, D_INNER), jnp.float32) * (1.0 / np.sqrt(D_INNER))
        A_log = jnp.log(jnp.abs(jax.random.normal(ks[5], (D_INNER, D_STATE), jnp.float32)) + 0.0001)
        D_param = jnp.ones((D_INNER,), jnp.float32)
        W_dt = jax.random.normal(ks[6], (D_INNER, 1), jnp.float32)
        b_dt = jax.random.normal(ks[7], (D_INNER,), jnp.float32) * 0.1
        W_out = jax.random.normal(ks[8], (D_MODEL, D_INNER), jnp.float32) * (1.0 / np.sqrt(D_INNER))
        return {'x': x, 'W_in': W_in, 'conv_w': conv_w, 'conv_b': conv_b, 'W_x': W_x, 'A_log': A_log, 'D_param': D_param, 'W_dt': W_dt, 'b_dt': b_dt, 'W_out': W_out}
    _L3_attn_in = _L3_attn_setup()

    def _L3_ffn_setup():
        import jax, jax.numpy as jnp
        import numpy as np
        GROUP = 16
        EPS = 1e-05

        def _dequant(q, scale):
            w = q.astype(jnp.float32) / 7.5 - 1.0
            return w * jnp.repeat(scale, GROUP, axis=1)

        def _qlora_linear(x, q, scale, bias, la, lb):
            w = _dequant(q, scale)
            base = jnp.einsum('btd,od->bto', x, w) + bias
            lora = jnp.einsum('btr,or->bto', jnp.einsum('btd,rd->btr', x, la), lb)
            return base + lora

        def _layernorm(x, g, b):
            mu = jnp.mean(x, axis=-1, keepdims=True)
            var = jnp.mean(jnp.square(x - mu), axis=-1, keepdims=True)
            return (x - mu) * jax.lax.rsqrt(var + EPS) * g + b
        key = jax.random.key(seed)
        ks = jax.random.split(key, 6)
        D, R, B, T = (128, 32, 8, 512)
        x = jax.random.normal(ks[0], (B, T, D), dtype=jnp.float32)
        qweights = jax.random.randint(ks[1], (6, D, D), 0, 16, dtype=jnp.int32)
        scales = jax.random.uniform(ks[2], (6, D, D // GROUP), dtype=jnp.float32)
        biases = jax.random.normal(ks[3], (6, D), dtype=jnp.float32) * 0.02
        lora_a = jax.random.normal(ks[4], (6, R, D), dtype=jnp.float32) * 0.02
        lora_b = jax.random.normal(ks[5], (6, D, R), dtype=jnp.float32) * 0.02
        ln_gamma = jnp.ones((3, D), dtype=jnp.float32)
        ln_beta = jnp.zeros((3, D), dtype=jnp.float32)
        return {'x': x, 'qweights': qweights, 'scales': scales, 'biases': biases, 'lora_a': lora_a, 'lora_b': lora_b, 'ln_gamma': ln_gamma, 'ln_beta': ln_beta}
    _L3_ffn_in = _L3_ffn_setup()
    _d = {'L0_attn_z': _L0_attn_in['z'], 'L0_attn_wq': _L0_attn_in['wq'], 'L0_attn_wk': _L0_attn_in['wk'], 'L0_attn_wv': _L0_attn_in['wv'], 'L0_attn_fcq_w': _L0_attn_in['fcq_w'], 'L0_attn_fcq_b': _L0_attn_in['fcq_b'], 'L0_attn_fck_w': _L0_attn_in['fck_w'], 'L0_attn_fck_b': _L0_attn_in['fck_b'], 'L0_attn_fcv_w': _L0_attn_in['fcv_w'], 'L0_attn_fcv_b': _L0_attn_in['fcv_b'], 'L0_attn_fco_w': _L0_attn_in['fco_w'], 'L0_attn_fco_b': _L0_attn_in['fco_b'], 'L0_ffn_ln_g': _L0_ffn_in['ln_g'], 'L0_ffn_ln_b': _L0_ffn_in['ln_b'], 'L0_ffn_w_qkv_l': _L0_ffn_in['w_qkv_l'], 'L0_ffn_w_out_l': _L0_ffn_in['w_out_l'], 'L0_ffn_null_q': _L0_ffn_in['null_q'], 'L0_ffn_rt_q': _L0_ffn_in['rt_q'], 'L0_ffn_rt_kv': _L0_ffn_in['rt_kv'], 'L0_ffn_rms_g': _L0_ffn_in['rms_g'], 'L0_ffn_w_q_h': _L0_ffn_in['w_q_h'], 'L0_ffn_w_kv_h': _L0_ffn_in['w_kv_h'], 'L0_ffn_null_kv': _L0_ffn_in['null_kv'], 'L0_ffn_w_out_h': _L0_ffn_in['w_out_h'], 'L1_attn_Wq': _L1_attn_in['Wq'], 'L1_attn_Wk': _L1_attn_in['Wk'], 'L1_attn_Wv': _L1_attn_in['Wv'], 'L1_attn_Wk_enc': _L1_attn_in['Wk_enc'], 'L1_attn_Wv_enc': _L1_attn_in['Wv_enc'], 'L1_attn_Wout': _L1_attn_in['Wout'], 'L1_ffn_w_router': _L1_ffn_in['w_router'], 'L1_ffn_w1': _L1_ffn_in['w1'], 'L1_ffn_w2': _L1_ffn_in['w2'], 'L1_ffn_w3': _L1_ffn_in['w3'], 'L2_attn_w_qkv': _L2_attn_in['w_qkv'], 'L2_attn_w_proj': _L2_attn_in['w_proj'], 'L2_attn_b_proj': _L2_attn_in['b_proj'], 'L2_ffn_Wr': _L2_ffn_in['Wr'], 'L2_ffn_W1': _L2_ffn_in['W1'], 'L2_ffn_W2': _L2_ffn_in['W2'], 'L3_attn_W_in': _L3_attn_in['W_in'], 'L3_attn_conv_w': _L3_attn_in['conv_w'], 'L3_attn_conv_b': _L3_attn_in['conv_b'], 'L3_attn_W_x': _L3_attn_in['W_x'], 'L3_attn_A_log': _L3_attn_in['A_log'], 'L3_attn_D_param': _L3_attn_in['D_param'], 'L3_attn_W_dt': _L3_attn_in['W_dt'], 'L3_attn_b_dt': _L3_attn_in['b_dt'], 'L3_attn_W_out': _L3_attn_in['W_out'], 'L3_ffn_qweights': _L3_ffn_in['qweights'], 'L3_ffn_scales': _L3_ffn_in['scales'], 'L3_ffn_biases': _L3_ffn_in['biases'], 'L3_ffn_lora_a': _L3_ffn_in['lora_a'], 'L3_ffn_lora_b': _L3_ffn_in['lora_b'], 'L3_ffn_ln_gamma': _L3_ffn_in['ln_gamma'], 'L3_ffn_ln_beta': _L3_ffn_in['ln_beta']}
    _x0 = _d['L0_attn_z']
    _d['L0_attn_z'] = jax.random.normal(jax.random.fold_in(jax.random.key(seed), 1), (8, 256, 128), dtype=_x0.dtype)
    del _x0
    return _d

def reference(L0_attn_z, L0_attn_wq, L0_attn_wk, L0_attn_wv, L0_attn_fcq_w, L0_attn_fcq_b, L0_attn_fck_w, L0_attn_fck_b, L0_attn_fcv_w, L0_attn_fcv_b, L0_attn_fco_w, L0_attn_fco_b, L0_ffn_ln_g, L0_ffn_ln_b, L0_ffn_w_qkv_l, L0_ffn_w_out_l, L0_ffn_null_q, L0_ffn_rt_q, L0_ffn_rt_kv, L0_ffn_rms_g, L0_ffn_w_q_h, L0_ffn_w_kv_h, L0_ffn_null_kv, L0_ffn_w_out_h, L1_attn_Wq, L1_attn_Wk, L1_attn_Wv, L1_attn_Wk_enc, L1_attn_Wv_enc, L1_attn_Wout, L1_ffn_w_router, L1_ffn_w1, L1_ffn_w2, L1_ffn_w3, L2_attn_w_qkv, L2_attn_w_proj, L2_attn_b_proj, L2_ffn_Wr, L2_ffn_W1, L2_ffn_W2, L3_attn_W_in, L3_attn_conv_w, L3_attn_conv_b, L3_attn_W_x, L3_attn_A_log, L3_attn_D_param, L3_attn_W_dt, L3_attn_b_dt, L3_attn_W_out, L3_ffn_qweights, L3_ffn_scales, L3_ffn_biases, L3_ffn_lora_a, L3_ffn_lora_b, L3_ffn_ln_gamma, L3_ffn_ln_beta):

    def _L0_attn_ref(z, wq, wk, wv, fcq_w, fcq_b, fck_w, fck_b, fcv_w, fcv_b, fco_w, fco_b):
        import jax, jax.numpy as jnp
        import numpy as np
        N_HEAD = 16
        D_K = 64
        D_V = 64
        EMBED = 128
        BATCH = 4
        SEQ = 256
        b, n, _ = z.shape
        scale = jnp.sqrt(jnp.float32(D_K))
        q = z @ wq @ fcq_w + fcq_b
        k = z @ wk @ fck_w + fck_b
        v = z @ wv @ fcv_w + fcv_b
        q = q.reshape(b, n, N_HEAD, D_K)
        k = k.reshape(b, n, N_HEAD, D_K)
        v = v.reshape(b, n, N_HEAD, D_V)
        scores = jnp.einsum('bihd,bjhd->bhij', q, k) / scale
        attn = jax.nn.softmax(scores, axis=-1)
        out = jnp.einsum('bhij,bjhd->bihd', attn, v)
        out = out.reshape(b, n, N_HEAD * D_V)
        return out @ fco_w + fco_b

    def _L0_ffn_ref(x, ln_g, ln_b, w_qkv_l, w_out_l, null_q, rt_q, rt_kv, rms_g, w_q_h, w_kv_h, null_kv, w_out_h):
        import jax, jax.numpy as jnp
        import numpy as np
        DIM = 128
        HEADS = 8
        DH = 64
        HDH = HEADS * DH
        SEQ = 1024
        BATCH = 2
        WIN = 64
        N_ITERS = 50
        EPS = 1.0
        NQ = 128
        NKV = 256
        FETCH_K = 9.0 / 8.0

        def rmsnorm(x, g):
            n = jnp.maximum(jnp.sqrt(jnp.sum(x * x, axis=-1, keepdims=True)), 1e-12)
            return x / n * DIM ** 0.5 * g

        def layernorm(x, g, b):
            m = jnp.mean(x, axis=-1, keepdims=True)
            v = jnp.mean((x - m) ** 2, axis=-1, keepdims=True)
            return (x - m) / jnp.sqrt(v + 1e-05) * g + b

        def coor_descent(s, k_eff):
            logk = jnp.log(jnp.float32(k_eff))

            def body(carry, _):
                a, b = carry
                sb = (s + b) / EPS
                a = EPS * (logk - jax.nn.logsumexp(sb, axis=-1, keepdims=True))
                b = -jax.nn.relu(s + a)
                return ((a, b), None)
            init = (jnp.zeros_like(s[..., :1]), -s)
            (a, b), _ = jax.lax.scan(body, init, None, length=N_ITERS)
            return jnp.exp((s + a + b) / EPS)

        def route(x, routing_token, num_tokens, k_eff):
            s = jnp.einsum('bnd,rd->brn', x, routing_token)[:, 0]
            scores = coor_descent(s, k_eff)
            sel_scores, sel_idx = jax.lax.top_k(scores, num_tokens)
            sel_scores = sel_scores + jax.lax.stop_gradient(1.0 - sel_scores)
            return (sel_scores, sel_idx)

        def light_attn(x, ln_g, ln_b, w_qkv, w_out):
            b, n, _ = x.shape
            xn = layernorm(x, ln_g, ln_b)
            q, k, v = jnp.split(xn @ w_qkv, 3, axis=-1)

            def towin(t):
                return t.reshape(b, n // WIN, WIN, HEADS, DH).transpose(0, 3, 1, 2, 4)
            q, k, v = (towin(q), towin(k), towin(v))

            def around(t):
                pad = jnp.pad(t, ((0, 0), (0, 0), (1, 1), (0, 0), (0, 0)))
                return jnp.concatenate([pad[:, :, :-2], pad[:, :, 1:-1], pad[:, :, 2:]], axis=3)
            kk, vv = (around(k), around(v))
            nw = n // WIN
            wvalid = jnp.pad(jnp.ones((nw,), bool), (1, 1))
            kmask = jnp.concatenate([jnp.repeat(wvalid[:-2, None], WIN, 1), jnp.repeat(wvalid[1:-1, None], WIN, 1), jnp.repeat(wvalid[2:, None], WIN, 1)], axis=1)
            sim = jnp.einsum('bhnwd,bhnWd->bhnwW', q * DH ** (-0.5), kk)
            sim = jnp.where(kmask[None, None, :, None, :], sim, -jnp.finfo(sim.dtype).max)
            attn = jax.nn.softmax(sim, axis=-1)
            o = jnp.einsum('bhnwW,bhnWd->bhnwd', attn, vv)
            o = o.transpose(0, 2, 3, 1, 4).reshape(b, n, HDH)
            return o @ w_out

        def heavy_attn(xq, ctx, scores_kv, rms_g, w_q, w_kv, null_kv, w_out):
            b = xq.shape[0]
            xq = rmsnorm(xq, rms_g)
            ctx = rmsnorm(ctx, rms_g)
            q = (xq @ w_q).reshape(b, -1, HEADS, DH).transpose(0, 2, 1, 3)
            kv = jnp.einsum('bni,ihd->bhnd', ctx, w_kv)
            k, v = (kv[..., :DH], kv[..., DH:])
            v = v * scores_kv[:, None, :, None]
            nk = jnp.broadcast_to(null_kv[0][None, :, None, :], (b, HEADS, 1, DH))
            nv = jnp.broadcast_to(null_kv[1][None, :, None, :], (b, HEADS, 1, DH))
            k = jnp.concatenate([nk, k], axis=2)
            v = jnp.concatenate([nv, v], axis=2)
            sim = jnp.einsum('bhqd,bhkd->bhqk', q * DH ** (-0.5), k)
            attn = jax.nn.softmax(sim, axis=-1)
            o = jnp.einsum('bhqk,bhkd->bhqd', attn, v)
            o = o.transpose(0, 2, 1, 3).reshape(b, -1, HDH)
            return o @ w_out

        def forward(x, ln_g, ln_b, w_qkv_l, w_out_l, null_q, rt_q, rt_kv, rms_g, w_q_h, w_kv_h, null_kv, w_out_h):
            light = light_attn(x, ln_g, ln_b, w_qkv_l, w_out_l)
            sq, iq = route(x, rt_q, NQ, min(NQ * FETCH_K, SEQ))
            skv, ikv = route(x, rt_kv, NKV, min(NKV * FETCH_K, SEQ))
            batch_idx = jnp.arange(x.shape[0])[:, None]
            xq = x[batch_idx, iq]
            xkv = x[batch_idx, ikv]
            routed_out = heavy_attn(xq, xkv, skv, rms_g, w_q_h, w_kv_h, null_kv, w_out_h)
            routed_out = routed_out * sq[..., None]
            out = jnp.broadcast_to(null_q, x.shape)
            out = out.at[batch_idx, iq].set(routed_out)
            return light + out
        return forward(x, ln_g, ln_b, w_qkv_l, w_out_l, null_q, rt_q, rt_kv, rms_g, w_q_h, w_kv_h, null_kv, w_out_h)

    def _L1_attn_ref(x, Wq, Wk, Wv, Wk_enc, Wv_enc, Wout):
        import jax, jax.numpy as jnp
        import numpy as np
        B, N, D = (2, 256, 128)
        H, FD, HD = (16, 16, 64)
        ENC = 64
        EPS = 1e-12
        RD = 4.0
        RRD = 2.0
        R2 = float(np.sqrt(2.0))

        def taylor_exp(x):
            x2 = (x[..., :, None] * x[..., None, :]).reshape(*x.shape[:-1], FD * FD) / R2
            return jnp.concatenate([jnp.ones_like(x[..., :1]), x / RRD, x2 / RD], axis=-1)
        b, n, _ = x.shape
        q = (x @ Wq.T).reshape(b, n, H, FD).transpose(0, 2, 1, 3)
        k = (x @ Wk.T).reshape(b, n, H, FD).transpose(0, 2, 1, 3)
        v = (x @ Wv.T).reshape(b, n, H, HD).transpose(0, 2, 1, 3)
        x_enc = x[:, :ENC]
        k_enc = (x_enc @ Wk_enc.T).reshape(b, ENC, H, FD).transpose(0, 2, 1, 3)
        v_enc = (x_enc @ Wv_enc.T).reshape(b, ENC, H, HD).transpose(0, 2, 1, 3)
        k_enc_f = taylor_exp(k_enc)
        q_f = taylor_exp(q)
        k_f = taylor_exp(k)
        A_qk = jnp.einsum('bhnd,bhmd->bhnm', q_f, k_f)
        A_qk = jnp.tril(A_qk)
        y1 = jnp.einsum('bhnm,bhme->bhne', A_qk, v)
        A_qk2 = jnp.einsum('bhnd,bhmd->bhnm', q_f, k_enc_f)
        y2 = jnp.einsum('bhnm,bhme->bhne', A_qk2, v_enc)
        k_state = k_enc_f.sum(axis=2, keepdims=True) + jnp.cumsum(k_f, axis=2)
        z = 1.0 / ((q_f * k_state).sum(axis=-1) + EPS)
        out = (y1 + y2) * z[..., None]
        out = out.transpose(0, 2, 1, 3).reshape(b, n, H * HD)
        return out @ Wout.T

    def _L1_ffn_ref(x, w_router, w1, w2, w3):
        import jax, jax.numpy as jnp
        import numpy as np
        B, S, D = (4, 256, 128)
        E, K = (8, 2)
        H = 176
        bsz, seqlen, dim = x.shape
        xf = x.reshape(-1, dim)
        scores = jax.nn.softmax(xf @ w_router.T, axis=-1)
        expert_weights, expert_indices = jax.lax.top_k(scores, K)
        h = jax.nn.silu(jnp.einsum('td,edh->eth', xf, w1)) * jnp.einsum('td,edh->eth', xf, w3)
        y = jnp.einsum('eth,ehd->etd', h, w2)
        y_t = jnp.swapaxes(y, 0, 1)
        sel = jnp.take_along_axis(y_t, expert_indices[:, :, None], axis=1)
        out = jnp.sum(expert_weights[:, :, None] * sel, axis=1)
        return out.reshape(bsz, seqlen, dim)

    def _L2_attn_ref(x, w_qkv, w_proj, b_proj):
        import jax, jax.numpy as jnp
        import numpy as np
        NUM_HEADS = 16

        def _rope_cos_sin(n, head_dim, dtype):
            inv_freq = 1.0 / 10000.0 ** (jnp.arange(0, head_dim, 2, dtype=jnp.float32) / head_dim)
            t = jnp.arange(n, dtype=jnp.float32)
            freqs = t[:, None] * inv_freq[None, :]
            return (jnp.cos(freqs).astype(dtype), jnp.sin(freqs).astype(dtype))

        def _apply_rope(x, cos, sin):
            x1, x2 = (x[..., ::2], x[..., 1::2])
            return jnp.concatenate([x1 * cos - x2 * sin, x2 * cos + x1 * sin], axis=-1)
        B, N, C = x.shape
        H = NUM_HEADS
        D = C // H
        scale = D ** (-0.5)
        qkv = jnp.einsum('bnc,dc->bnd', x, w_qkv).reshape(B, N, 3, H, D)
        qkv = jnp.transpose(qkv, (2, 0, 3, 1, 4))
        q, k, v = (qkv[0], qkv[1], qkv[2])
        cos, sin = _rope_cos_sin(N, D, x.dtype)
        q = _apply_rope(q, cos, sin)
        k = _apply_rope(k, cos, sin)
        attn = jax.nn.softmax(jnp.einsum('bhqd,bhkd->bhqk', q, k) * scale, axis=-1)
        out = jnp.einsum('bhqk,bhkd->bhqd', attn, v)
        out = jnp.transpose(out, (0, 2, 1, 3)).reshape(B, N, C)
        return out @ w_proj.T + b_proj

    def _L2_ffn_ref(h, Wr, W1, W2):
        import jax, jax.numpy as jnp
        import numpy as np
        B, S, H, E, F = (2, 256, 128, 8, 512)
        g = jax.nn.softmax(h @ Wr, axis=-1)
        top2_w, top2_idx = jax.lax.top_k(g, 2)
        top2_w = top2_w / jnp.sum(top2_w, axis=-1, keepdims=True)
        hid = jax.nn.relu(jnp.einsum('bsh,ehf->bsef', h, W1))
        expert_out = jnp.einsum('bsef,efh->bseh', hid, W2)
        top2_out = jnp.take_along_axis(expert_out, top2_idx[..., None], axis=2)
        return jnp.sum(top2_out * top2_w[..., None], axis=2)

    def _L3_attn_ref(x, W_in, conv_w, conv_b, W_x, A_log, D_param, W_dt, b_dt, W_out):
        import jax, jax.numpy as jnp
        import numpy as np
        D_MODEL = 128
        D_STATE = 16
        D_CONV = 4
        EXPAND = 2
        D_INNER = D_MODEL * EXPAND

        def _forward(x, W_in, conv_w, conv_b, W_x, A_log, D_param, W_dt, b_dt, W_out):
            B, L, _ = x.shape
            xz = x @ W_in.T
            x_ssm, z = jnp.split(xz, 2, axis=-1)
            xc = jnp.transpose(x_ssm, (0, 2, 1))
            xc = jax.lax.conv_general_dilated(xc, conv_w, window_strides=(1,), padding=[(D_CONV - 1, 0)], feature_group_count=D_INNER, dimension_numbers=('NCH', 'OIH', 'NCH'))
            xc = xc + conv_b[None, :, None]
            x_ssm = jax.nn.silu(jnp.transpose(xc, (0, 2, 1)))
            proj = x_ssm @ W_x.T
            B_ssm = proj[..., :D_STATE]
            C_ssm = proj[..., D_STATE:2 * D_STATE]
            dt = jax.nn.softplus(proj[..., -1:] * W_dt[:, 0] + b_dt)
            A = -jnp.exp(A_log)

            def step(h, inp):
                dt_t, Bt, Ct, xt = inp
                dA = jnp.exp(dt_t[..., None] * A)
                h = dA * h + (xt * dt_t)[..., None] * Bt[:, None, :]
                y = jnp.einsum('bdn,bn->bd', h, Ct)
                return (h, y)
            h0 = jnp.zeros((B, D_INNER, D_STATE), x.dtype)
            inputs = (jnp.transpose(dt, (1, 0, 2)), jnp.transpose(B_ssm, (1, 0, 2)), jnp.transpose(C_ssm, (1, 0, 2)), jnp.transpose(x_ssm, (1, 0, 2)))
            _, ys = jax.lax.scan(step, h0, inputs)
            y = jnp.transpose(ys, (1, 0, 2)) + x_ssm * D_param
            y = y * jax.nn.silu(z)
            return y @ W_out.T
        return _forward(x, W_in, conv_w, conv_b, W_x, A_log, D_param, W_dt, b_dt, W_out)

    def _L3_ffn_ref(x, qweights, scales, biases, lora_a, lora_b, ln_gamma, ln_beta):
        import jax, jax.numpy as jnp
        import numpy as np
        GROUP = 16
        EPS = 1e-05

        def _dequant(q, scale):
            w = q.astype(jnp.float32) / 7.5 - 1.0
            return w * jnp.repeat(scale, GROUP, axis=1)

        def _qlora_linear(x, q, scale, bias, la, lb):
            w = _dequant(q, scale)
            base = jnp.einsum('btd,od->bto', x, w) + bias
            lora = jnp.einsum('btr,or->bto', jnp.einsum('btd,rd->btr', x, la), lb)
            return base + lora

        def _layernorm(x, g, b):
            mu = jnp.mean(x, axis=-1, keepdims=True)
            var = jnp.mean(jnp.square(x - mu), axis=-1, keepdims=True)
            return (x - mu) * jax.lax.rsqrt(var + EPS) * g + b
        h = x
        for blk in range(3):
            i0, i1 = (2 * blk, 2 * blk + 1)
            y = _qlora_linear(h, qweights[i0], scales[i0], biases[i0], lora_a[i0], lora_b[i0])
            y = _layernorm(y, ln_gamma[blk], ln_beta[blk])
            y = jax.nn.gelu(y, approximate=False)
            y = _qlora_linear(y, qweights[i1], scales[i1], biases[i1], lora_a[i1], lora_b[i1])
            h = y + h
        return h
    x = L0_attn_z
    xn = _layernorm(x, axis=-1)
    x = x + _L0_attn_ref(xn, L0_attn_wq, L0_attn_wk, L0_attn_wv, L0_attn_fcq_w, L0_attn_fcq_b, L0_attn_fck_w, L0_attn_fck_b, L0_attn_fcv_w, L0_attn_fcv_b, L0_attn_fco_w, L0_attn_fco_b) + _L0_ffn_ref(xn, L0_ffn_ln_g, L0_ffn_ln_b, L0_ffn_w_qkv_l, L0_ffn_w_out_l, L0_ffn_null_q, L0_ffn_rt_q, L0_ffn_rt_kv, L0_ffn_rms_g, L0_ffn_w_q_h, L0_ffn_w_kv_h, L0_ffn_null_kv, L0_ffn_w_out_h)
    xn = _layernorm(x, axis=-1)
    x = x + _L1_attn_ref(xn, L1_attn_Wq, L1_attn_Wk, L1_attn_Wv, L1_attn_Wk_enc, L1_attn_Wv_enc, L1_attn_Wout) + _L1_ffn_ref(xn, L1_ffn_w_router, L1_ffn_w1, L1_ffn_w2, L1_ffn_w3)
    xn = _layernorm(x, axis=-1)
    x = x + _L2_attn_ref(xn, L2_attn_w_qkv, L2_attn_w_proj, L2_attn_b_proj) + _L2_ffn_ref(xn, L2_ffn_Wr, L2_ffn_W1, L2_ffn_W2)
    xn = _layernorm(x, axis=-1)
    x = x + _L3_attn_ref(xn, L3_attn_W_in, L3_attn_conv_w, L3_attn_conv_b, L3_attn_W_x, L3_attn_A_log, L3_attn_D_param, L3_attn_W_dt, L3_attn_b_dt, L3_attn_W_out) + _L3_ffn_ref(xn, L3_ffn_qweights, L3_ffn_scales, L3_ffn_biases, L3_ffn_lora_a, L3_ffn_lora_b, L3_ffn_ln_gamma, L3_ffn_ln_beta)
    return x

_drawn_inputs = setup_inputs


def setup_inputs(seed=0):
    import zlib

    import numpy as np

    out = dict(_drawn_inputs(seed))
    spreads = {'L0_ffn_ln_g': (1.0, 0.6),
     'L0_ffn_ln_b': (0.0, 0.294),
     'L0_ffn_rms_g': (1.0, 0.6),
     'L2_attn_b_proj': (0.0, 0.1),
     'L3_attn_D_param': (1.0, 0.6),
     'L3_ffn_ln_gamma': (1.0, 0.2),
     'L3_ffn_ln_beta': (0.0, 0.1)}
    factors = {'L0_attn_fcq_b': 22.805,
     'L0_attn_fck_b': 200.0,
     'L0_ffn_rt_kv': 200.0,
     'L0_ffn_w_q_h': 8.0,
     'L0_ffn_null_kv': 6.53,
     'L1_ffn_w_router': 8.0,
     'L1_ffn_w1': 8.0,
     'L1_ffn_w2': 8.0,
     'L1_ffn_w3': 8.0,
     'L3_attn_b_dt': 3.756,
     'L3_ffn_biases': 6.109,
     'L3_ffn_lora_a': 6.797,
     'L3_ffn_lora_b': 6.484}
    for name, (base, spread) in spreads.items():
        noise = np.random.default_rng([zlib.crc32(name.encode()), seed]).standard_normal(out[name].shape)
        drawn = base * np.exp(spread * noise) if base else spread * noise
        out[name] = jnp.asarray(drawn.astype(out[name].dtype))
    for name, factor in factors.items():
        out[name] = (out[name] * factor).astype(out[name].dtype)
    return out
```

```python
from contextlib import ExitStack, contextmanager

import numpy as np
import concourse.bass as bass
from concourse import mybir

F32 = mybir.dt.float32
I32 = mybir.dt.int32
ALU = mybir.AluOpType
ACT = mybir.ActivationFunctionType
AXX = mybir.AxisListType.X

BATCH, SEQ, DIM = 8, 256, 128
P = 128
TOKENS = BATCH * SEQ
TILES = TOKENS // P
SUB = SEQ // P
CHUNK = 512
CHUNKS = TOKENS // CHUNK
CT = CHUNK // P
LN_EPS = 1e-5

HEADS = 16
HD = 64
PAIRS = HEADS // 2
DESCENTS = 50
NQ, NKV = 128, 256
KQ, KKV = NQ * 9.0 / 8.0, NKV * 9.0 / 8.0
DESCENTS_PER_SEQ = 6

L1_FD = 16
L1_ENC = 64
L1_EPS = 1e-12
L1_E, L1_H = 8, 176
L1_HC = L1_E * L1_H // P
L2_D = 8
L2_E, L2_F = 8, 512
L2_FC = L2_F // P
L3_IN, L3_N, L3_CONV = 256, 16, 4
L3_DC = L3_IN // P
L3_R, L3_GROUP, L3_LIN = 32, 16, 6



class Names(dict):

    def __getattr__(self, name):
        return self[name]


@contextmanager
def signals(nc, *names):
    with ExitStack() as held:
        sems = {n: held.enter_context(nc.semaphore(n)) for n in names}
        yield Names(**sems)
        for s in sems.values():
            nc.sync.sem_clear(s)
        nc.all_engine_barrier()


class Steps:

    def __init__(self, engine, sem):
        self.engine, self.sem, self.n = engine, sem, 0

    def add(self, instruction):
        instruction.then_inc(self.sem, 1)
        self.n += 1
        return self.n

    def wait(self):
        self.engine.wait_ge(self.sem, self.n)


def bank(k, i):
    return k.psum[i]



def layer_norm_stage(nc, k, loads=(), first=None):
    with signals(nc, "x_loaded", "weights_loaded", "dve_step", "moments_ready", "rstd_ready", "tile_normed", "group_turned", "group_saved") as s:
        with nc.Block() as block:
            @block.sync
            def _(sp):
                if first is not None:
                    sp.dma_start(k.x[:, :, :], first).then_inc(s.x_loaded, 16)
                    sp.dma_start(k.ident[:, :], k.dram["ident"]).then_inc(s.x_loaded, 16)
                for dst, src in loads:
                    sp.dma_start(dst, src).then_inc(s.weights_loaded, 16)
                if loads:
                    sp.wait_ge(s.weights_loaded, 16 * len(loads))

            @block.vector
            def _(dve):
                step = Steps(dve, s.dve_step)
                if first is not None:
                    dve.wait_ge(s.x_loaded, 32)
                for t in range(TILES):
                    step.add(nc.vector.bn_stats(k.stats[:, t, :], k.x[:, t, :]))
                step.wait()
                for t in range(TILES):
                    step.add(nc.vector.bn_aggr(k.moments[:, t, :], k.stats[:, t, :]))
                step.wait()
                step.add(nc.vector.tensor_scalar(k.rstd[:, :], k.moments[:, :, 1], LN_EPS, None, ALU.add))
                step.wait()
                nc.vector.reciprocal(k.rstd[:, :], k.rstd[:, :]).then_inc(s.moments_ready, 1)
                dve.wait_ge(s.rstd_ready, 1)
                for t in range(TILES):
                    nc.vector.tensor_scalar(k.xn[:, t, :], k.x[:, t, :], k.moments[:, t, 0:1], k.rstd[:, t:t + 1],
                                            ALU.subtract, ALU.mult).then_inc(s.tile_normed, 1)


            @block.tensor
            def _(pe):
                if first is not None:
                    pe.wait_ge(s.x_loaded, 32)
                for g in range(CHUNKS):
                    pe.wait_ge(s.tile_normed, CT * (g + 1))
                    if g >= 2:
                        pe.wait_ge(s.group_saved, g - 1)
                    for j in range(CT):
                        last = nc.tensor.transpose(bank(k, g % 2)[:, P * j:P * (j + 1)], k.xn[:, CT * g + j, :], k.ident[:, :])
                    last.then_inc(s.group_turned, 1)

            @block.scalar
            def _(act):
                act.wait_ge(s.moments_ready, 1)
                nc.scalar.activation(k.rstd[:, :], k.rstd[:, :], ACT.Sqrt).then_inc(s.rstd_ready, 1)
                for g in range(CHUNKS):
                    act.wait_ge(s.group_turned, g + 1)
                    nc.scalar.activation(k.xnT[:, CHUNK * g:CHUNK * (g + 1)], bank(k, g % 2)[:, :], ACT.Copy).then_inc(s.group_saved, 1)


def layer0_prepare_stage(nc, k, w):
    with signals(nc, "dve_step", "moments_ready", "factors_ready", "light_normed", "rms_normed", "turned", "saved", "logits_made", "logits_saved", "route_dve", "route_act",
                 "fused_made", "fused_saved", "nullw_made", "act_step", "pool_step") as s:
        with nc.Block() as block:
            @block.vector
            def _(dve):
                step = Steps(dve, s.dve_step)
                for t in range(TILES):
                    step.add(nc.vector.bn_stats(k.stats[:, t, :], k.xn[:, t, :]))
                step.wait()
                for t in range(TILES):
                    step.add(nc.vector.bn_aggr(k.moments[:, t, :], k.stats[:, t, :]))
                step.wait()
                step.add(nc.vector.tensor_tensor(k.rms[:, :], k.moments[:, :, 0], k.moments[:, :, 0], ALU.mult))
                step.wait()
                step.add(nc.vector.tensor_tensor(k.rms[:, :], k.rms[:, :], k.moments[:, :, 1], ALU.add))
                step.wait()
                step.add(nc.vector.tensor_scalar(k.rms[:, :], k.rms[:, :], float(DIM), 1e-24, ALU.mult, ALU.max))
                step.add(nc.vector.tensor_scalar(k.rstd[:, :], k.moments[:, :, 1], LN_EPS, None, ALU.add))
                step.wait()
                nc.vector.reciprocal(k.rms[:, :], k.rms[:, :]).then_inc(s.moments_ready, 1)
                nc.vector.reciprocal(k.rstd[:, :], k.rstd[:, :]).then_inc(s.moments_ready, 1)
                dve.wait_ge(s.factors_ready, 2)
                for t in range(TILES):
                    if t >= 8:
                        dve.wait_ge(s.turned, (t - 8) // CT + 1)
                    nc.vector.tensor_scalar(k.norm8[:, t % 8, :], k.xn[:, t, :], k.moments[:, t, 0:1], k.rstd[:, t:t + 1],
                                            ALU.subtract, ALU.mult).then_inc(s.light_normed, 1)
                for t in range(TILES):
                    dve.wait_ge(s.turned, (t + 8) // CT + 1)
                    nc.vector.tensor_scalar(k.norm8[:, t % 8, :], k.xn[:, t, :], k.rms[:, t:t + 1], None, ALU.mult).then_inc(s.rms_normed, 1)
                dve.wait_ge(s.logits_made, 1)
                step.add(nc.vector.tensor_copy(k.logits[:, :], bank(k, 7)[0:16, 0:SEQ]))
                step.wait()
                step.add(nc.vector.reduce_max(k.logit_max[:, :], k.logits[:, :], AXX))
                step.add(nc.vector.tensor_scalar(k.neg_a[:, :], k.logk[:, :], -1.0, float(np.log(np.float32(SEQ))), ALU.mult, ALU.add))
                step.wait()
                step.add(nc.vector.tensor_scalar(k.floor_m[:, :], k.neg_a[:, :], k.logit_max[:, :], None, ALU.min))
                for i in range(1, DESCENTS - BATCH * DESCENTS_PER_SEQ):
                    step.wait()
                    descend_dve_first(nc, k).then_inc(s.route_dve, 1)
                    dve.wait_ge(s.route_act, i)
                    step.add(descend_dve_a(nc, k))
                    step.wait()
                    step.add(descend_dve_m(nc, k))

            @block.scalar
            def _(act):
                act.wait_ge(s.moments_ready, 2)
                nc.scalar.activation(k.rstd[:, :], k.rstd[:, :], ACT.Sqrt).then_inc(s.factors_ready, 1)
                nc.scalar.activation(k.rms[:, :], k.rms[:, :], ACT.Sqrt, scale=float(DIM)).then_inc(s.factors_ready, 1)
                for g in range(2 * CHUNKS):
                    light = g < CHUNKS
                    act.wait_ge(s.turned, g + 1)
                    dst = (w.xlT if light else w.xrT)[:, CHUNK * (g % CHUNKS):CHUNK * (g % CHUNKS + 1)]
                    if light:
                        ins = nc.scalar.activation(dst, bank(k, g % 2)[:, :], ACT.Identity, scale=w.cols[:, 0:1], bias=w.cols[:, 1:2])
                    else:
                        ins = nc.scalar.activation(dst, bank(k, g % 2)[:, :], ACT.Copy, scale=w.cols[:, 2:3])
                    ins.then_inc(s.saved, 1)
                for i in range(6):
                    act.wait_ge(s.fused_made, i + 1)
                    nc.scalar.activation(w.fused[:, i // 2, CHUNK * (i % 2):CHUNK * (i % 2 + 1)], bank(k, 2 + i % 2)[:, :], ACT.Copy)\
                        .then_inc(s.fused_saved, 1)
                act.wait_ge(s.nullw_made, 1)
                act.wait_ge(s.pool_step, 2)
                nc.scalar.activation(w.null_out[0:8, :], bank(k, 4)[0:8, 0:P], ACT.Copy).then_inc(s.act_step, 1)
                nc.scalar.activation(w.qbias[:, :], w.qbias[:, :], ACT.Copy, scale=HD ** -0.5).then_inc(s.act_step, 1)
                for i in range(1, DESCENTS - BATCH * DESCENTS_PER_SEQ):
                    act.wait_ge(s.route_dve, i)
                    nc.scalar.activation(k.route_exp[:, :], k.route_arg[:, :], ACT.Exp, accum_out=k.route_sum[:, :]).then_inc(s.act_step, 1)
                    act.wait_ge(s.act_step, 2 + i)
                    nc.scalar.activation(k.route_log[:, :], k.route_sum[:, :], ACT.Ln).then_inc(s.route_act, 1)

            @block.gpsimd
            def _(pool):
                nc.gpsimd.memset(w.null_out[:, :], 0.0).then_inc(s.pool_step, 1)
                nc.gpsimd.memset(k.null_probsT[:, :], 0.0).then_inc(s.pool_step, 1)
                nc.gpsimd.memset(k.keys[:, :, :], 0.0).then_inc(s.pool_step, 1)

            @block.tensor
            def _(pe):
                for g in range(2 * CHUNKS):
                    light = g < CHUNKS
                    if light:
                        pe.wait_ge(s.light_normed, CT * (g + 1))
                    else:
                        pe.wait_ge(s.rms_normed, CT * (g - CHUNKS + 1))
                    if g >= 2:
                        pe.wait_ge(s.saved, g - 1)
                    for j in range(CT):
                        last = nc.tensor.transpose(bank(k, g % 2)[:, P * j:P * (j + 1)], k.norm8[:, (CT * g + j) % 8, :], k.ident[:, :])
                    last.then_inc(s.turned, 1)
                for b in range(BATCH):
                    last = nc.tensor.matmul(bank(k, 7)[0:16, 0:SEQ], w.route_tokens[:, b, :], k.xnT[:, SEQ * b:SEQ * (b + 1)],
                                            start=(b == 0), stop=(b == BATCH - 1))
                last.then_inc(s.logits_made, 1)
                for i in range(6):
                    if i >= 2:
                        pe.wait_ge(s.fused_saved, i - 1)
                    nc.tensor.matmul(bank(k, 2 + i % 2)[:, :], w.inT[:, i // 2, :], w.fc[:, i // 2, CHUNK * (i % 2):CHUNK * (i % 2 + 1)],
                                     start=True, stop=True).then_inc(s.fused_made, 1)
                for c in range(4):
                    last = nc.tensor.matmul(bank(k, 4)[0:8, 0:P], w.null_v[:, c, :], w.wo_h[:, c, :], start=(c == 0), stop=(c == 3))
                last.then_inc(s.nullw_made, 1)


def descend_dve_first(nc, k):
    return nc.vector.tensor_scalar(k.route_arg[:, :], k.logits[:, :], k.neg_a[:, :], k.floor_m[:, :], ALU.min, ALU.subtract)


def descend_dve_a(nc, k):
    return nc.vector.tensor_scalar(k.neg_a[:, :], k.route_log[:, :], k.floor_m[:, :], k.logk[:, :], ALU.add, ALU.subtract)


def descend_dve_m(nc, k):
    return nc.vector.tensor_scalar(k.floor_m[:, :], k.neg_a[:, :], k.logit_max[:, :], None, ALU.min)



PT_LAG, PV_LAG = 2, 3
PBUF = 4


def softmax_attention_stage(nc, k, b, c):
    l0, ffn, l2 = c.kind == "l0", c.kind == "l0ffn", c.kind == "l2"
    per_out = 4 if l2 else 2
    outs = HEADS // per_out
    mcols = P // per_out
    SB, TB, OB, PB = (0, 1, 2), (3, 4), (5, 6), 7

    def masked(h):
        return ffn and h < PAIRS

    def nulled(h):
        return ffn and h >= PAIRS

    with signals(nc, "x_copied", "pair_made", "query_saved", "key_saved", "values_made", "values_saved", "scores_ready",
                 "masked_ready", "negmax_ready", "probs_ready", "recip_ready", "probs_normed", "turned", "turned_saved", "values_weighed",
                 "out_saved", "null_scores", "null_args", "null_exps", "null_weights", "null_taken", "weights_picked", "null_turned", "null_saved", "y_made", "y_saved", "y_turned",
                 "x_added", "route_dve", "route_act", "act_step", "dve_step", "pool_step") as s:
        with nc.Block() as block:

            @block.gpsimd
            def _(pool):
                if ffn:
                    nc.gpsimd.tensor_copy(k.xb[:, 0, :], c.w.xlT[:, bass.ds(b * SEQ, SEQ)]).then_inc(s.x_copied, 1)
                    nc.gpsimd.tensor_copy(k.xb[:, 1, :], c.w.xrT[:, bass.ds(b * SEQ, SEQ)]).then_inc(s.x_copied, 1)
                else:
                    nc.gpsimd.tensor_copy(k.xb[:, 0, :], k.xnT[:, bass.ds(b * SEQ, SEQ)]).then_inc(s.x_copied, 1)
                if l2:
                    pool.wait_ge(s.key_saved, 1)
                    for h in range(HEADS):
                        nc.gpsimd.tensor_scalar(k.keys[:, h, :], k.rot[:, 1, :], k.head8[:, h:h + 1], None, ALU.mult).then_inc(s.pool_step, 1)
                for h in range(HEADS):
                    pool.wait_ge(s.recip_ready, h + 1)
                    for t in range(SUB):
                        piece = k.probs[:, h % PBUF, t, :]
                        nc.gpsimd.tensor_scalar(piece, piece, k.recip[:, h, t:t + 1], None, ALU.mult).then_inc(s.probs_normed, 1)

            @block.tensor
            def _(pe):
                pe.wait_ge(s.x_copied, 2 if ffn else 1)

                def project_pair(p):
                    if p >= 1:
                        pe.wait_ge(s.query_saved, p)
                        pe.wait_ge(s.key_saved, 2 * p)
                    if ffn and p >= 5:
                        pe.wait_ge(s.null_taken, p - 4)
                    src = k.xb[:, 1 if ffn and p >= 4 else 0, :]
                    nc.tensor.matmul(k.psum[PB][:, 0:SEQ], c.wq(p), src, start=True, stop=True)
                    nc.tensor.matmul(k.psum[PB][:, SEQ:2 * SEQ], c.wk(p), src, start=True, stop=True).then_inc(s.pair_made, 1)

                def project_values():
                    for i in range(2 * SUB):
                        t, half = i // 2, i % 2
                        src = k.xb[:, 1 if ffn and half else 0, P * t:P * (t + 1)]
                        nc.tensor.matmul(k.psum[3 + i][:, :], src, c.wv(half), start=True, stop=True).then_inc(s.values_made, 1)

                def scores(h):
                    if l2:
                        pe.wait_ge(s.query_saved, 1)
                        pe.wait_ge(s.pool_step, h + 1)
                    else:
                        pe.wait_ge(s.query_saved, h // 2 + 1)
                        pe.wait_ge(s.key_saved, 2 * (h // 2 + 1))
                    if h >= 3:
                        if masked(h - 3):
                            pe.wait_ge(s.masked_ready, h - 2)
                        else:
                            pe.wait_ge(s.probs_ready, 2 * (h - 2))
                    sb = k.psum[SB[h % 3]]
                    for t in range(SUB):
                        last = nc.tensor.matmul(sb[:, SEQ * t:SEQ * (t + 1)], c.query(h, t), k.keys[:, h, :], start=True, stop=True)
                    last.then_inc(s.scores_ready, 1)

                def null_scores(p):
                    for t in range(SUB):
                        last = nc.tensor.matmul(k.psum[PB][:, 2 * t:2 * t + 2], c.query(2 * p, t), c.w.null_k[:, p - 4, :],
                                                start=True, stop=True)
                    last.then_inc(s.null_scores, 1)

                def turn(h):
                    pe.wait_ge(s.probs_normed, 2 * (h + 1))
                    if h >= 2:
                        pe.wait_ge(s.turned_saved, h - 1)
                    elif not l2:
                        pe.wait_ge(s.values_saved, 2 * SUB)
                    tb = k.psum[TB[h % 2]]
                    for kt in range(SUB):
                        for t in range(SUB):
                            last = nc.tensor.transpose(tb[:, SEQ * kt + P * t:SEQ * kt + P * (t + 1)],
                                                       k.probs[:, h % PBUF, t, P * kt:P * (kt + 1)], k.ident[:, :])
                    last.then_inc(s.turned, 1)

                def weigh_values(h):
                    pe.wait_ge(s.turned_saved, h + 1)
                    o = h // per_out
                    if h == 0:
                        pe.wait_ge(s.values_saved, 2 if l2 else 2 * SUB)
                    if o >= 2 and h % per_out == 0:
                        pe.wait_ge(s.out_saved, o - 1)
                    r = mcols * (h % per_out)
                    for kt in range(SUB):
                        last = nc.tensor.matmul(k.psum[OB[o % 2]][r:r + mcols, 0:SEQ], c.value(h, kt), k.probsT[:, h % 3, kt, :],
                                                start=(kt == 0), stop=(kt == SUB - 1))
                    last.then_inc(s.values_weighed, 1)

                if l2:
                    for i in range(4):
                        last = nc.tensor.matmul(k.psum[PB if i < 2 else OB[0]][:, SEQ * (i % 2):SEQ * (i % 2 + 1)], c.w.w_rot[:, i, :],
                                                k.xb[:, 0, :], start=True, stop=True)
                    last.then_inc(s.pair_made, 1)
                    for t in range(SUB):
                        last = nc.tensor.matmul(k.psum[OB[1]][:, P * t:P * (t + 1)], k.xb[:, 0, P * t:P * (t + 1)], c.w.w_v[:, :],
                                                start=True, stop=True)
                    last.then_inc(s.values_made, 1)
                else:
                    project_pair(0)
                    project_values()
                for h in range(HEADS + PV_LAG):
                    if h < HEADS:
                        scores(h)
                        if nulled(h) and h % 2 == 0:
                            null_scores(h // 2)
                        if not l2 and h % 2 == 0 and h // 2 + 1 < PAIRS:
                            project_pair(h // 2 + 1)
                    if 0 <= h - PT_LAG < HEADS:
                        turn(h - PT_LAG)
                    if 0 <= h - PV_LAG:
                        weigh_values(h - PV_LAG)

                pe.wait_ge(s.out_saved, outs)
                groups = [(0, 4), (4, 8)] if ffn else [(0, outs)]
                if ffn:
                    pe.wait_ge(s.null_weights, PAIRS)
                    for t in range(SUB):
                        last = nc.tensor.transpose(k.psum[TB[0]][0:8, P * t:P * (t + 1)], k.null_probs[:, t, :], k.ident[:, :])
                    last.then_inc(s.null_turned, 1)
                    pe.wait_ge(s.null_saved, 1)
                for g, (o0, o1) in enumerate(groups):
                    for o in range(o0, o1):
                        last = nc.tensor.matmul(k.psum[SB[0]][:, SEQ * g:SEQ * (g + 1)], c.wo(o), k.outT[:, o, :],
                                                start=(o == o0), stop=(o == o1 - 1 and g == 0))
                    if g == 1:
                        last = nc.tensor.matmul(k.psum[SB[0]][:, SEQ:2 * SEQ], c.w.null_out[:, :], k.null_probsT[:, :], start=False, stop=True)
                last.then_inc(s.y_made, 1)
                pe.wait_ge(s.y_saved, 1)
                for g in range(len(groups)):
                    for t in range(SUB):
                        last = nc.tensor.transpose(k.psum[SB[1]][:, SEQ * g + P * t:SEQ * g + P * (t + 1)],
                                                   k.yT[:, g, P * t:P * (t + 1)], k.ident[:, :])
                last.then_inc(s.y_turned, 1)

            @block.scalar
            def _(act):
                def save_query(p):
                    act.wait_ge(s.pair_made, p + 1)
                    nc.scalar.activation(k.queryT[:, p, :], k.psum[PB][:, 0:SEQ], ACT.Identity, scale=HD ** -0.5,
                                         bias=c.qbias(p)).then_inc(s.query_saved, 1)

                def save_values():
                    for i in range(2 * SUB):
                        t, half = i // 2, i % 2
                        if l0 or half == 0:
                            continue
                        act.wait_ge(s.values_made, i + 1)
                        nc.scalar.activation(k.values[:, t, CHUNK:2 * CHUNK], k.psum[3 + i][:, :], ACT.Copy,
                                             scale=k.route_b[:, 2, t:t + 1]).then_inc(s.values_saved, 1)

                def exponentials(h):
                    act.wait_ge(s.negmax_ready, h + 1)
                    if h >= PBUF:
                        act.wait_ge(s.turned, h - PBUF + 1)
                    for t in range(SUB):
                        src = k.masked_scores[:, h % 2, t, :] if masked(h) else k.psum[SB[h % 3]][:, SEQ * t:SEQ * (t + 1)]
                        nc.scalar.activation(k.probs[:, h % PBUF, t, :], src, ACT.Exp, bias=k.negmax[:, h, t:t + 1],
                                             accum_out=k.prob_sum[:, h, t:t + 1]).then_inc(s.probs_ready, 1)
                    if nulled(h):
                        act.wait_ge(s.null_args, h - PAIRS + 1)
                        nc.scalar.activation(k.null_exp[:, h - PAIRS, :], k.null_arg[:, h - PAIRS, :], ACT.Exp).then_inc(s.null_exps, 1)

                def save_out(o):
                    act.wait_ge(s.values_weighed, per_out * (o + 1))
                    nc.scalar.activation(k.outT[:, o, :], k.psum[OB[o % 2]][:, 0:SEQ], ACT.Copy).then_inc(s.out_saved, 1)

                def descend(i):
                    act.wait_ge(s.route_dve, i + 1)
                    nc.scalar.activation(k.route_exp[:, :], k.route_arg[:, :], ACT.Exp, accum_out=k.route_sum[:, :]).then_inc(s.act_step, 1)
                    act.wait_ge(s.act_step, i + 1)
                    nc.scalar.activation(k.route_log[:, :], k.route_sum[:, :], ACT.Ln).then_inc(s.route_act, 1)

                if not l2:
                    save_query(0)
                    if ffn:
                        act.wait_ge(s.weights_picked, 1)
                        save_values()
                for h in range(HEADS + PV_LAG + 1):
                    if h < HEADS:
                        if not l2 and h % 2 == 0 and h // 2 + 1 < PAIRS:
                            save_query(h // 2 + 1)
                        exponentials(h)
                    if l0 and h % 2 == 1 and h // 2 < DESCENTS_PER_SEQ:
                        descend(h // 2)
                    done = h - PV_LAG
                    if done >= 0 and done % per_out == per_out - 1:
                        save_out(done // per_out)
                if ffn:
                    act.wait_ge(s.null_turned, 1)
                    nc.scalar.activation(k.null_probsT[0:8, :], k.psum[TB[0]][0:8, 0:SEQ], ACT.Copy).then_inc(s.null_saved, 1)
                act.wait_ge(s.y_made, 1)
                if ffn:
                    nc.scalar.activation(k.yT[:, :, :].rearrange("p g n -> p (g n)"), k.psum[SB[0]][:, :], ACT.Copy).then_inc(s.y_saved, 1)
                else:
                    nc.scalar.activation(k.yT[:, 0, :], k.psum[SB[0]][:, 0:SEQ], ACT.Identity, bias=c.obias).then_inc(s.y_saved, 1)

            @block.vector
            def _(dve):
                step = Steps(dve, s.dve_step)
                n_null = Steps(dve, s.null_args)

                def save_keys(p):
                    dve.wait_ge(s.query_saved, p + 1)
                    for j in range(2):
                        rows = slice(HD * j, HD * (j + 1))
                        src = k.psum[PB][rows, SEQ:2 * SEQ]
                        if l0:
                            ins = nc.vector.tensor_scalar(k.keys[rows, 2 * p + j, :], src, c.w.kbias[rows, p:p + 1], None, ALU.add)
                        else:
                            ins = nc.vector.tensor_copy(k.keys[rows, 2 * p + j, :], src)
                        ins.then_inc(s.key_saved, 1)

                def save_values():
                    for i in range(2 * SUB):
                        t, half = i // 2, i % 2
                        if ffn and half:
                            continue
                        dve.wait_ge(s.values_made, i + 1)
                        dst = k.values[:, t, CHUNK * half:CHUNK * (half + 1)]
                        if l0:
                            ins = nc.vector.tensor_tensor(dst, k.psum[3 + i][:, :], c.w.vbias[:, CHUNK * half:CHUNK * (half + 1)], ALU.add)
                        else:
                            ins = nc.vector.tensor_copy(dst, k.psum[3 + i][:, :])
                        ins.then_inc(s.values_saved, 1)

                def negmax(h):
                    dve.wait_ge(s.scores_ready, h + 1)
                    sb = k.psum[SB[h % 3]][:, :].rearrange("p (t n) -> p t n", t=SUB)
                    if masked(h):
                        if h >= 2:
                            dve.wait_ge(s.probs_ready, 2 * (h - 1))
                        nc.vector.tensor_tensor(k.masked_scores[:, h % 2, :, :], sb, k.window_mask[:, :, :], ALU.add).then_inc(s.masked_ready, 1)
                        dve.wait_ge(s.masked_ready, h + 1)
                        sb = k.masked_scores[:, h % 2, :, :]
                    if not nulled(h):
                        nc.vector.reduce_max(k.negmax[:, h, :], sb, AXX, negate=True).then_inc(s.negmax_ready, 1)
                        return
                    p, j = h // 2, h % 2
                    if j == 0:
                        dve.wait_ge(s.null_scores, p - 3)
                        nc.vector.tensor_copy(k.null_scores[:, p % 2, :], k.psum[PB][:, 0:2 * SUB]).then_inc(s.null_taken, 1)
                    step.add(nc.vector.reduce_max(k.key_negmax[:, :], sb, AXX, negate=True))
                    step.wait()
                    dve.wait_ge(s.null_taken, p - 3)
                    null = k.null_scores[:, p % 2, :].rearrange("p (t j) -> p t j", j=2)[:, :, j]
                    nc.vector.scalar_tensor_tensor(k.negmax[:, h, :], null, -1.0, k.key_negmax[:, :], ALU.mult, ALU.min).then_inc(s.negmax_ready, 1)
                    dve.wait_ge(s.negmax_ready, h + 1)
                    n_null.add(nc.vector.tensor_tensor(k.null_arg[:, h - PAIRS, :], null, k.negmax[:, h, :], ALU.add))

                def reciprocal(h):
                    dve.wait_ge(s.probs_ready, 2 * (h + 1))
                    if nulled(h):
                        dve.wait_ge(s.null_exps, h - PAIRS + 1)
                        step.add(nc.vector.tensor_tensor(k.prob_sum[:, h, :], k.prob_sum[:, h, :], k.null_exp[:, h - PAIRS, :], ALU.add))
                        step.wait()
                    nc.vector.reciprocal(k.recip[:, h, :], k.prob_sum[:, h, :]).then_inc(s.recip_ready, 1)
                    if nulled(h):
                        dve.wait_ge(s.recip_ready, h + 1)
                        nc.vector.tensor_tensor(k.null_probs[:, :, h - PAIRS], k.null_exp[:, h - PAIRS, :], k.recip[:, h, :], ALU.mult)\
                            .then_inc(s.null_weights, 1)

                def save_turned(h):
                    dve.wait_ge(s.turned, h + 1)
                    if h >= 3:
                        dve.wait_ge(s.values_weighed, h - 2)
                    nc.vector.tensor_copy(k.probsT[:, h % 3, :, :].rearrange("p a n -> p (a n)"), k.psum[TB[h % 2]][:, :]).then_inc(s.turned_saved, 1)

                if l2:
                    dve.wait_ge(s.pair_made, 1)
                    pb = k.psum[PB][:, :].rearrange("p (i n) -> p i n", i=2)
                    ob = k.psum[OB[0]][:, :].rearrange("p (i n) -> p i n", i=2)
                    step.add(nc.vector.tensor_tensor(k.rot[:, :, :], pb, k.rot_cos[:, :, :], ALU.mult))
                    step.add(nc.vector.tensor_tensor(k.rot2[:, :, :], ob, k.rot_sin[:, :, :], ALU.mult))
                    step.wait()
                    last = nc.vector.tensor_tensor(k.rot[:, :, :], k.rot[:, :, :], k.rot2[:, :, :], ALU.add)
                    last.then_inc(s.key_saved, 1)
                    dve.wait_ge(s.key_saved, 1)
                    nc.vector.tensor_copy(k.queryT[:, 0, :], k.rot[:, 0, :]).then_inc(s.query_saved, 1)
                    dve.wait_ge(s.values_made, 1)
                    for t in range(SUB):
                        src = k.psum[OB[1]][:, P * t:P * (t + 1)].rearrange("p (h d) -> p h d", d=L2_D)
                        nc.vector.tensor_copy(c.w.padded_values[:, t, :, 0:L2_D], src).then_inc(s.values_saved, 1)
                else:
                    if ffn:
                        nc.vector.tensor_copy(k.route_b[:, :, :], k.route_w[:, :, bass.ds(b * SUB, SUB)]).then_inc(s.weights_picked, 1)
                    save_keys(0)
                    save_values()
                for h in range(HEADS + PT_LAG):
                    if h < HEADS:
                        if not l2 and h % 2 == 1 and h // 2 + 1 < PAIRS:
                            save_keys(h // 2 + 1)
                        negmax(h)
                    if 1 <= h <= HEADS:
                        reciprocal(h - 1)
                    if l0 and h % 2 == 0 and h // 2 <= DESCENTS_PER_SEQ:
                        i = h // 2
                        if i >= 1:
                            dve.wait_ge(s.route_act, i)
                            step.add(descend_dve_a(nc, k))
                            step.wait()
                            step.add(descend_dve_m(nc, k))
                            step.wait()
                        if i < DESCENTS_PER_SEQ:
                            descend_dve_first(nc, k).then_inc(s.route_dve, 1)
                    if h >= PT_LAG:
                        save_turned(h - PT_LAG)
                dve.wait_ge(s.y_turned, 1)
                tb = k.psum[SB[1]]
                if not ffn:
                    nc.vector.tensor_tensor(k.x[:, bass.ds(b * SUB, SUB), :], k.x[:, bass.ds(b * SUB, SUB), :],
                                            tb[:, 0:SEQ].rearrange("p (t n) -> p t n", t=SUB), ALU.add).then_inc(s.x_added, 1)
                else:
                    for t in range(SUB):
                        step.add(nc.vector.scalar_tensor_tensor(k.mix[:, t, :], tb[:, SEQ + P * t:SEQ + P * (t + 1)], k.route_b[:, 0, t:t + 1],
                                                                k.x[:, bass.ds(b * SUB + t, 1), :].rearrange("p a n -> p (a n)"),
                                                                ALU.mult, ALU.add))
                    step.wait()
                    for t in range(SUB):
                        step.add(nc.vector.scalar_tensor_tensor(k.mix[:, t, :], c.w.null_q[:, :], k.route_b[:, 1, t:t + 1], k.mix[:, t, :],
                                                                ALU.mult, ALU.add))
                    step.wait()
                    nc.vector.tensor_tensor(k.x[:, bass.ds(b * SUB, SUB), :], k.mix[:, :, :],
                                            tb[:, 0:SEQ].rearrange("p (t n) -> p t n", t=SUB), ALU.add).then_inc(s.x_added, 1)


def route_stage(nc, k, w):
    with signals(nc, "dve_step", "scored", "exped", "weighted", "sent", "spread", "turned", "cols_saved") as s:
        with nc.Block() as block:
            @block.vector
            def _(dve):
                step = Steps(dve, s.dve_step)
                step.add(nc.vector.tensor_scalar(k.logits[:, :], k.logits[:, :], k.neg_a[:, :], 0.0, ALU.subtract, ALU.min))
                step.wait()
                nc.vector.tensor_scalar(k.logits[:, :], k.logits[:, :], -103.0, None, ALU.max).then_inc(s.scored, 1)
                dve.wait_ge(s.exped, 1)
                step.add(nc.vector.tensor_scalar(k.route_arg[:, :], k.route_exp[:, :], -1.0, 1.0, ALU.mult, ALU.add))
                step.wait()
                nc.vector.tensor_tensor(k.route_arg[:, :], k.route_arg[:, :], k.route_exp[:, :], ALU.add).then_inc(s.weighted, 1)
                dve.wait_ge(s.turned, 1)
                nc.vector.tensor_copy(k.route_cols[:, :, :, :].rearrange("p a t r -> p (a t r)"), k.psum[0][:, 0:4 * 16]).then_inc(s.cols_saved, 1)
                dve.wait_ge(s.cols_saved, 1)
                dve.wait_ge(s.spread, 16)
                n = 0
                for b in range(BATCH):
                    for t in range(SUB):
                        mine = k.route_cols[:, 0, t, b:b + 1]
                        i = SUB * b + t
                        if n >= 2:
                            dve.wait_ge(s.dve_step, step.n - 2)
                        step.add(nc.vector.tensor_scalar(w.compare[:, n % 2, :], w.scores_all[:, b, :], mine, 0.0, ALU.is_gt, ALU.add,
                                                         accum_out=k.rank[:, 0, i:i + 1]))
                        step.add(nc.vector.scalar_tensor_tensor(w.compare[:, 2 + n % 2, :], w.scores_all[:, b, :], mine, w.earlier[:, t, :],
                                                                ALU.is_equal, ALU.mult, accum_out=k.rank[:, 1, i:i + 1]))
                        n += 1
                step.wait()
                step.add(nc.vector.tensor_tensor(k.rank[:, 0, :], k.rank[:, 0, :], k.rank[:, 1, :], ALU.add))
                step.wait()
                selected = k.route_w[:, 0, :]
                step.add(nc.vector.tensor_scalar(selected, k.rank[:, 0, :], float(NQ), None, ALU.is_lt))
                step.add(nc.vector.tensor_scalar(k.route_w[:, 1, :], k.rank[:, 0, :], float(NQ), None, ALU.is_ge))
                step.wait()
                by_token = k.route_cols[:, 1, :, :].rearrange("p t r -> p r t")
                step.add(nc.vector.tensor_tensor(selected.rearrange("p (b t) -> p b t", t=SUB), selected.rearrange("p (b t) -> p b t", t=SUB),
                                                 by_token[:, 0:BATCH, :], ALU.mult))
                step.add(nc.vector.tensor_copy(k.route_w[:, 2, :].rearrange("p (b t) -> p b t", t=SUB), by_token[:, BATCH:2 * BATCH, :]))

            @block.scalar
            def _(act):
                act.wait_ge(s.scored, 1)
                nc.scalar.activation(k.route_exp[:, :], k.logits[:, :], ACT.Exp).then_inc(s.exped, 1)

            @block.sync
            def _(sp):
                sp.wait_ge(s.scored, 1)
                sp.dma_start(k.scratch, k.logits[0:BATCH, :]).then_inc(s.sent, 16)
                sp.wait_ge(s.sent, 16)
                sp.dma_start(w.scores_all[:, :, :].rearrange("p b n -> p (b n)"),
                             k.scratch.rearrange("b n -> (b n)").partition_broadcast(P)).then_inc(s.spread, 16)

            @block.tensor
            def _(pe):
                pe.wait_ge(s.scored, 1)
                for t in range(SUB):
                    nc.tensor.transpose(k.psum[0][:, 16 * t:16 * (t + 1)], k.logits[:, P * t:P * (t + 1)], k.ident[0:16, 0:16])
                pe.wait_ge(s.weighted, 1)
                for t in range(SUB):
                    last = nc.tensor.transpose(k.psum[0][:, 16 * (SUB + t):16 * (SUB + t + 1)], k.route_arg[:, P * t:P * (t + 1)],
                                               k.ident[0:16, 0:16])
                last.then_inc(s.turned, 1)



def taylor_attention_stage(nc, k, b, w):
    LAG = 2
    ABUF = 3
    SB, EB, OB = (0, 1), (2, 3), (4, 5)
    WIDE = SEQ + P
    with signals(nc, "x_copied", "proj_made", "query_saved", "keys_saved", "values_made", "act_values", "dve_values", "enc_made",
                 "head_query", "scores_ready", "squared", "kernel_ready", "weighed", "dve_step", "out_saved", "y_made", "y_saved",
                 "y_turned", "x_added") as s:
        with nc.Block() as block:
            @block.gpsimd
            def _(pool):
                nc.gpsimd.tensor_copy(k.xb[:, 0, :], k.xnT[:, bass.ds(b * SEQ, SEQ)]).then_inc(s.x_copied, 1)
                pool.wait_ge(s.query_saved, 1)
                for h in range(HEADS):
                    nc.gpsimd.tensor_scalar(k.keys[:, h, :], k.queryT[:, h // 8, :], k.head16[:, h % 8:h % 8 + 1], None, ALU.mult)\
                        .then_inc(s.head_query, 1)

            @block.tensor
            def _(pe):
                xb = k.xb[:, 0, :]
                pe.wait_ge(s.x_copied, 1)
                for i in range(2):
                    nc.tensor.matmul(k.psum[6][:, SEQ * i:SEQ * (i + 1)], w.w_q[:, P * i:P * (i + 1)], xb, start=True, stop=True)
                    last = nc.tensor.matmul(k.psum[7][:, SEQ * i:SEQ * (i + 1)], w.w_k[:, P * i:P * (i + 1)], xb, start=True, stop=True)
                last.then_inc(s.proj_made, 1)
                for i in range(2):
                    last = nc.tensor.matmul(k.psum[2][:, L1_ENC * i:L1_ENC * (i + 1)], w.w_k_enc[:, P * i:P * (i + 1)], xb[:, 0:L1_ENC],
                                            start=True, stop=True)
                last.then_inc(s.proj_made, 1)
                for i in range(2 * SUB):
                    t, half = i // 2, i % 2
                    nc.tensor.matmul(k.psum[(0, 1, 4, 5)[i]][:, :], xb[:, P * t:P * (t + 1)], w.w_v[:, CHUNK * half:CHUNK * (half + 1)],
                                     start=True, stop=True).then_inc(s.values_made, 1)
                for half in range(2):
                    if half:
                        pe.wait_ge(s.query_saved, 1)
                    nc.tensor.matmul(k.psum[(3, 6)[half]][0:L1_ENC, :], xb[:, 0:L1_ENC], w.w_v_enc[:, CHUNK * half:CHUNK * (half + 1)],
                                     start=True, stop=True).then_inc(s.enc_made, 1)
                pe.wait_ge(s.keys_saved, 2)
                pe.wait_ge(s.act_values, 4)
                pe.wait_ge(s.dve_values, 2)

                def scores(h):
                    pe.wait_ge(s.head_query, h + 1)
                    if h >= 2:
                        pe.wait_ge(s.squared, 2 * (h - 1))
                    c, q = h // 8, k.keys[:, h, :]
                    sb = k.psum[SB[h % 2]]
                    nc.tensor.matmul(sb[:, 0:SEQ], w.kT[:, c, 0:P], q, start=True, stop=True)
                    nc.tensor.matmul(sb[:, SEQ:WIDE], w.kT[:, c, P:2 * P], q[:, P:2 * P], start=True, stop=True)
                    nc.tensor.matmul(k.psum[EB[h % 2]][0:L1_ENC, 0:SEQ], w.k_encT[:, c, :], q, start=True, stop=True).then_inc(s.scores_ready, 1)

                def weigh(h):
                    pe.wait_ge(s.kernel_ready, 2 * (h + 1))
                    o = h // 2
                    if o >= 2 and h % 2 == 0:
                        pe.wait_ge(s.out_saved, o - 1)
                    rows = slice(HD * (h % 2), HD * (h % 2 + 1))
                    ob = k.psum[OB[o % 2]]
                    A, E = w.kernel[:, h % ABUF, :], w.kernel_enc[:, h % ABUF, :]
                    for col, vals in ((0, [k.values[:, 0, HD * h:HD * (h + 1)], k.values[:, 1, HD * h:HD * (h + 1)], w.v_enc[:, HD * h:HD * (h + 1)]]),
                                      (SEQ, [w.ones[:, :]] * 3)):
                        nc.tensor.matmul(ob[rows, col:col + SEQ], vals[0], A[:, 0:SEQ], start=True, stop=False)
                        nc.tensor.matmul(ob[rows, col + P:col + SEQ], vals[1], A[:, SEQ:WIDE], start=False, stop=False)
                        last = nc.tensor.matmul(ob[rows, col:col + SEQ], vals[2], E, start=False, stop=True)
                    last.then_inc(s.weighed, 1)

                for h in range(HEADS + LAG):
                    if h < HEADS:
                        scores(h)
                    if h >= LAG:
                        weigh(h - LAG)
                pe.wait_ge(s.out_saved, PAIRS)
                for o in range(PAIRS):
                    last = nc.tensor.matmul(k.psum[6][:, 0:SEQ], w.w_out[:, o, :], k.outT[:, o, :], start=(o == 0), stop=(o == PAIRS - 1))
                last.then_inc(s.y_made, 1)
                pe.wait_ge(s.y_saved, 1)
                for t in range(SUB):
                    last = nc.tensor.transpose(k.psum[7][:, P * t:P * (t + 1)], k.yT[:, 0, P * t:P * (t + 1)], k.ident[:, :])
                last.then_inc(s.y_turned, 1)

            @block.scalar
            def _(act):
                act.wait_ge(s.proj_made, 1)
                nc.scalar.activation(k.queryT[:, 0:2, :].rearrange("p c n -> p (c n)"), k.psum[6][:, :], ACT.Copy).then_inc(s.query_saved, 1)
                for i in range(2):
                    act.wait_ge(s.values_made, i + 1)
                    nc.scalar.activation(k.values[:, 0, CHUNK * i:CHUNK * (i + 1)], k.psum[i][:, :], ACT.Copy).then_inc(s.act_values, 1)
                for i in range(2):
                    act.wait_ge(s.enc_made, i + 1)
                    nc.scalar.activation(w.v_enc[0:L1_ENC, CHUNK * i:CHUNK * (i + 1)], k.psum[(3, 6)[i]][0:L1_ENC, :], ACT.Copy)\
                        .then_inc(s.act_values, 1)
                for h in range(HEADS):
                    act.wait_ge(s.scores_ready, h + 1)
                    if h >= ABUF:
                        act.wait_ge(s.weighed, h - ABUF + 1)
                    nc.scalar.activation(w.kernel[:, h % ABUF, :], k.psum[SB[h % 2]][:, 0:WIDE], ACT.Square, scale=0.25, bias=1.0)\
                        .then_inc(s.squared, 1)
                    nc.scalar.activation(w.kernel_enc[0:L1_ENC, h % ABUF, :], k.psum[EB[h % 2]][0:L1_ENC, 0:SEQ], ACT.Square, scale=0.25,
                                         bias=1.0).then_inc(s.squared, 1)
                act.wait_ge(s.y_made, 1)
                nc.scalar.activation(k.yT[:, 0, :], k.psum[6][:, 0:SEQ], ACT.Copy).then_inc(s.y_saved, 1)

            @block.vector
            def _(dve):
                step = Steps(dve, s.dve_step)
                dve.wait_ge(s.proj_made, 2)
                nc.vector.tensor_copy(w.kT[:, :, :].rearrange("p c n -> p (c n)"), k.psum[7][:, :]).then_inc(s.keys_saved, 1)
                nc.vector.tensor_copy(w.k_encT[:, :, :].rearrange("p c n -> p (c n)"), k.psum[2][:, 0:2 * L1_ENC]).then_inc(s.keys_saved, 1)
                for i in range(2):
                    dve.wait_ge(s.values_made, 3 + i)
                    nc.vector.tensor_copy(k.values[:, 1, CHUNK * i:CHUNK * (i + 1)], k.psum[4 + i][:, :]).then_inc(s.dve_values, 1)

                def divide(o):
                    dve.wait_ge(s.weighed, 2 * (o + 1))
                    ob = k.psum[OB[o % 2]]
                    step.add(nc.vector.tensor_scalar(w.norm[:, o % 2, :], ob[:, SEQ:2 * SEQ], 2 * L1_EPS, None, ALU.add))
                    step.wait()
                    step.add(nc.vector.reciprocal(w.norm[:, o % 2, :], w.norm[:, o % 2, :]))
                    step.wait()
                    nc.vector.tensor_tensor(k.outT[:, o, :], ob[:, 0:SEQ], w.norm[:, o % 2, :], ALU.mult).then_inc(s.out_saved, 1)

                for h in range(HEADS + LAG + 1):
                    if h < HEADS:
                        dve.wait_ge(s.squared, 2 * (h + 1))
                        A, E = w.kernel[:, h % ABUF, :], w.kernel_enc[0:L1_ENC, h % ABUF, :]
                        nc.vector.scalar_tensor_tensor(A, A, 1.0, w.causal[:, :], ALU.add, ALU.mult).then_inc(s.kernel_ready, 1)
                        nc.vector.tensor_scalar(E, E, 1.0, None, ALU.add).then_inc(s.kernel_ready, 1)
                    done = h - LAG - 1
                    if done >= 0 and done % 2:
                        divide(done // 2)
                dve.wait_ge(s.y_turned, 1)
                nc.vector.tensor_tensor(k.x[:, bass.ds(b * SUB, SUB), :], k.x[:, bass.ds(b * SUB, SUB), :],
                                        k.psum[7][:, 0:SEQ].rearrange("p (t n) -> p t n", t=SUB), ALU.add).then_inc(s.x_added, 1)



def gate_stage(nc, k, w_router, renormalise, zeros=()):
    E = 8
    with signals(nc, "logits_made", "centred", "exped", "dve_step", "gated", "turned", "saved", "pool_step") as s:
        with nc.Block() as block:
            @block.gpsimd
            def _(pool):
                nc.gpsimd.memset(k.gateT[:, :], 0.0).then_inc(s.pool_step, 1)
                for z in zeros:
                    nc.gpsimd.memset(z, 0.0)

            @block.tensor
            def _(pe):
                for t in range(TILES):
                    last = nc.tensor.matmul(k.psum[0][:, E * t:E * (t + 1)], k.xnT[:, P * t:P * (t + 1)], w_router, start=True, stop=True)
                last.then_inc(s.logits_made, 1)
                pe.wait_ge(s.gated, 1)
                for g in range(CHUNKS):
                    for j in range(CT):
                        last = nc.tensor.transpose(k.psum[1 + g][0:E, P * j:P * (j + 1)], k.gate[:, CT * g + j, :], k.ident[:, :])
                    last.then_inc(s.turned, 1)

            @block.scalar
            def _(act):
                act.wait_ge(s.centred, 1)
                nc.scalar.activation(k.gate[:, :, :], k.gate[:, :, :], ACT.Exp).then_inc(s.exped, 1)
                act.wait_ge(s.pool_step, 1)
                for g in range(CHUNKS):
                    act.wait_ge(s.turned, g + 1)
                    nc.scalar.activation(k.gateT[0:E, CHUNK * g:CHUNK * (g + 1)], k.psum[1 + g][0:E, :], ACT.Copy).then_inc(s.saved, 1)

            @block.vector
            def _(dve):
                step = Steps(dve, s.dve_step)
                logits = k.psum[0][:, 0:E * TILES].rearrange("p (t e) -> p t e", e=E)
                per_tile = k.gate_sum[:, :].unsqueeze(2).to_broadcast([P, TILES, E])
                step.add(nc.vector.memset(k.gate_cmp[:, :, :, :], 0.0))
                dve.wait_ge(s.logits_made, 1)
                step.add(nc.vector.reduce_max(k.gate_sum[:, :], logits, AXX))
                step.wait()
                nc.vector.tensor_tensor(k.gate[:, :, :], logits, per_tile, ALU.subtract).then_inc(s.centred, 1)
                dve.wait_ge(s.exped, 1)
                step.add(nc.vector.reduce_sum(k.gate_sum[:, :], k.gate[:, :, :], AXX))
                step.wait()
                step.add(nc.vector.reciprocal(k.gate_sum[:, :], k.gate_sum[:, :]))
                step.wait()
                step.add(nc.vector.tensor_tensor(k.gate[:, :, :], k.gate[:, :, :], per_tile, ALU.mult))
                step.wait()
                for j in range(E):
                    rival = k.gate[:, :, j:j + 1]
                    if j > 0:
                        step.add(nc.vector.tensor_tensor(k.gate_cmp[:, j, :, 0:j], rival.to_broadcast([P, TILES, j]), k.gate[:, :, 0:j], ALU.is_gt))
                    if j < E - 1:
                        step.add(nc.vector.tensor_tensor(k.gate_cmp[:, j, :, j + 1:E], rival.to_broadcast([P, TILES, E - 1 - j]),
                                                         k.gate[:, :, j + 1:E], ALU.is_ge))
                step.wait()
                step.add(nc.vector.reduce_sum(k.gate_rank[:, :, :].rearrange("p t e -> p (t e)"),
                                              k.gate_cmp[:, :, :, :].rearrange("p j t e -> p (t e) j"), AXX))
                step.wait()
                last = nc.vector.scalar_tensor_tensor(k.gate[:, :, :], k.gate_rank[:, :, :], 2.0, k.gate[:, :, :], ALU.is_lt, ALU.mult)
                if renormalise:
                    step.add(last)
                    step.wait()
                    step.add(nc.vector.reduce_sum(k.gate_sum[:, :], k.gate[:, :, :], AXX))
                    step.wait()
                    step.add(nc.vector.reciprocal(k.gate_sum[:, :], k.gate_sum[:, :]))
                    step.wait()
                    last = nc.vector.tensor_tensor(k.gate[:, :, :], k.gate[:, :, :], per_tile, ALU.mult)
                last.then_inc(s.gated, 1)


def finish_chunk_pe(nc, k, pe, s):
    pe.wait_ge(s.y_saved, 1)
    for j in range(CT):
        last = nc.tensor.transpose(k.psum[7][:, P * j:P * (j + 1)], k.y_chunk[:, P * j:P * (j + 1)], k.ident[:, :])
    last.then_inc(s.y_turned, 1)


def finish_chunk_dve(nc, k, dve, s, c):
    dve.wait_ge(s.y_turned, 1)
    rows = k.x[:, bass.ds(c * CT, CT), :]
    nc.vector.tensor_tensor(rows, rows, k.psum[7][:, :].rearrange("p (t n) -> p t n", t=CT), ALU.add).then_inc(s.x_added, 1)


def swiglu_experts_stage(nc, k, c, w):
    HB = 3
    with signals(nc, "up_ready", "silu_ready", "product_ready", "hidden_ready", "down_done", "y_made", "y_saved", "y_turned", "x_added") as s:
        with nc.Block() as block:
            @block.tensor
            def _(pe):
                xs, gs = k.xnT[:, bass.ds(c * CHUNK, CHUNK)], k.gateT[:, bass.ds(c * CHUNK, CHUNK)]
                for i in range(L1_HC + 1):
                    if i < L1_HC:
                        if i >= 2:
                            pe.wait_ge(s.hidden_ready, i - 1)
                        cols = slice(P * i, P * (i + 1))
                        nc.tensor.matmul(k.psum[i % 2][:, :], w.w1[:, cols], xs, start=True, stop=True)
                        nc.tensor.matmul(k.psum[2 + i % 2][:, :], w.w3[:, cols], xs, start=True, stop=True)
                        nc.tensor.matmul(k.psum[4 + i % 2][:, :], w.expert_of[:, cols], gs, start=True, stop=True).then_inc(s.up_ready, 1)
                    if i >= 1:
                        pe.wait_ge(s.hidden_ready, i)
                        last = nc.tensor.matmul(k.psum[6][:, :], w.w2[:, i - 1, :], w.hidden[:, (i - 1) % HB, :], start=(i == 1),
                                                stop=(i == L1_HC))
                        last.then_inc(s.down_done, 1)
                finish_chunk_pe(nc, k, pe, s)

            @block.scalar
            def _(act):
                for i in range(L1_HC):
                    act.wait_ge(s.up_ready, i + 1)
                    if i >= 2:
                        act.wait_ge(s.product_ready, i - 1)
                    nc.scalar.activation(w.silu[:, i % 2, :], k.psum[i % 2][:, :], ACT.Silu).then_inc(s.silu_ready, 1)
                act.wait_ge(s.down_done, L1_HC)
                nc.scalar.activation(k.y_chunk[:, :], k.psum[6][:, :], ACT.Copy).then_inc(s.y_saved, 1)

            @block.vector
            def _(dve):
                for i in range(L1_HC):
                    dve.wait_ge(s.silu_ready, i + 1)
                    if i >= HB:
                        dve.wait_ge(s.down_done, i - HB + 1)
                    hid = w.hidden[:, i % HB, :]
                    nc.vector.tensor_tensor(hid, w.silu[:, i % 2, :], k.psum[2 + i % 2][:, :], ALU.mult).then_inc(s.product_ready, 1)
                    dve.wait_ge(s.product_ready, i + 1)
                    nc.vector.tensor_tensor(hid, hid, k.psum[4 + i % 2][:, :], ALU.mult).then_inc(s.hidden_ready, 1)
                finish_chunk_dve(nc, k, dve, s, c)


def relu_experts_stage(nc, k, c, w):
    HB, UB, STEPS = 3, 4, L2_E * L2_FC
    with signals(nc, "gate_made", "gate_saved", "up_ready", "hidden_ready", "down_done", "y_saved", "y_turned", "x_added") as s:
        with nc.Block() as block:
            @block.tensor
            def _(pe):
                xs, gs = k.xnT[:, bass.ds(c * CHUNK, CHUNK)], k.gateT[:, bass.ds(c * CHUNK, CHUNK)]

                def spread(e):
                    if e >= 2:
                        pe.wait_ge(s.gate_saved, e - 1)
                    nc.tensor.matmul(k.psum[4 + e % 2][:, :], k.ident[:, e:e + 1].to_broadcast([P, P]), gs, start=True, stop=True)\
                        .then_inc(s.gate_made, 1)

                spread(0)
                for i in range(STEPS + 2):
                    if i < STEPS:
                        if i % L2_FC == 0 and i // L2_FC + 1 < L2_E:
                            spread(i // L2_FC + 1)
                        if i >= UB:
                            pe.wait_ge(s.hidden_ready, i - UB + 1)
                        nc.tensor.matmul(k.psum[i % UB][:, :], w.w1[:, P * i:P * (i + 1)], xs, start=True, stop=True).then_inc(s.up_ready, 1)
                    if i >= 2:
                        j = i - 2
                        pe.wait_ge(s.hidden_ready, j + 1)
                        nc.tensor.matmul(k.psum[6][:, :], w.w2[:, j, :], w.hidden[:, j % HB, :], start=(j == 0), stop=(j == STEPS - 1))\
                            .then_inc(s.down_done, 1)
                finish_chunk_pe(nc, k, pe, s)

            @block.scalar
            def _(act):
                for e in range(L2_E):
                    act.wait_ge(s.gate_made, e + 1)
                    if e >= 2:
                        act.wait_ge(s.hidden_ready, L2_FC * (e - 1))
                    nc.scalar.activation(w.gate_all[:, e % 2, :], k.psum[4 + e % 2][:, :], ACT.Copy).then_inc(s.gate_saved, 1)
                act.wait_ge(s.down_done, STEPS)
                nc.scalar.activation(k.y_chunk[:, :], k.psum[6][:, :], ACT.Copy).then_inc(s.y_saved, 1)

            @block.vector
            def _(dve):
                for i in range(STEPS):
                    dve.wait_ge(s.up_ready, i + 1)
                    dve.wait_ge(s.gate_saved, i // L2_FC + 1)
                    if i >= HB:
                        dve.wait_ge(s.down_done, i - HB + 1)
                    nc.vector.scalar_tensor_tensor(w.hidden[:, i % HB, :], k.psum[i % UB][:, :], 0.0, w.gate_all[:, i // L2_FC % 2, :],
                                                   ALU.max, ALU.mult).then_inc(s.hidden_ready, 1)
                finish_chunk_dve(nc, k, dve, s, c)



HALF = TOKENS // 2
HALF_SEQS = HALF // SEQ


def ssm_prepare_stage(nc, k, w):
    with signals(nc, "cleared", "in_made", "in_saved", "x_saved", "conv_made", "ssm_ready", "proj_made", "proj_saved", "dt_made", "dt_biased",
                 "dt_folded", "dt_exped", "dt_logged", "decay_exped", "dve_step", "conv_step", "lora_made", "linear_made", "linear_turned",
                 "linear_saved") as s:
        with nc.Block() as block:
            @block.gpsimd
            def _(pool):
                nc.gpsimd.memset(w.padded[:, :, :, 0:L3_CONV - 1], 0.0).then_inc(s.cleared, 1)
                nc.gpsimd.memset(w.projT[:, :], 0.0).then_inc(s.cleared, 1)
                nc.gpsimd.memset(w.decay[:, :, :, 0:1], 0.0).then_inc(s.cleared, 1)

            @block.tensor
            def _(pe):
                n = 0
                for m in range(2 * L3_DC):
                    for g in range(CHUNKS):
                        if n >= 4:
                            pe.wait_ge(s.in_saved, n - 3)
                        nc.tensor.matmul(k.psum[n % 4][:, :], w.w_in[:, P * m:P * (m + 1)], k.xnT[:, CHUNK * g:CHUNK * (g + 1)],
                                         start=True, stop=True).then_inc(s.in_made, 1)
                        n += 1
                for l in range(L3_LIN):
                    last = nc.tensor.matmul(k.psum[4 + l // 4][:, P * (l % 4):P * (l % 4 + 1)], w.lora_b[:, l, :], w.lora_a[:, l, :],
                                            start=True, stop=True)
                last.then_inc(s.lora_made, 1)
                pe.wait_ge(s.linear_made, 2)
                for l in range(L3_LIN):
                    last = nc.tensor.transpose(k.psum[6 + l // 4][:, P * (l % 4):P * (l % 4 + 1)], w.linear[:, l, :], k.ident[:, :])
                last.then_inc(s.linear_turned, 1)
                pe.wait_ge(s.ssm_ready, L3_DC)
                pe.wait_ge(s.linear_saved, 2)
                for g in range(CHUNKS):
                    for m in range(L3_DC):
                        last = nc.tensor.matmul(k.psum[g][0:2 * L3_N + 1, :], w.w_x[:, m, :], w.xs[:, m, CHUNK * g:CHUNK * (g + 1)],
                                                start=(m == 0), stop=(m == L3_DC - 1))
                    last.then_inc(s.proj_made, 1)
                pe.wait_ge(s.proj_saved, CHUNKS)
                for m in range(L3_DC):
                    for g in range(CHUNKS):
                        last = nc.tensor.matmul(k.psum[4 * m + g][:, :], w.w_dt[:, m, :], w.projT[:, CHUNK * g:CHUNK * (g + 1)], start=True, stop=True)
                    last.then_inc(s.dt_made, 1)

            @block.scalar
            def _(act):
                n = 0
                for m in range(2 * L3_DC):
                    for g in range(CHUNKS):
                        act.wait_ge(s.in_made, n + 1)
                        seqs = slice(2 * g, 2 * g + 2)
                        if m < L3_DC:
                            last = nc.scalar.activation(w.padded[:, m, seqs, L3_CONV - 1:], k.psum[n % 4][:, :].rearrange("p (b n) -> p b n", b=2), ACT.Copy)
                        else:
                            last = nc.scalar.activation(w.z[:, m - L3_DC, CHUNK * g:CHUNK * (g + 1)], k.psum[n % 4][:, :], ACT.Silu)
                        last.then_inc(s.in_saved, 1)
                        n += 1
                for m in range(L3_DC):
                    act.wait_ge(s.conv_made, m + 1)
                    nc.scalar.activation(w.xs[:, m, :], w.xs[:, m, :], ACT.Silu, bias=w.conv_b[:, m:m + 1]).then_inc(s.ssm_ready, 1)
                act.wait_ge(s.linear_turned, 1)
                for i in range(2):
                    width = (4, 2)[i]
                    nc.scalar.activation(w.linearT[:, 4 * i:4 * i + width, :].rearrange("p l n -> p (l n)"), k.psum[6 + i][:, 0:P * width], ACT.Copy)\
                        .then_inc(s.linear_saved, 1)
                act.wait_ge(s.cleared, 2)
                for g in range(CHUNKS):
                    act.wait_ge(s.proj_made, g + 1)
                    nc.scalar.activation(w.projT[0:2 * L3_N + 1, CHUNK * g:CHUNK * (g + 1)], k.psum[g][0:2 * L3_N + 1, :], ACT.Copy)\
                        .then_inc(s.proj_saved, 1)
                nc.scalar.activation(w.a_neg[:, :, :], w.a_neg[:, :, :], ACT.Exp).then_inc(s.decay_exped, 1)
                for m in range(L3_DC):
                    act.wait_ge(s.dt_folded, m + 1)
                    nc.scalar.activation(w.xdt[:, m, :], w.xdt[:, m, :], ACT.Exp).then_inc(s.dt_exped, 1)
                for m in range(L3_DC):
                    act.wait_ge(s.dt_exped, m + 1)
                    nc.scalar.activation(w.xdt[:, m, :], w.xdt[:, m, :], ACT.Ln, bias=1.0).then_inc(s.dt_logged, 1)

            @block.vector
            def _(dve):
                step, conv = Steps(dve, s.dve_step), Steps(dve, s.conv_step)
                step.add(nc.vector.tensor_scalar(w.linear[:, :, :], w.codes[:, :, :], 1.0 / 7.5, -1.0, ALU.mult, ALU.add))
                step.wait()
                grouped = w.linear[:, :, :].rearrange("p l (g n) -> p (l g) n", n=L3_GROUP)
                step.add(nc.vector.tensor_tensor(grouped, grouped, w.scales[:, :].unsqueeze(2).to_broadcast([P, L3_LIN * P // L3_GROUP, L3_GROUP]),
                                                 ALU.mult))
                step.wait()
                dve.wait_ge(s.lora_made, 1)
                for i in range(2):
                    width = (4, 2)[i]
                    part = w.linear[:, 4 * i:4 * i + width, :].rearrange("p l n -> p (l n)")
                    nc.vector.tensor_tensor(part, part, k.psum[4 + i][:, 0:P * width], ALU.add).then_inc(s.linear_made, 1)
                dve.wait_ge(s.cleared, 3)
                for m in range(L3_DC):
                    dve.wait_ge(s.in_saved, CHUNKS * (m + 1))
                    out = w.xs[:, m, :].rearrange("p (b n) -> p b n", b=BATCH)
                    conv.add(nc.vector.tensor_scalar(out, w.padded[:, m, :, 0:SEQ], w.conv_w[:, m, 0:1], None, ALU.mult))
                    for j in range(1, L3_CONV):
                        conv.wait()
                        last = nc.vector.scalar_tensor_tensor(out, w.padded[:, m, :, j:j + SEQ], w.conv_w[:, m, j:j + 1], out, ALU.mult, ALU.add)
                        if j < L3_CONV - 1:
                            conv.add(last)
                        else:
                            last.then_inc(s.conv_made, 1)
                for m in range(L3_DC):
                    dve.wait_ge(s.dt_made, m + 1)
                    nc.vector.tensor_scalar(w.dt[:, m, :], k.psum_all[:, 4 * CHUNK * m:4 * CHUNK * (m + 1)], w.b_dt[:, m:m + 1], None, ALU.add)\
                        .then_inc(s.dt_biased, 1)
                    dve.wait_ge(s.dt_biased, m + 1)
                    nc.vector.scalar_tensor_tensor(w.xdt[:, m, :], w.dt[:, m, :], -1.0, w.dt[:, m, :], ALU.mult, ALU.min).then_inc(s.dt_folded, 1)
                dve.wait_ge(s.decay_exped, 1)
                step.add(nc.vector.tensor_scalar(w.a_neg[:, :, :], w.a_neg[:, :, :], -1.0, None, ALU.mult))
                for m in range(L3_DC):
                    dve.wait_ge(s.dt_logged, m + 1)
                    step.add(nc.vector.scalar_tensor_tensor(w.dt[:, m, :], w.dt[:, m, :], 0.0, w.xdt[:, m, :], ALU.max, ALU.add))
                    step.wait()
                    step.add(nc.vector.tensor_tensor(w.xdt[:, m, :], w.dt[:, m, :], w.xs[:, m, :], ALU.mult))


def ssm_scan_stage(nc, k, hf, w):
    UNITS = L3_N * L3_DC
    BUF = 3
    with signals(nc, "b_spread", "c_spread", "c_saved", "decay_ready", "input_ready", "scanned", "weighted", "summed", "dve_step", "y_ready",
                 "out_made", "y_saved", "y_turned", "x_added") as s:
        with nc.Block() as block:
            @block.tensor
            def _(pe):
                def spread(n):
                    if n >= 1:
                        pe.wait_ge(s.input_ready, L3_DC * n)
                    for j in range(2):
                        last = nc.tensor.matmul(k.psum[j][:, :], k.ident[:, n:n + 1].to_broadcast([P, P]),
                                                w.projT[:, bass.ds(hf * HALF + CHUNK * j, CHUNK)], start=True, stop=True)
                    last.then_inc(s.b_spread, 1)
                    if n >= 1:
                        pe.wait_ge(s.c_saved, n)
                    for j in range(2):
                        last = nc.tensor.matmul(k.psum[2 + j][:, :], k.ident[:, L3_N + n:L3_N + n + 1].to_broadcast([P, P]),
                                                w.projT[:, bass.ds(hf * HALF + CHUNK * j, CHUNK)], start=True, stop=True)
                    last.then_inc(s.c_spread, 1)

                def accumulate(u):
                    pe.wait_ge(s.weighted, u + 1)
                    n, m = u // L3_DC, u % L3_DC
                    for j in range(2):
                        last = nc.tensor.matmul(k.psum[4 + 2 * m + j][:, :], k.ident[:, :], w.weighted[:, u % BUF, CHUNK * j:CHUNK * (j + 1)],
                                                start=(n == 0), stop=(n == L3_N - 1))
                    last.then_inc(s.summed, 1)

                spread(0)
                for n in range(L3_N):
                    if n + 1 < L3_N:
                        spread(n + 1)
                    if n >= 1:
                        for m in range(L3_DC):
                            accumulate(L3_DC * (n - 1) + m)
                for m in range(L3_DC):
                    accumulate(L3_DC * (L3_N - 1) + m)
                pe.wait_ge(s.y_ready, L3_DC)
                for j in range(2):
                    for m in range(L3_DC):
                        last = nc.tensor.matmul(k.psum[j][:, :], w.w_out[:, m, :], w.gated[:, m, CHUNK * j:CHUNK * (j + 1)],
                                                start=(m == 0), stop=(m == L3_DC - 1))
                last.then_inc(s.out_made, 1)
                for j in range(2):
                    pe.wait_ge(s.y_saved, j + 1)
                    for t in range(CT):
                        last = nc.tensor.transpose(k.psum[2 + j][:, P * t:P * (t + 1)], w.out_T[:, j, P * t:P * (t + 1)], k.ident[:, :])
                    last.then_inc(s.y_turned, 1)

            @block.scalar
            def _(act):
                for n in range(L3_N):
                    for m in range(L3_DC):
                        u = L3_DC * n + m
                        if u >= BUF:
                            act.wait_ge(s.scanned, u - BUF + 1)
                        nc.scalar.activation(w.decay[:, u % BUF, :, 1:], w.dt[:, m, bass.ds(hf * HALF, HALF)].rearrange("p (b n) -> p b n", n=SEQ)[:, :, 1:],
                                             ACT.Exp, scale=w.a_neg[:, m, n:n + 1]).then_inc(s.decay_ready, 1)
                    act.wait_ge(s.c_spread, n + 1)
                    if n >= 2:
                        act.wait_ge(s.weighted, L3_DC * (n - 1))
                    nc.scalar.activation(w.c_all[:, n % 2, :], k.psum_all[:, 2 * CHUNK:4 * CHUNK], ACT.Copy).then_inc(s.c_saved, 1)
                act.wait_ge(s.out_made, 1)
                for j in range(2):
                    nc.scalar.activation(w.out_T[:, j, :], k.psum[j][:, :], ACT.Copy).then_inc(s.y_saved, 1)

            @block.gpsimd
            def _(pool):
                for u in range(UNITS):
                    pool.wait_ge(s.scanned, u + 1)
                    pool.wait_ge(s.c_saved, u // L3_DC + 1)
                    if u >= BUF:
                        pool.wait_ge(s.summed, u - BUF + 1)
                    nc.gpsimd.tensor_tensor(w.weighted[:, u % BUF, :], w.state[:, u % BUF, :], w.c_all[:, u // L3_DC % 2, :], ALU.mult)\
                        .then_inc(s.weighted, 1)

            @block.vector
            def _(dve):
                step = Steps(dve, s.dve_step)
                for u in range(UNITS):
                    n, m = u // L3_DC, u % L3_DC
                    if m == 0:
                        dve.wait_ge(s.b_spread, n + 1)
                    nc.vector.tensor_tensor(w.inflow[:, u % 2, :], w.xdt[:, m, bass.ds(hf * HALF, HALF)], k.psum_all[:, 0:HALF], ALU.mult)\
                        .then_inc(s.input_ready, 1)
                    dve.wait_ge(s.input_ready, u + 1)
                    dve.wait_ge(s.decay_ready, u + 1)
                    if u >= BUF:
                        dve.wait_ge(s.weighted, u - BUF + 1)
                    nc.vector.tensor_tensor_scan(w.state[:, u % BUF, :], w.decay[:, u % BUF, :, :].rearrange("p b n -> p (b n)"), w.inflow[:, u % 2, :],
                                                 0.0, ALU.mult, ALU.add).then_inc(s.scanned, 1)
                dve.wait_ge(s.summed, UNITS)
                for m in range(L3_DC):
                    step.add(nc.vector.scalar_tensor_tensor(w.gated[:, m, :], w.xs[:, m, bass.ds(hf * HALF, HALF)], w.d_skip[:, m:m + 1],
                                                            k.psum_all[:, CHUNK * (4 + 2 * m):CHUNK * (6 + 2 * m)], ALU.mult, ALU.add))
                    step.wait()
                    nc.vector.tensor_tensor(w.gated[:, m, :], w.gated[:, m, :], w.z[:, m, bass.ds(hf * HALF, HALF)], ALU.mult).then_inc(s.y_ready, 1)
                for j in range(2):
                    dve.wait_ge(s.y_turned, j + 1)
                    rows = k.x[:, bass.ds(hf * (HALF // P) + CT * j, CT), :]
                    nc.vector.tensor_tensor(rows, rows, k.psum[2 + j][:, :].rearrange("p (t n) -> p t n", t=CT), ALU.add).then_inc(s.x_added, 1)


def quantised_ffn_stage(nc, k, w):
    BLOCKS = L3_LIN // 2
    with signals(nc, "first_made", "first_biased", "dve_step", "moments_ready", "rstd_ready", "normed", "turned", "gelu_ready", "second_made",
                 "h_ready", "h_turned", "x_added") as s:
        with nc.Block() as block:
            @block.tensor
            def _(pe):
                n_turn = 0
                for blk in range(BLOCKS):
                    h = k.xnT if blk == 0 else w.hT
                    for g in range(CHUNKS):
                        if blk:
                            pe.wait_ge(s.h_ready, CHUNKS * (blk - 1) + g + 1)
                            pe.wait_ge(s.first_biased, CHUNKS * (blk - 1) + g + 1)
                        for j in range(CT):
                            c = CHUNK * g + P * j
                            last = nc.tensor.matmul(k.psum[g][:, P * j:P * (j + 1)], h[:, c:c + P], w.linearT[:, 2 * blk, :], start=True, stop=True)
                        last.then_inc(s.first_made, 1)
                    for g in range(CHUNKS):
                        pe.wait_ge(s.normed, TILES * blk + CT * (g + 1))
                        if n_turn >= 2:
                            pe.wait_ge(s.gelu_ready, n_turn - 1)
                        for j in range(CT):
                            last = nc.tensor.transpose(k.psum[4 + n_turn % 2][:, P * j:P * (j + 1)], w.y[:, CT * g + j, :], k.ident[:, :])
                        last.then_inc(s.turned, 1)
                        n_turn += 1
                        pe.wait_ge(s.gelu_ready, n_turn)
                        if n_turn > 2:
                            pe.wait_ge(s.h_ready, n_turn - 2)
                        nc.tensor.matmul(k.psum[6 + n_turn % 2][:, :], w.linearT[:, 2 * blk + 1, :], w.gelu[:, (n_turn - 1) % 2, :],
                                         start=True, stop=True).then_inc(s.second_made, 1)
                for g in range(CHUNKS):
                    pe.wait_ge(s.h_ready, CHUNKS * (BLOCKS - 1) + g + 1)
                    for j in range(CT):
                        c = CHUNK * g + P * j
                        last = nc.tensor.transpose(k.psum[g][:, P * j:P * (j + 1)], w.hT[:, c:c + P], k.ident[:, :])
                    last.then_inc(s.h_turned, 1)

            @block.scalar
            def _(act):
                n = 0
                for blk in range(BLOCKS):
                    act.wait_ge(s.moments_ready, blk + 1)
                    nc.scalar.activation(k.rstd[:, :], k.rstd[:, :], ACT.Sqrt).then_inc(s.rstd_ready, 1)
                    for g in range(CHUNKS):
                        act.wait_ge(s.turned, n + 1)
                        if n >= 2:
                            act.wait_ge(s.second_made, n - 1)
                        nc.scalar.activation(w.gelu[:, n % 2, :], k.psum[4 + n % 2][:, :], ACT.Gelu, scale=w.gamma[:, blk:blk + 1],
                                             bias=w.beta[:, blk:blk + 1]).then_inc(s.gelu_ready, 1)
                        n += 1

            @block.vector
            def _(dve):
                step = Steps(dve, s.dve_step)
                for blk in range(BLOCKS):
                    for g in range(CHUNKS):
                        dve.wait_ge(s.first_made, CHUNKS * blk + g + 1)
                        if blk:
                            dve.wait_ge(s.turned, CHUNKS * blk)
                        bias = w.bias_rows[:, blk, :].unsqueeze(1).to_broadcast([P, CT, P])
                        nc.vector.tensor_tensor(w.y[:, CT * g:CT * (g + 1), :], k.psum[g][:, :].rearrange("p (t n) -> p t n", t=CT), bias, ALU.add)\
                            .then_inc(s.first_biased, 1)
                    dve.wait_ge(s.first_biased, CHUNKS * (blk + 1))
                    for t in range(TILES):
                        step.add(nc.vector.bn_stats(k.stats[:, t, :], w.y[:, t, :]))
                    step.wait()
                    for t in range(TILES):
                        step.add(nc.vector.bn_aggr(k.moments[:, t, :], k.stats[:, t, :]))
                    step.wait()
                    step.add(nc.vector.tensor_scalar(k.rstd[:, :], k.moments[:, :, 1], LN_EPS, None, ALU.add))
                    step.wait()
                    nc.vector.reciprocal(k.rstd[:, :], k.rstd[:, :]).then_inc(s.moments_ready, 1)
                    dve.wait_ge(s.rstd_ready, blk + 1)
                    for t in range(TILES):
                        nc.vector.tensor_scalar(w.y[:, t, :], w.y[:, t, :], k.moments[:, t, 0:1], k.rstd[:, t:t + 1], ALU.subtract, ALU.mult)\
                            .then_inc(s.normed, 1)
                    for g in range(CHUNKS):
                        n = CHUNKS * blk + g
                        dve.wait_ge(s.second_made, n + 1)
                        if blk:
                            dve.wait_ge(s.h_ready, CHUNKS * (blk - 1) + g + 1)
                        before = (k.xnT if blk == 0 else w.hT)[:, CHUNK * g:CHUNK * (g + 1)]
                        nc.vector.scalar_tensor_tensor(w.hT[:, CHUNK * g:CHUNK * (g + 1)], k.psum[6 + (n + 1) % 2][:, :], w.bias_cols[:, blk:blk + 1],
                                                       before, ALU.add, ALU.add).then_inc(s.h_ready, 1)
                for g in range(CHUNKS):
                    dve.wait_ge(s.h_turned, g + 1)
                    rows = k.x[:, CT * g:CT * (g + 1), :]
                    nc.vector.tensor_tensor(rows, rows, k.psum[g][:, :].rearrange("p (t n) -> p t n", t=CT), ALU.add).then_inc(s.x_added, 1)


def layer3(nc, k, d):
    with ExitStack() as held:
        def sb(name, shape, dt=F32):
            return held.enter_context(nc.sbuf_tensor(name, shape, dt))
        w = Names(
            w_in=sb("w_in", [P, 4 * P]), conv_w=sb("conv_w", [P, L3_DC, L3_CONV]), conv_b=sb("conv_b", [P, L3_DC]),
            w_x=sb("w_x", [P, L3_DC, 2 * L3_N + 1]), a_neg=sb("a_neg", [P, L3_DC, L3_N]), d_skip=sb("d_skip", [P, L3_DC]),
            w_dt=sb("w_dt", [P, L3_DC, P]), b_dt=sb("b_dt", [P, L3_DC]), w_out=sb("w_out3", [P, L3_DC, P]),
            codes=sb("codes", [P, L3_LIN, P], I32), scales=sb("scales", [P, L3_LIN * P // L3_GROUP]), linear=sb("linear", [P, L3_LIN, P]),
            linearT=sb("linearT", [P, L3_LIN, P]), lora_a=sb("lora_a", [L3_R, L3_LIN, P]), lora_b=sb("lora_b", [L3_R, L3_LIN, P]),
            gamma=sb("gamma", [P, 3]), beta=sb("beta", [P, 3]), bias_rows=sb("bias_rows", [P, 3, P]), bias_cols=sb("bias_cols", [P, 3]),
            xs=sb("xs", [P, L3_DC, TOKENS]), z=sb("z", [P, L3_DC, TOKENS]), dt=sb("dt", [P, L3_DC, TOKENS]), xdt=sb("xdt", [P, L3_DC, TOKENS]),
            projT=sb("projT", [P, TOKENS]), decay=sb("decay", [P, 3, HALF_SEQS, SEQ]))
        loads = [(w.w_in[:, :], d["w_in3"]), (w.conv_w[:, :, :], d["conv_w"]), (w.conv_b[:, :], d["conv_b"]), (w.w_x[:, :, :], d["w_x"]),
                 (w.a_neg[:, :, :], d["a_log"]), (w.d_skip[:, :], d["d_skip"]), (w.w_dt[:, :, :], d["w_dt"]), (w.b_dt[:, :], d["b_dt"]),
                 (w.w_out[:, :, :], d["w_out3"]), (w.codes[:, :, :], d["codes"]), (w.scales[:, :], d["scales"]), (w.lora_a[:, :, :], d["lora_a"]),
                 (w.lora_b[:, :, :], d["lora_b"]), (w.gamma[:, :], d["gamma"]), (w.beta[:, :], d["beta"]),
                 (w.bias_rows[:, :, :].rearrange("p l n -> p (l n)"), d["bias_rows"].partition_broadcast(P)), (w.bias_cols[:, :], d["bias_cols"])]
        layer_norm_stage(nc, k, loads)
        with nc.sbuf_tensor("padded", [P, L3_DC, BATCH, L3_CONV - 1 + SEQ], F32) as padded:
            w.padded = padded
            ssm_prepare_stage(nc, k, w)
        with ExitStack() as scan:
            def sc(name, shape):
                return scan.enter_context(nc.sbuf_tensor(name, shape, F32))
            w.c_all, w.weighted, w.state = sc("c_all", [P, 2, HALF]), sc("weighted", [P, 3, HALF]), sc("state", [P, 3, HALF])
            w.inflow = sc("inflow", [P, 2, HALF])
            w.gated, w.out_T = w.state, w.inflow[:, :, 0:CHUNK]
            with nc.Fori(0, 2) as hf:
                ssm_scan_stage(nc, k, hf, w)
        with ExitStack() as ffn:
            w.y = k.xn
            w.hT = ffn.enter_context(nc.sbuf_tensor("hT", [P, TOKENS], F32))
            w.gelu = ffn.enter_context(nc.sbuf_tensor("gelu", [P, 2, CHUNK], F32))
            quantised_ffn_stage(nc, k, w)



def layer0(nc, k, d):
    with ExitStack() as held:
        def sb(name, shape):
            return held.enter_context(nc.sbuf_tensor(name, shape, F32))
        w = Names(
            cols=sb("norm_cols", [P, 3]), inT=sb("in_T", [HD, 3, P]), fc=sb("fc", [HD, 3, HEADS * HD]), fused=sb("fused", [P, 3, HEADS * HD]),
            qbias=sb("qbias", [P, PAIRS]), kbias=sb("kbias", [P, PAIRS]), vbias=sb("vbias", [P, HEADS * HD]), obias=sb("obias", [P, 1]),
            wo=sb("wo", [P, PAIRS, P]), qkv_l=sb("qkv_l", [P, 3, 512]), qkv_h=sb("qkv_h", [P, 3, 512]), wo_l=sb("wo_l", [P, 4, P]),
            wo_h=sb("wo_h", [P, 4, P]), null_k=sb("null_k", [P, 4, 2]), null_v=sb("null_v", [P, 4, 8]), null_q=sb("null_q", [P, P]),
            route_tokens=sb("route_tokens", [P, BATCH, 16]), xlT=sb("xlT", [P, TOKENS]), xrT=sb("xrT", [P, TOKENS]),
            null_out=sb("null_out", [P, P]), earlier=sb("earlier", [P, SUB, SEQ]), compare=sb("compare", [P, 4, SEQ]),
            scores_all=sb("scores_all", [P, BATCH, SEQ]))
        loads = [(w.cols[:, :], d["cols"]), (w.inT[:, :, :], d["inT"]), (w.fc[:, :, :], d["fc"]), (w.qbias[:, :], d["qbias"]),
                 (w.kbias[:, :], d["kbias"]), (w.vbias[:, :], d["vbias"].partition_broadcast(P)), (w.obias[:, :], d["obias0"]),
                 (w.wo[:, :, :], d["wo0"]), (w.qkv_l[:, :, :], d["qkv_l"]), (w.qkv_h[:, :, :], d["qkv_h"]), (w.wo_l[:, :, :], d["wo_l"]),
                 (w.wo_h[:, :, :], d["wo_h"]), (w.null_k[:, :, :], d["null_k"]), (w.null_v[:, :, :], d["null_v"]),
                 (w.null_q[:, :], d["null_q"].partition_broadcast(P)), (w.route_tokens[:, :, :], d["route_tokens"]), (k.logk[:, :], d["logk"]),
                 (k.window_mask[:, :, :], d["window_mask"]), (w.earlier[:, :, :], d["earlier"]), (k.head16[:, :], d["head16"]),
                 (k.head8[:, :], d["head8"]), (k.rot_cos[:, :, :], d["rot_cos"]), (k.rot_sin[:, :, :], d["rot_sin"])]
        layer_norm_stage(nc, k, loads, first=d["x"])
        layer0_prepare_stage(nc, k, w)
        main = Names(
            kind="l0", w=w, wq=lambda p: w.fused[:, 0, P * p:P * (p + 1)], wk=lambda p: w.fused[:, 1, P * p:P * (p + 1)],
            wv=lambda half: w.fused[:, 2, CHUNK * half:CHUNK * (half + 1)], qbias=lambda p: w.qbias[:, p:p + 1],
            query=lambda h, t: k.queryT[:, h // 2, P * t:P * (t + 1)], value=lambda h, kt: k.values[:, kt, HD * h:HD * (h + 1)],
            wo=lambda o: w.wo[:, o, :], obias=w.obias[:, 0:1])
        with nc.Fori(0, BATCH) as b:
            softmax_attention_stage(nc, k, b, main)
        route_stage(nc, k, w)

        def of(p, i):
            return (w.qkv_l if p < 4 else w.qkv_h)[:, i, P * (p % 4):P * (p % 4 + 1)]
        routed = Names(
            kind="l0ffn", w=w, wq=lambda p: of(p, 0), wk=lambda p: of(p, 1), wv=lambda half: (w.qkv_h if half else w.qkv_l)[:, 2, :],
            qbias=lambda p: 0.0, query=main.query, value=main.value, wo=lambda o: (w.wo_l if o < 4 else w.wo_h)[:, o % 4, :])
        with nc.Fori(0, BATCH) as b:
            softmax_attention_stage(nc, k, b, routed)


def layer1(nc, k, d):
    with ExitStack() as held:
        def sb(name, shape):
            return held.enter_context(nc.sbuf_tensor(name, shape, F32))
        w = Names(
            w_q=sb("w_q", [P, 256]), w_k=sb("w_k", [P, 256]), w_k_enc=sb("w_k_enc", [P, 256]), w_v=sb("w_v", [P, 1024]),
            w_v_enc=sb("w_v_enc", [P, 1024]), w_out=sb("w_out", [P, PAIRS, P]), router=sb("router1", [P, L1_E]),
            w1=sb("w1", [P, L1_E * L1_H]), w3=sb("w3", [P, L1_E * L1_H]), w2=sb("w2", [P, L1_HC, P]),
            expert_of=sb("expert_of", [P, L1_E * L1_H]), causal=sb("causal", [P, SEQ + P]), ones=sb("ones", [P, HD]),
            kT=sb("kT", [P, 2, SEQ]), k_encT=sb("k_encT", [P, 2, L1_ENC]), v_enc=sb("v_enc", [P, 1024]), kernel=sb("kernel", [P, 3, SEQ + P]),
            kernel_enc=sb("kernel_enc", [P, 3, SEQ]), norm=sb("norm", [P, 2, SEQ]), silu=sb("silu", [P, 2, CHUNK]),
            hidden=sb("hidden1", [P, 3, CHUNK]))
        loads = [(dst, d[name]) for dst, name in (
            (w.w_q[:, :], "w_q1"), (w.w_k[:, :], "w_k1"), (w.w_k_enc[:, :], "w_k_enc1"), (w.w_v[:, :], "w_v1"), (w.w_v_enc[:, :], "w_v_enc1"),
            (w.w_out[:, :, :], "w_out1"), (w.router[:, :], "router1"), (w.w1[:, :], "w1_1"), (w.w3[:, :], "w3_1"), (w.w2[:, :, :], "w2_1"),
            (w.expert_of[:, :], "expert_of"), (w.causal[:, :], "causal"), (w.ones[:, :], "ones"))]
        layer_norm_stage(nc, k, loads)
        gate_stage(nc, k, w.router[:, :], False, zeros=(w.v_enc[:, :], w.kernel_enc[:, :, :]))
        with nc.Fori(0, BATCH) as b:
            taylor_attention_stage(nc, k, b, w)
        with nc.Fori(0, CHUNKS) as c:
            swiglu_experts_stage(nc, k, c, w)


def layer2(nc, k, d):
    with ExitStack() as held:
        def sb(name, shape):
            return held.enter_context(nc.sbuf_tensor(name, shape, F32))
        w = Names(
            w_rot=sb("w_rot", [P, 4, P]), w_v=sb("w_v2", [P, P]), wo=sb("wo2", [P, 4, P]), obias=sb("obias2", [P, 1]),
            router=sb("router2", [P, L2_E]), w1=sb("w1_2", [P, L2_E * L2_F]), w2=sb("w2_2", [P, L2_E * L2_FC, P]),
            padded_values=sb("padded_values", [P, SUB, HEADS, 32]), hidden=sb("hidden2", [P, 3, CHUNK]), gate_all=sb("gate_all", [P, 2, CHUNK]))
        loads = [(w.w_rot[:, :, :], d["w_rot"]), (w.w_v[:, :], d["w_v2"]), (w.wo[:, :, :], d["wo2"]), (w.obias[:, :], d["obias2"]),
                 (w.router[:, :], d["router2"]), (w.w1[:, :], d["w1_2"]), (w.w2[:, :, :], d["w2_2"])]
        layer_norm_stage(nc, k, loads)
        gate_stage(nc, k, w.router[:, :], True, zeros=(w.padded_values[:, :, :, :],))
        narrow = Names(
            kind="l2", w=w, query=lambda h, t: k.queryT[:, 0, P * t:P * (t + 1)], value=lambda h, kt: w.padded_values[:, kt, h, :],
            wo=lambda o: w.wo[:, o, :], obias=w.obias[:, 0:1])
        with nc.Fori(0, BATCH) as b:
            softmax_attention_stage(nc, k, b, narrow)
        with nc.Fori(0, CHUNKS) as c:
            relu_experts_stage(nc, k, c, w)


def store_stage(nc, k, out):
    with signals(nc, "stored") as s:
        with nc.Block() as block:
            @block.sync
            def _(sp):
                sp.dma_start(out, k.x[:, :, :]).then_inc(s.stored, 16)
                sp.wait_ge(s.stored, 16)


def build(nc, d, out, layers=4):
    with ExitStack() as held:
        def sb(name, shape):
            return held.enter_context(nc.sbuf_tensor(name, shape, F32))
        k = Names(
            dram=d, scratch=nc.dram_tensor("scratch", (BATCH, SEQ), F32, kind="Internal").ap(),
            psum_all=held.enter_context(nc.psum_tensor("psum_all", [P, 8 * CHUNK], F32)),
            x=sb("x", [P, TILES, P]), xn=sb("xn", [P, TILES, P]), xnT=sb("xnT", [P, TOKENS]), ident=sb("ident", [P, P]),
            stats=sb("stats", [P, TILES, 6]), moments=sb("moments", [P, TILES, 2]), rstd=sb("rstd", [P, TILES]), rms=sb("rms", [P, TILES]),
            logits=sb("logits", [16, SEQ]), logit_max=sb("logit_max", [16, 1]), neg_a=sb("neg_a", [16, 1]), floor_m=sb("floor_m", [16, 1]),
            logk=sb("logk", [16, 1]), route_arg=sb("route_arg", [16, SEQ]), route_exp=sb("route_exp", [16, SEQ]),
            route_sum=sb("route_sum", [16, 1]), route_log=sb("route_log", [16, 1]), route_cols=sb("route_cols", [P, 2, SUB, 16]),
            rank=sb("rank", [P, 2, TILES]), route_w=sb("route_w", [P, 3, TILES]), route_b=sb("route_b", [P, 3, SUB]),
            window_mask=sb("window_mask", [P, SUB, SEQ]), head16=sb("head16", [P, 8]), head8=sb("head8", [P, HEADS]),
            rot_cos=sb("rot_cos", [P, 2, SEQ]), rot_sin=sb("rot_sin", [P, 2, SEQ]),
            gateT=sb("gateT", [P, TOKENS]), gate=sb("gate", [P, TILES, 8]), gate_sum=sb("gate_sum", [P, TILES]),
            gate_rank=sb("gate_rank", [P, TILES, 8]), gate_cmp=sb("gate_cmp", [P, 8, TILES, 8]), y_chunk=sb("y_chunk", [P, CHUNK]))
        k.psum = [k.psum_all[:, CHUNK * i:CHUNK * (i + 1)] for i in range(8)]
        with ExitStack() as attn:
            def sa(name, shape):
                return attn.enter_context(nc.sbuf_tensor(name, shape, F32))
            k.norm8 = sa("norm8", [P, 8, P])
            k.xb = sa("xb", [P, 2, SEQ])
            k.keys = sa("keys", [P, HEADS, SEQ])
            k.queryT = sa("queryT", [P, PAIRS, SEQ])
            k.values = sa("values", [P, SUB, HEADS * HD])
            k.probs = sa("probs", [P, PBUF, SUB, SEQ])
            k.probsT = sa("probsT", [P, 3, SUB, SEQ])
            k.outT = sa("outT", [P, PAIRS, SEQ])
            k.yT = sa("yT", [P, 2, SEQ])
            k.masked_scores = sa("masked_scores", [P, 2, SUB, SEQ])
            k.negmax = sa("negmax", [P, HEADS, SUB])
            k.null_scores = sa("null_scores_sb", [P, 2, 2 * SUB])
            k.key_negmax = sa("key_negmax", [P, SUB])
            k.prob_sum = sa("prob_sum", [P, HEADS, SUB])
            k.recip = sa("recip", [P, HEADS, SUB])
            k.null_arg = sa("null_arg", [P, PAIRS, SUB])
            k.null_exp = sa("null_exp", [P, PAIRS, SUB])
            k.null_probs = sa("null_probs", [P, SUB, PAIRS])
            k.null_probsT = sa("null_probsT", [P, SEQ])
            k.mix = sa("mix", [P, SUB, P])
            k.rot = sa("rot", [P, 2, SEQ])
            k.rot2 = sa("rot2", [P, 2, SEQ])
            layer0(nc, k, d)
            if layers > 1:
                layer1(nc, k, d)
            if layers > 2:
                layer2(nc, k, d)
        if layers > 3:
            layer3(nc, k, d)
        store_stage(nc, k, out)


def rows_first(a, n):
    return a.reshape(n, P, -1).transpose(1, 0, 2)


def lay_out(i):
    z = np.zeros
    f = np.float32
    a = {}
    a["x"] = i["L0_attn_z"]
    a["ident"] = np.eye(P, dtype=f)
    a["cols"] = np.stack([i["L0_ffn_ln_g"], i["L0_ffn_ln_b"], i["L0_ffn_rms_g"]], 1)
    a["inT"] = np.stack([i[f"L0_attn_{n}"].T for n in ("wq", "wk", "wv")], 1)
    a["fc"] = np.stack([i[f"L0_attn_{n}"] for n in ("fcq_w", "fck_w", "fcv_w")], 1)
    a["qbias"] = i["L0_attn_fcq_b"].reshape(PAIRS, P).T
    a["kbias"] = i["L0_attn_fck_b"].reshape(PAIRS, P).T
    a["vbias"] = i["L0_attn_fcv_b"]
    a["obias0"] = i["L0_attn_fco_b"].reshape(P, 1)
    a["wo0"] = rows_first(i["L0_attn_fco_w"], PAIRS)
    a["qkv_l"] = i["L0_ffn_w_qkv_l"].reshape(P, 3, 512)
    kv = i["L0_ffn_w_kv_h"]
    a["qkv_h"] = np.stack([i["L0_ffn_w_q_h"], kv[:, :, :HD].reshape(P, 512), kv[:, :, HD:].reshape(P, 512)], 1)
    a["wo_l"] = rows_first(i["L0_ffn_w_out_l"], 4)
    a["wo_h"] = rows_first(i["L0_ffn_w_out_h"], 4)
    nk, nv = i["L0_ffn_null_kv"]
    null_k, null_v = z((P, 4, 2), f), z((P, 4, 8), f)
    for h in range(PAIRS):
        rows = slice(HD * (h % 2), HD * (h % 2 + 1))
        null_k[rows, h // 2, h % 2] = nk[h]
        null_v[rows, h // 2, h] = nv[h]
    a["null_k"], a["null_v"] = null_k, null_v
    a["null_q"] = i["L0_ffn_null_q"]
    rt = z((P, BATCH, 16), f)
    for b in range(BATCH):
        rt[:, b, b] = i["L0_ffn_rt_q"][0]
        rt[:, b, BATCH + b] = i["L0_ffn_rt_kv"][0]
    a["route_tokens"] = rt
    a["logk"] = np.log(np.array([[KQ]] * BATCH + [[KKV]] * BATCH, f))
    token = np.arange(SEQ)
    mine = (np.arange(P)[:, None, None] + P * np.arange(SUB)[None, :, None])
    a["window_mask"] = np.where(abs(mine // 64 - token // 64) <= 1, 0.0, -3e38).astype(f)
    a["earlier"] = (token < mine).astype(f)
    r = np.arange(P)
    a["head16"] = (r[:, None] // L1_FD == np.arange(8)).astype(f)
    a["head8"] = (r[:, None] // L2_D == np.arange(HEADS)).astype(f)
    inv = (f(1.0) / f(10000.0) ** (np.arange(0, L2_D, 2, dtype=f) / f(L2_D))).astype(f)
    angle = (token.astype(f)[None, :] * inv[r % L2_D % 4][:, None]).astype(f)
    sign = np.where(r % L2_D < 4, -1.0, 1.0)[:, None]
    scale = np.array([L2_D ** -0.5, 1.0])[None, :, None]
    a["rot_cos"] = (np.cos(angle.astype(np.float64))[:, None, :] * scale).astype(f)
    a["rot_sin"] = ((sign * np.sin(angle.astype(np.float64)))[:, None, :] * scale).astype(f)
    for n, m in (("w_q1", "Wq"), ("w_k1", "Wk"), ("w_k_enc1", "Wk_enc"), ("w_v1", "Wv"), ("w_v_enc1", "Wv_enc")):
        a[n] = i[f"L1_attn_{m}"].T
    a["w_out1"] = rows_first(i["L1_attn_Wout"].T, PAIRS)
    a["router1"] = i["L1_ffn_w_router"].T
    a["w1_1"] = i["L1_ffn_w1"].transpose(1, 0, 2).reshape(P, -1)
    a["w3_1"] = i["L1_ffn_w3"].transpose(1, 0, 2).reshape(P, -1)
    a["w2_1"] = rows_first(i["L1_ffn_w2"].reshape(-1, P), L1_HC)
    a["expert_of"] = (np.arange(L1_E * L1_H)[None, :] // L1_H == r[:, None]).astype(f)
    c = np.arange(P)
    tri = (c[None, :] >= r[:, None]).astype(f)
    a["causal"] = np.concatenate([tri, np.ones((P, P), f), tri], 1)
    a["ones"] = np.ones((P, HD), f)
    w = i["L2_attn_w_qkv"].reshape(3, HEADS, L2_D, P)
    straight, swapped = [0, 2, 4, 6, 1, 3, 5, 7], [1, 3, 5, 7, 0, 2, 4, 6]
    a["w_rot"] = np.stack([w[n][:, order].reshape(P, P).T for order in (straight, swapped) for n in (0, 1)], 1)
    a["w_v2"] = w[2].reshape(P, P).T
    wo = z((4, 32, 4, P), f)
    wo[:, :L2_D] = i["L2_attn_w_proj"].T.reshape(4, 4, L2_D, P).transpose(1, 2, 0, 3)
    a["wo2"] = wo.reshape(P, 4, P)
    a["obias2"] = i["L2_attn_b_proj"].reshape(P, 1)
    a["router2"] = i["L2_ffn_Wr"]
    a["w1_2"] = i["L2_ffn_W1"].transpose(1, 0, 2).reshape(P, -1)
    a["w2_2"] = rows_first(i["L2_ffn_W2"].reshape(-1, P), L2_E * L2_FC)
    a["w_in3"] = i["L3_attn_W_in"].T
    a["conv_w"] = i["L3_attn_conv_w"].reshape(L3_DC, P, L3_CONV).transpose(1, 0, 2)
    a["w_x"] = rows_first(i["L3_attn_W_x"].T, L3_DC)
    a["a_log"] = rows_first(i["L3_attn_A_log"], L3_DC)
    w_dt = z((P, L3_DC, P), f)
    w_dt[2 * L3_N] = i["L3_attn_W_dt"].reshape(L3_DC, P)
    a["w_dt"] = w_dt
    for n, m in (("conv_b", "conv_b"), ("d_skip", "D_param"), ("b_dt", "b_dt")):
        a[n] = i[f"L3_attn_{m}"].reshape(L3_DC, P).T
    a["w_out3"] = rows_first(i["L3_attn_W_out"].T, L3_DC)
    a["codes"] = i["L3_ffn_qweights"].transpose(1, 0, 2)
    a["scales"] = i["L3_ffn_scales"].transpose(1, 0, 2).reshape(P, -1)
    a["lora_a"] = i["L3_ffn_lora_a"].transpose(1, 0, 2)
    a["lora_b"] = i["L3_ffn_lora_b"].transpose(2, 0, 1)
    a["gamma"], a["beta"] = i["L3_ffn_ln_gamma"].T, i["L3_ffn_ln_beta"].T
    a["bias_rows"] = i["L3_ffn_biases"][0::2].reshape(-1)
    a["bias_cols"] = i["L3_ffn_biases"][1::2].T
    return {n: np.ascontiguousarray(v) for n, v in a.items()}


def kernel(**inputs):
    import concourse.bacc as bacc
    from concourse.bass_utils import run_bass_kernel_spmd

    nc = bacc.Bacc("TRN2", target_bir_lowering=False, num_devices=1)
    arrays = lay_out({n: np.asarray(v) for n, v in inputs.items()})
    d = {n: nc.dram_tensor(n + "_dram", v.shape, mybir.dt.from_np(v.dtype), kind="ExternalInput").ap() for n, v in arrays.items()}
    d["x"] = d["x"].rearrange("b (s p) n -> p (b s) n", p=P)
    out = nc.dram_tensor("out_dram", (BATCH, SEQ, DIM), F32, kind="ExternalOutput").ap()
    build(nc, d, out.rearrange("b (s p) n -> p (b s) n", p=P))
    r = run_bass_kernel_spmd(nc, [{n + "_dram": v for n, v in arrays.items()}], core_ids=[0])
    return r.results[0]["out_dram"]
```

```python
from contextlib import ExitStack, contextmanager

import numpy as np
import concourse.bass as bass
from concourse import mybir

F32 = mybir.dt.float32
I32 = mybir.dt.int32
ALU = mybir.AluOpType
ACT = mybir.ActivationFunctionType
AXX = mybir.AxisListType.X

BATCH, SEQ, DIM = 8, 256, 128
P = 128
TOKENS = BATCH * SEQ
TILES = TOKENS // P
SUB = SEQ // P
CHUNK = 512
CHUNKS = TOKENS // CHUNK
CT = CHUNK // P
LN_EPS = 1e-5

HEADS = 16
HD = 64
PAIRS = HEADS // 2
DESCENTS = 50
NQ, NKV = 128, 256
KQ, KKV = NQ * 9.0 / 8.0, NKV * 9.0 / 8.0
DESCENTS_PER_SEQ = 6

L1_FD = 16
L1_ENC = 64
L1_EPS = 1e-12
L1_E, L1_H = 8, 176
L1_HC = L1_E * L1_H // P
L2_D = 8
L2_E, L2_F = 8, 512
L2_FC = L2_F // P
L3_IN, L3_N, L3_CONV = 256, 16, 4
L3_DC = L3_IN // P
L3_R, L3_GROUP, L3_LIN = 32, 16, 6



class Names(dict):

    def __getattr__(self, name):
        return self[name]


@contextmanager
def signals(nc, *names):
    with ExitStack() as held:
        sems = {n: held.enter_context(nc.semaphore(n)) for n in names}
        yield Names(**sems)
        for s in sems.values():
            nc.sync.sem_clear(s)
        nc.all_engine_barrier()


class Steps:

    def __init__(self, engine, sem):
        self.engine, self.sem, self.n = engine, sem, 0

    def add(self, instruction):
        instruction.then_inc(self.sem, 1)
        self.n += 1
        return self.n

    def wait(self):
        self.engine.wait_ge(self.sem, self.n)


def bank(k, i):
    return k.psum[i]



def layer_norm_stage(nc, k, loads=(), first=None):
    with signals(nc, "x_loaded", "weights_loaded", "dve_step", "moments_ready", "rstd_ready", "tile_normed", "group_turned", "group_saved") as s:
        with nc.Block() as block:
            @block.sync
            def _(sp):
                if first is not None:
                    sp.dma_start(k.x[:, :, :], first).then_inc(s.x_loaded, 16)
                    sp.dma_start(k.ident[:, :], k.dram["ident"]).then_inc(s.x_loaded, 16)
                for dst, src in loads:
                    sp.dma_start(dst, src).then_inc(s.weights_loaded, 16)
                if loads:
                    sp.wait_ge(s.weights_loaded, 16 * len(loads))

            @block.vector
            def _(dve):
                step = Steps(dve, s.dve_step)
                if first is not None:
                    dve.wait_ge(s.x_loaded, 32)
                for t in range(TILES):
                    step.add(nc.vector.bn_stats(k.stats[:, t, :], k.x[:, t, :]))
                step.wait()
                for t in range(TILES):
                    step.add(nc.vector.bn_aggr(k.moments[:, t, :], k.stats[:, t, :]))
                step.wait()
                step.add(nc.vector.tensor_scalar(k.rstd[:, :], k.moments[:, :, 1], LN_EPS, None, ALU.add))
                step.wait()
                nc.vector.reciprocal(k.rstd[:, :], k.rstd[:, :]).then_inc(s.moments_ready, 1)
                dve.wait_ge(s.rstd_ready, 1)
                for t in range(TILES):
                    nc.vector.tensor_scalar(k.xn[:, t, :], k.x[:, t, :], k.moments[:, t, 0:1], k.rstd[:, t:t + 1],
                                            ALU.subtract, ALU.mult).then_inc(s.tile_normed, 1)


            @block.tensor
            def _(pe):
                if first is not None:
                    pe.wait_ge(s.x_loaded, 32)
                for g in range(CHUNKS):
                    pe.wait_ge(s.tile_normed, CT * (g + 1))
                    if g >= 2:
                        pe.wait_ge(s.group_saved, g - 1)
                    for j in range(CT):
                        last = nc.tensor.transpose(bank(k, g % 2)[:, P * j:P * (j + 1)], k.xn[:, CT * g + j, :], k.ident[:, :])
                    last.then_inc(s.group_turned, 1)

            @block.scalar
            def _(act):
                act.wait_ge(s.moments_ready, 1)
                nc.scalar.activation(k.rstd[:, :], k.rstd[:, :], ACT.Sqrt).then_inc(s.rstd_ready, 1)
                for g in range(CHUNKS):
                    act.wait_ge(s.group_turned, g + 1)
                    nc.scalar.activation(k.xnT[:, CHUNK * g:CHUNK * (g + 1)], bank(k, g % 2)[:, :], ACT.Copy).then_inc(s.group_saved, 1)


def layer0_prepare_stage(nc, k, w):
    with signals(nc, "dve_step", "moments_ready", "factors_ready", "light_normed", "rms_normed", "turned", "saved", "logits_made", "logits_saved", "route_dve", "route_act",
                 "fused_made", "fused_saved", "nullw_made", "act_step", "pool_step") as s:
        with nc.Block() as block:
            @block.vector
            def _(dve):
                step = Steps(dve, s.dve_step)
                for t in range(TILES):
                    step.add(nc.vector.bn_stats(k.stats[:, t, :], k.xn[:, t, :]))
                step.wait()
                for t in range(TILES):
                    step.add(nc.vector.bn_aggr(k.moments[:, t, :], k.stats[:, t, :]))
                step.wait()
                step.add(nc.vector.tensor_tensor(k.rms[:, :], k.moments[:, :, 0], k.moments[:, :, 0], ALU.mult))
                step.wait()
                step.add(nc.vector.tensor_tensor(k.rms[:, :], k.rms[:, :], k.moments[:, :, 1], ALU.add))
                step.wait()
                step.add(nc.vector.tensor_scalar(k.rms[:, :], k.rms[:, :], float(DIM), 1e-24, ALU.mult, ALU.max))
                step.add(nc.vector.tensor_scalar(k.rstd[:, :], k.moments[:, :, 1], LN_EPS, None, ALU.add))
                step.wait()
                nc.vector.reciprocal(k.rms[:, :], k.rms[:, :]).then_inc(s.moments_ready, 1)
                nc.vector.reciprocal(k.rstd[:, :], k.rstd[:, :]).then_inc(s.moments_ready, 1)
                dve.wait_ge(s.factors_ready, 2)
                for t in range(TILES):
                    if t >= 8:
                        dve.wait_ge(s.turned, (t - 8) // CT + 1)
                    nc.vector.tensor_scalar(k.norm8[:, t % 8, :], k.xn[:, t, :], k.moments[:, t, 0:1], k.rstd[:, t:t + 1],
                                            ALU.subtract, ALU.mult).then_inc(s.light_normed, 1)
                for t in range(TILES):
                    dve.wait_ge(s.turned, (t + 8) // CT + 1)
                    nc.vector.tensor_scalar(k.norm8[:, t % 8, :], k.xn[:, t, :], k.rms[:, t:t + 1], None, ALU.mult).then_inc(s.rms_normed, 1)
                dve.wait_ge(s.logits_made, 1)
                step.add(nc.vector.tensor_copy(k.logits[:, :], bank(k, 7)[0:16, 0:SEQ]))
                step.wait()
                step.add(nc.vector.reduce_max(k.logit_max[:, :], k.logits[:, :], AXX))
                step.add(nc.vector.tensor_scalar(k.neg_a[:, :], k.logk[:, :], -1.0, float(np.log(np.float32(SEQ))), ALU.mult, ALU.add))
                step.wait()
                step.add(nc.vector.tensor_scalar(k.floor_m[:, :], k.neg_a[:, :], k.logit_max[:, :], None, ALU.min))
                for i in range(1, DESCENTS - BATCH * DESCENTS_PER_SEQ):
                    step.wait()
                    descend_dve_first(nc, k).then_inc(s.route_dve, 1)
                    dve.wait_ge(s.route_act, i)
                    step.add(descend_dve_a(nc, k))
                    step.wait()
                    step.add(descend_dve_m(nc, k))

            @block.scalar
            def _(act):
                act.wait_ge(s.moments_ready, 2)
                nc.scalar.activation(k.rstd[:, :], k.rstd[:, :], ACT.Sqrt).then_inc(s.factors_ready, 1)
                nc.scalar.activation(k.rms[:, :], k.rms[:, :], ACT.Sqrt, scale=float(DIM)).then_inc(s.factors_ready, 1)
                for g in range(2 * CHUNKS):
                    light = g < CHUNKS
                    act.wait_ge(s.turned, g + 1)
                    dst = (w.xlT if light else w.xrT)[:, CHUNK * (g % CHUNKS):CHUNK * (g % CHUNKS + 1)]
                    if light:
                        ins = nc.scalar.activation(dst, bank(k, g % 2)[:, :], ACT.Identity, scale=w.cols[:, 0:1], bias=w.cols[:, 1:2])
                    else:
                        ins = nc.scalar.activation(dst, bank(k, g % 2)[:, :], ACT.Copy, scale=w.cols[:, 2:3])
                    ins.then_inc(s.saved, 1)
                for i in range(6):
                    act.wait_ge(s.fused_made, i + 1)
                    nc.scalar.activation(w.fused[:, i // 2, CHUNK * (i % 2):CHUNK * (i % 2 + 1)], bank(k, 2 + i % 2)[:, :], ACT.Copy)\
                        .then_inc(s.fused_saved, 1)
                act.wait_ge(s.nullw_made, 1)
                act.wait_ge(s.pool_step, 2)
                nc.scalar.activation(w.null_out[0:8, :], bank(k, 4)[0:8, 0:P], ACT.Copy).then_inc(s.act_step, 1)
                nc.scalar.activation(w.qbias[:, :], w.qbias[:, :], ACT.Copy, scale=HD ** -0.5).then_inc(s.act_step, 1)
                nc.scalar.preload_act_table_set("natural_log_exp_and_others")
                for i in range(1, DESCENTS - BATCH * DESCENTS_PER_SEQ):
                    act.wait_ge(s.route_dve, i)
                    nc.scalar.activation(k.route_exp[:, :], k.route_arg[:, :], ACT.Exp, accum_out=k.route_sum[:, :]).then_inc(s.act_step, 1)
                    act.wait_ge(s.act_step, 2 + i)
                    nc.scalar.activation(k.route_log[:, :], k.route_sum[:, :], ACT.Ln).then_inc(s.route_act, 1)

            @block.gpsimd
            def _(pool):
                nc.gpsimd.memset(w.null_out[:, :], 0.0).then_inc(s.pool_step, 1)
                nc.gpsimd.memset(k.null_probsT[:, :], 0.0).then_inc(s.pool_step, 1)
                nc.gpsimd.memset(k.keys[:, :, :], 0.0).then_inc(s.pool_step, 1)

            @block.tensor
            def _(pe):
                for g in range(2 * CHUNKS):
                    light = g < CHUNKS
                    if light:
                        pe.wait_ge(s.light_normed, CT * (g + 1))
                    else:
                        pe.wait_ge(s.rms_normed, CT * (g - CHUNKS + 1))
                    if g >= 2:
                        pe.wait_ge(s.saved, g - 1)
                    for j in range(CT):
                        last = nc.tensor.transpose(bank(k, g % 2)[:, P * j:P * (j + 1)], k.norm8[:, (CT * g + j) % 8, :], k.ident[:, :])
                    last.then_inc(s.turned, 1)
                for b in range(BATCH):
                    last = nc.tensor.matmul(bank(k, 7)[0:16, 0:SEQ], w.route_tokens[:, b, :], k.xnT[:, SEQ * b:SEQ * (b + 1)],
                                            start=(b == 0), stop=(b == BATCH - 1))
                last.then_inc(s.logits_made, 1)
                for i in range(6):
                    if i >= 2:
                        pe.wait_ge(s.fused_saved, i - 1)
                    nc.tensor.matmul(bank(k, 2 + i % 2)[:, :], w.inT[:, i // 2, :], w.fc[:, i // 2, CHUNK * (i % 2):CHUNK * (i % 2 + 1)],
                                     start=True, stop=True).then_inc(s.fused_made, 1)
                for c in range(4):
                    last = nc.tensor.matmul(bank(k, 4)[0:8, 0:P], w.null_v[:, c, :], w.wo_h[:, c, :], start=(c == 0), stop=(c == 3))
                last.then_inc(s.nullw_made, 1)


def descend_dve_first(nc, k):
    return nc.vector.tensor_scalar(k.route_arg[:, :], k.logits[:, :], k.neg_a[:, :], k.floor_m[:, :], ALU.min, ALU.subtract)


def descend_dve_a(nc, k):
    return nc.vector.tensor_scalar(k.neg_a[:, :], k.route_log[:, :], k.floor_m[:, :], k.logk[:, :], ALU.add, ALU.subtract)


def descend_dve_m(nc, k):
    return nc.vector.tensor_scalar(k.floor_m[:, :], k.neg_a[:, :], k.logit_max[:, :], None, ALU.min)



PT_LAG, PV_LAG = 2, 3
PBUF = 4
SEQS = 2


def attention_jobs(kind):
    before, at = [], [[] for _ in range(SEQS * HEADS + 6)]
    for q in range(SEQS):
        if kind == "l2":
            first = [("straight", q, 0), ("swapped", q, 0), ("narrow_values", q, 0)]
        else:
            first = [("pair", q, 0)] + [("values", q, i) for i in range(2 * SUB)]
        if q == 0:
            before += first
        elif kind == "l2":
            for i, job in enumerate(first):
                at[HEADS * (q - 1) + 5 + 2 * i].append(job)
        else:
            for i, job in enumerate(first[1:]):
                at[HEADS * (q - 1) + 5 + 2 * i].append(job)
            at[HEADS * q - 2].append(first[0])
        if kind != "l2":
            for p in range(1, PAIRS):
                at[HEADS * q + 2 * (p - 1)].append(("pair", q, p))
        if kind == "l0ffn":
            at[HEADS * (q + 1) + 3].append(("null_probs", q, 0))
        at[HEADS * (q + 1) + 4].append(("output", q, 0))
        at[HEADS * (q + 1) + 5].append(("output_turned", q, 0))
    return before, at


def softmax_attention_stage(nc, k, b, c):
    l0, ffn, l2 = c.kind == "l0", c.kind == "l0ffn", c.kind == "l2"
    per_out = 4 if l2 else 2
    outs = HEADS // per_out
    mcols = P // per_out
    SB, TB, OB, JB = (0, 1), (3, 4), (5, 6), (7, 2)
    N = SEQS * HEADS
    before, at = attention_jobs(c.kind)
    order = before + [job for jobs in at for job in jobs]
    number = {job: i for i, job in enumerate(order)}
    steps = range(N + 6)

    def job_bank(job):
        return k.psum[JB[number[job] % 2]]

    def saver(job):
        what, _, i = job
        if what in ("null_probs", "output") or (ffn and what == "values" and i % 2):
            return "act"
        return "dve"

    def saved_count(job):
        return sum(saver(j) == saver(job) for j in order[:number[job] + 1])

    def masked(g):
        return ffn and g % HEADS < PAIRS

    def nulled(g):
        return ffn and g % HEADS >= PAIRS

    def null_pairs(g):
        return 4 * (g // HEADS) + g % HEADS // 2 - 3

    def null_heads(g):
        return PAIRS * (g // HEADS) + g % HEADS - PAIRS + 1

    def by_act(g):
        return g % 2 == 1 if l2 else g % 4 == 3 if ffn else False

    with signals(nc, "x_copied", "job_made", "query_saved", "act_saved_job", "dve_saved_job", "head_keys", "scores_ready",
                 "masked_ready", "negmax_ready", "probs_ready", "recip_ready", "probs_normed", "turned", "dve_turned", "act_turned",
                 "values_weighed", "out_saved", "null_scores", "null_taken", "null_args", "null_exps", "null_weights", "weights_picked",
                 "route_dve", "route_act", "act_step", "dve_step") as s:

        def wait_saved(engine, job):
            engine.wait_ge(s.act_saved_job if saver(job) == "act" else s.dve_saved_job, saved_count(job))

        def wait_made(engine, job):
            engine.wait_ge(s.job_made, number[job] + 1)

        with nc.Block() as block:

            @block.gpsimd
            def _(pool):
                def copy_inputs(q):
                    cols = bass.ds((b * SEQS + q) * SEQ, SEQ)
                    for i, src in enumerate((c.w.xlT, c.w.xrT) if ffn else (k.xnT,)):
                        nc.gpsimd.tensor_copy(k.xb[:, q % 2, i, :], src[:, cols]).then_inc(s.x_copied, 1)

                for q in range(min(SEQS, 2)):
                    copy_inputs(q)
                for q in range(SEQS):
                    if l2:
                        pool.wait_ge(s.query_saved, q + 1)
                        for h in range(HEADS):
                            if q:
                                pool.wait_ge(s.scores_ready, HEADS * (q - 1) + h + 1)
                            nc.gpsimd.tensor_scalar(k.keys[:, h, :], k.rot[:, q % 2, 1, :], k.head8[:, h:h + 1], None, ALU.mult).then_inc(s.head_keys, 1)

            @block.tensor
            def _(pe):
                def do(job):
                    what, q, i = job
                    n = number[job]
                    if n >= 2:
                        wait_saved(pe, order[n - 2])
                    jb = job_bank(job)
                    xb = k.xb[:, q % 2]
                    if what in ("pair", "values", "straight"):
                        pe.wait_ge(s.x_copied, (2 if ffn else 1) * (q + 1))
                    if what == "pair":
                        src = xb[:, 1 if ffn and i >= 4 else 0, :]
                        nc.tensor.matmul(jb[:, 0:SEQ], c.wq(i), src, start=True, stop=True)
                        last = nc.tensor.matmul(jb[:, SEQ:2 * SEQ], c.wk(i), src, start=True, stop=True)
                    elif what == "values":
                        t, half = i // 2, i % 2
                        last = nc.tensor.matmul(jb[:, :], xb[:, 1 if ffn and half else 0, P * t:P * (t + 1)], c.wv(half), start=True, stop=True)
                    elif what in ("straight", "swapped"):
                        for j in range(2):
                            last = nc.tensor.matmul(jb[:, SEQ * j:SEQ * (j + 1)], c.w.w_rot[:, (what == "swapped") * 2 + j, :], xb[:, 0, :],
                                                    start=True, stop=True)
                    elif what == "narrow_values":
                        for t in range(SUB):
                            last = nc.tensor.matmul(jb[:, P * t:P * (t + 1)], xb[:, 0, P * t:P * (t + 1)], c.w.w_v[:, :], start=True, stop=True)
                    elif what == "null_probs":
                        pe.wait_ge(s.null_weights, PAIRS * (q + 1))
                        for t in range(SUB):
                            last = nc.tensor.transpose(jb[0:8, P * t:P * (t + 1)], k.null_probs[:, t, :], k.ident[:, :])
                    elif what == "output":
                        pe.wait_ge(s.out_saved, outs * (q + 1))
                        for g, (o0, o1) in enumerate([(0, 4), (4, 8)] if ffn else [(0, outs)]):
                            for o in range(o0, o1):
                                last = nc.tensor.matmul(jb[:, SEQ * g:SEQ * (g + 1)], c.wo(o), k.outT[:, q % 2, o, :],
                                                        start=(o == o0), stop=(o == o1 - 1 and g == 0))
                            if g == 1:
                                wait_saved(pe, ("null_probs", q, 0))
                                last = nc.tensor.matmul(jb[:, SEQ:2 * SEQ], c.w.null_out[:, :], k.null_probsT[:, :], start=False, stop=True)
                    else:
                        wait_saved(pe, ("output", q, 0))
                        for g in range(2 if ffn else 1):
                            for t in range(SUB):
                                last = nc.tensor.transpose(jb[:, SEQ * g + P * t:SEQ * g + P * (t + 1)], k.yT[:, g, P * t:P * (t + 1)], k.ident[:, :])
                    last.then_inc(s.job_made, 1)

                def scores(g):
                    q, h = g // HEADS, g % HEADS
                    if l2:
                        pe.wait_ge(s.query_saved, q + 1)
                        pe.wait_ge(s.head_keys, g + 1)
                    else:
                        wait_saved(pe, ("pair", q, h // 2))
                    if g >= 2:
                        if masked(g - 2):
                            pe.wait_ge(s.masked_ready, PAIRS * ((g - 2) // HEADS) + (g - 2) % HEADS + 1)
                        else:
                            pe.wait_ge(s.probs_ready, 2 * (g - 1))
                    sb = k.psum[SB[g % 2]]
                    for t in range(SUB):
                        last = nc.tensor.matmul(sb[:, SEQ * t:SEQ * (t + 1)], c.query(q, h, t), k.keys[:, h, :], start=True, stop=True)
                    last.then_inc(s.scores_ready, 1)

                def null_scores(g):
                    q, p = g // HEADS, g % HEADS // 2
                    jb = job_bank(("pair", q, p))
                    for t in range(SUB):
                        last = nc.tensor.matmul(jb[:, 2 * t:2 * t + 2], c.query(q, 2 * p, t), c.w.null_k[:, p - 4, :], start=True, stop=True)
                    last.then_inc(s.null_scores, 1)

                def wait_turned(g):
                    mine = sum(by_act(i) == by_act(g) for i in range(g + 1))
                    pe.wait_ge(s.act_turned if by_act(g) else s.dve_turned, mine)

                def turn(g):
                    pe.wait_ge(s.probs_normed, 2 * (g + 1))
                    if g >= 2:
                        wait_turned(g - 2)
                    tb = k.psum[TB[g % 2]]
                    for kt in range(SUB):
                        for t in range(SUB):
                            last = nc.tensor.transpose(tb[:, SEQ * kt + P * t:SEQ * kt + P * (t + 1)],
                                                       k.probs[:, g % PBUF, t, P * kt:P * (kt + 1)], k.ident[:, :])
                    last.then_inc(s.turned, 1)

                def weigh_values(g):
                    wait_turned(g)
                    q, h = g // HEADS, g % HEADS
                    o = g // per_out
                    if h == 0:
                        for job in [("narrow_values", q, 0)] if l2 else [("values", q, 2), ("values", q, 3)]:
                            wait_saved(pe, job)
                    if o >= 2 and g % per_out == 0:
                        pe.wait_ge(s.out_saved, o - 1)
                    r = mcols * (g % per_out)
                    for kt in range(SUB):
                        last = nc.tensor.matmul(k.psum[OB[o % 2]][r:r + mcols, 0:SEQ], c.value(q, h, kt), k.probsT[:, g % 3, kt, :],
                                                start=(kt == 0), stop=(kt == SUB - 1))
                    last.then_inc(s.values_weighed, 1)

                for job in before:
                    do(job)
                for g in steps:
                    if g < N:
                        scores(g)
                        if nulled(g) and g % 2 == 0:
                            null_scores(g)
                            pe.wait_ge(s.null_taken, null_pairs(g))
                    for job in at[g]:
                        do(job)
                    if 0 <= g - PT_LAG < N:
                        turn(g - PT_LAG)
                    if 0 <= g - PV_LAG < N:
                        weigh_values(g - PV_LAG)

            @block.scalar
            def _(act):
                def do(job):
                    what, q, i = job
                    jb = job_bank(job)
                    if what == "pair":
                        wait_made(act, job)
                        nc.scalar.activation(k.queryT[:, i, :], jb[:, 0:SEQ], ACT.Identity, scale=HD ** -0.5, bias=c.qbias(i)).then_inc(s.query_saved, 1)
                    elif saver(job) == "act":
                        wait_made(act, job)
                        if what == "values":
                            act.wait_ge(s.weights_picked, 1)
                            ins = nc.scalar.activation(k.values[:, q % 2, i // 2, CHUNK:2 * CHUNK], jb[:, :], ACT.Copy, scale=k.route_b[:, 2, SUB * q + i // 2:SUB * q + i // 2 + 1])
                        elif what == "null_probs":
                            ins = nc.scalar.activation(k.null_probsT[0:8, :], jb[0:8, 0:SEQ], ACT.Copy)
                        elif ffn:
                            ins = nc.scalar.activation(k.yT[:, :, :].rearrange("p g n -> p (g n)"), jb[:, :], ACT.Copy)
                        else:
                            ins = nc.scalar.activation(k.yT[:, 0, :], jb[:, 0:SEQ], ACT.Identity, bias=c.obias)
                        ins.then_inc(s.act_saved_job, 1)

                def exponentials(g):
                    act.wait_ge(s.negmax_ready, g + 1)
                    if g >= PBUF:
                        act.wait_ge(s.turned, g - PBUF + 1)
                    for t in range(SUB):
                        src = k.masked_scores[:, g % 2, t, :] if masked(g) else k.psum[SB[g % 2]][:, SEQ * t:SEQ * (t + 1)]
                        nc.scalar.activation(k.probs[:, g % PBUF, t, :], src, ACT.Exp, bias=k.negmax[:, g % HEADS, t:t + 1],
                                             accum_out=k.prob_sum[:, g % HEADS, t:t + 1]).then_inc(s.probs_ready, 1)
                    if nulled(g):
                        act.wait_ge(s.null_args, null_heads(g))
                        i = g % HEADS - PAIRS
                        nc.scalar.activation(k.null_exp[:, i, :], k.null_arg[:, i, :], ACT.Exp).then_inc(s.null_exps, 1)

                def save_out(o):
                    act.wait_ge(s.values_weighed, per_out * (o + 1))
                    nc.scalar.activation(k.outT[:, o // outs % 2, o % outs, :], k.psum[OB[o % 2]][:, 0:SEQ], ACT.Copy).then_inc(s.out_saved, 1)

                def save_turned(g):
                    act.wait_ge(s.turned, g + 1)
                    if g >= 3:
                        act.wait_ge(s.values_weighed, g - 2)
                    nc.scalar.activation(k.probsT[:, g % 3, :, :].rearrange("p a n -> p (a n)"), k.psum[TB[g % 2]][:, :], ACT.Copy)\
                        .then_inc(s.act_turned, 1)

                def descend(i):
                    act.wait_ge(s.route_dve, i + 1)
                    nc.scalar.activation(k.route_exp[:, :], k.route_arg[:, :], ACT.Exp, accum_out=k.route_sum[:, :]).then_inc(s.act_step, 1)
                    act.wait_ge(s.act_step, i + 1)
                    nc.scalar.activation(k.route_log[:, :], k.route_sum[:, :], ACT.Ln).then_inc(s.route_act, 1)

                for job in before:
                    do(job)
                for g in steps:
                    for job in at[g]:
                        do(job)
                    if 0 <= g - PT_LAG < N and by_act(g - PT_LAG):
                        save_turned(g - PT_LAG)
                    if g < N:
                        exponentials(g)
                    if l0 and g % 2 == 1 and g // 2 < SEQS * DESCENTS_PER_SEQ:
                        descend(g // 2)
                    done = g - PV_LAG
                    if 0 <= done < N and done % per_out == per_out - 1:
                        save_out(done // per_out)

            @block.vector
            def _(dve):
                step = Steps(dve, s.dve_step)

                def add_output(job):
                    _, q, _ = job
                    jb = job_bank(job)
                    tile = (b * SEQS + q) * SUB
                    rows = k.x[:, bass.ds(tile, SUB), :]
                    if not ffn:
                        return nc.vector.tensor_tensor(rows, rows, jb[:, 0:SEQ].rearrange("p (t n) -> p t n", t=SUB), ALU.add)
                    for t in range(SUB):
                        i = SUB * q + t
                        step.add(nc.vector.scalar_tensor_tensor(k.mix[:, t, :], jb[:, SEQ + P * t:SEQ + P * (t + 1)], k.route_b[:, 0, i:i + 1],
                                                                k.x[:, bass.ds(tile + t, 1), :].rearrange("p a n -> p (a n)"),
                                                                ALU.mult, ALU.add))
                    step.wait()
                    for t in range(SUB):
                        i = SUB * q + t
                        step.add(nc.vector.scalar_tensor_tensor(k.mix[:, t, :], c.w.null_q[:, :], k.route_b[:, 1, i:i + 1], k.mix[:, t, :],
                                                                ALU.mult, ALU.add))
                    step.wait()
                    return nc.vector.tensor_tensor(rows, k.mix[:, :, :], jb[:, 0:SEQ].rearrange("p (t n) -> p t n", t=SUB), ALU.add)

                def do(job):
                    what, q, i = job
                    jb = job_bank(job)
                    if saver(job) != "dve":
                        return
                    wait_made(dve, job)
                    if what == "pair":
                        dve.wait_ge(s.query_saved, PAIRS * q + i + 1)
                        for j in range(2):
                            rows = slice(HD * j, HD * (j + 1))
                            dst, src = k.keys[rows, 2 * i + j, :], jb[rows, SEQ:2 * SEQ]
                            if l0:
                                ins = nc.vector.tensor_scalar(dst, src, c.w.kbias[rows, i:i + 1], None, ALU.add)
                            else:
                                ins = nc.vector.tensor_copy(dst, src)
                    elif what == "values":
                        t, half = i // 2, i % 2
                        dst = k.values[:, q % 2, t, CHUNK * half:CHUNK * (half + 1)]
                        if l0:
                            ins = nc.vector.tensor_tensor(dst, jb[:, :], c.w.vbias[:, CHUNK * half:CHUNK * (half + 1)], ALU.add)
                        else:
                            ins = nc.vector.tensor_copy(dst, jb[:, :])
                    elif what == "straight":
                        ins = nc.vector.tensor_tensor(k.rot[:, q % 2, :, :], jb[:, :].rearrange("p (i n) -> p i n", i=2), k.rot_cos[:, :, :], ALU.mult)
                    elif what == "swapped":
                        ins = nc.vector.tensor_tensor(k.rot2[:, :, :], jb[:, :].rearrange("p (i n) -> p i n", i=2), k.rot_sin[:, :, :], ALU.mult)
                        ins.then_inc(s.dve_saved_job, 1)
                        wait_saved(dve, job)
                        nc.vector.tensor_tensor(k.rot[:, q % 2, :, :], k.rot[:, q % 2, :, :], k.rot2[:, :, :], ALU.add).then_inc(s.query_saved, 1)
                        return
                    elif what == "narrow_values":
                        ins = nc.vector.tensor_copy(c.w.padded_values[:, q % 2, :, :, 0:L2_D],
                                                    jb[:, 0:SEQ].rearrange("p (t h d) -> p t h d", t=SUB, d=L2_D))
                    else:
                        ins = add_output(job)
                    ins.then_inc(s.dve_saved_job, 1)

                def negmax(g):
                    dve.wait_ge(s.scores_ready, g + 1)
                    h = g % HEADS
                    sb = k.psum[SB[g % 2]][:, :].rearrange("p (t n) -> p t n", t=SUB)
                    if masked(g):
                        n = PAIRS * (g // HEADS) + h + 1
                        if g >= 2:
                            dve.wait_ge(s.probs_ready, 2 * (g - 1))
                        nc.vector.tensor_tensor(k.masked_scores[:, g % 2, :, :], sb, k.window_mask[:, :, :], ALU.add).then_inc(s.masked_ready, 1)
                        dve.wait_ge(s.masked_ready, n)
                        sb = k.masked_scores[:, g % 2, :, :]
                    if not nulled(g):
                        nc.vector.reduce_max(k.negmax[:, h, :], sb, AXX, negate=True).then_inc(s.negmax_ready, 1)
                        return
                    p, j = h // 2, h % 2
                    if j == 0:
                        dve.wait_ge(s.null_scores, null_pairs(g))
                        nc.vector.tensor_copy(k.null_scores[:, p % 2, :], job_bank(("pair", g // HEADS, p))[:, 0:2 * SUB]).then_inc(s.null_taken, 1)
                    step.add(nc.vector.reduce_max(k.key_negmax[:, :], sb, AXX, negate=True))
                    step.wait()
                    dve.wait_ge(s.null_taken, null_pairs(g))
                    null = k.null_scores[:, p % 2, :].rearrange("p (t j) -> p t j", j=2)[:, :, j]
                    nc.vector.scalar_tensor_tensor(k.negmax[:, h, :], null, -1.0, k.key_negmax[:, :], ALU.mult, ALU.min).then_inc(s.negmax_ready, 1)
                    dve.wait_ge(s.negmax_ready, g + 1)
                    nc.vector.tensor_tensor(k.null_arg[:, h - PAIRS, :], null, k.negmax[:, h, :], ALU.add).then_inc(s.null_args, 1)

                def reciprocal(g):
                    h = g % HEADS
                    dve.wait_ge(s.probs_ready, 2 * (g + 1))
                    if nulled(g):
                        dve.wait_ge(s.null_exps, null_heads(g))
                        step.add(nc.vector.tensor_tensor(k.prob_sum[:, h, :], k.prob_sum[:, h, :], k.null_exp[:, h - PAIRS, :], ALU.add))
                        step.wait()
                    nc.vector.reciprocal(k.recip[:, h, :], k.prob_sum[:, h, :]).then_inc(s.recip_ready, 1)
                    dve.wait_ge(s.recip_ready, g + 1)
                    if nulled(g):
                        nc.vector.tensor_tensor(k.null_probs[:, :, h - PAIRS], k.null_exp[:, h - PAIRS, :], k.recip[:, h, :], ALU.mult)\
                            .then_inc(s.null_weights, 1)

                def normalise(g):
                    for t in range(SUB):
                        piece = k.probs[:, g % PBUF, t, :]
                        nc.vector.tensor_scalar(piece, piece, k.recip[:, g % HEADS, t:t + 1], None, ALU.mult).then_inc(s.probs_normed, 1)

                def save_turned(g):
                    dve.wait_ge(s.turned, g + 1)
                    if g >= 3:
                        dve.wait_ge(s.values_weighed, g - 2)
                    nc.vector.tensor_copy(k.probsT[:, g % 3, :, :].rearrange("p a n -> p (a n)"), k.psum[TB[g % 2]][:, :]).then_inc(s.dve_turned, 1)

                def descend(i):
                    if i >= 1:
                        dve.wait_ge(s.route_act, i)
                        step.add(descend_dve_a(nc, k))
                        step.wait()
                        step.add(descend_dve_m(nc, k))
                        step.wait()
                    if i < SEQS * DESCENTS_PER_SEQ:
                        descend_dve_first(nc, k).then_inc(s.route_dve, 1)

                if ffn:
                    nc.vector.tensor_copy(k.route_b[:, :, :], k.route_w[:, :, bass.ds(b * SEQS * SUB, SEQS * SUB)]).then_inc(s.weights_picked, 1)
                    dve.wait_ge(s.weights_picked, 1)
                for job in before:
                    do(job)
                for g in steps:
                    for job in at[g - 1] if g else []:
                        do(job)
                    if g < N:
                        negmax(g)
                    if 1 <= g <= N:
                        reciprocal(g - 1)
                        normalise(g - 1)
                    if l0 and g % 2 == 0 and g // 2 <= SEQS * DESCENTS_PER_SEQ:
                        descend(g // 2)
                    if 0 <= g - PT_LAG < N and not by_act(g - PT_LAG):
                        save_turned(g - PT_LAG)
                for job in at[steps[-1]]:
                    do(job)


def route_stage(nc, k, w):
    with signals(nc, "dve_step", "scored", "exped", "weighted", "sent", "spread", "turned", "cols_saved") as s:
        with nc.Block() as block:
            @block.vector
            def _(dve):
                step = Steps(dve, s.dve_step)
                step.add(nc.vector.tensor_scalar(k.logits[:, :], k.logits[:, :], k.neg_a[:, :], 0.0, ALU.subtract, ALU.min))
                step.wait()
                nc.vector.tensor_scalar(k.logits[:, :], k.logits[:, :], -103.0, None, ALU.max).then_inc(s.scored, 1)
                dve.wait_ge(s.exped, 1)
                step.add(nc.vector.tensor_scalar(k.route_arg[:, :], k.route_exp[:, :], -1.0, 1.0, ALU.mult, ALU.add))
                step.wait()
                nc.vector.tensor_tensor(k.route_arg[:, :], k.route_arg[:, :], k.route_exp[:, :], ALU.add).then_inc(s.weighted, 1)
                dve.wait_ge(s.turned, 1)
                nc.vector.tensor_copy(k.route_cols[:, :, :, :].rearrange("p a t r -> p (a t r)"), k.psum[0][:, 0:4 * 16]).then_inc(s.cols_saved, 1)
                dve.wait_ge(s.cols_saved, 1)
                dve.wait_ge(s.spread, 16)
                n = 0
                for b in range(BATCH):
                    for t in range(SUB):
                        mine = k.route_cols[:, 0, t, b:b + 1]
                        i = SUB * b + t
                        if n >= 2:
                            dve.wait_ge(s.dve_step, step.n - 2)
                        step.add(nc.vector.tensor_scalar(w.compare[:, n % 2, :], w.scores_all[:, b, :], mine, 0.0, ALU.is_gt, ALU.add,
                                                         accum_out=k.rank[:, 0, i:i + 1]))
                        step.add(nc.vector.scalar_tensor_tensor(w.compare[:, 2 + n % 2, :], w.scores_all[:, b, :], mine, w.earlier[:, t, :],
                                                                ALU.is_equal, ALU.mult, accum_out=k.rank[:, 1, i:i + 1]))
                        n += 1
                step.wait()
                step.add(nc.vector.tensor_tensor(k.rank[:, 0, :], k.rank[:, 0, :], k.rank[:, 1, :], ALU.add))
                step.wait()
                selected = k.route_w[:, 0, :]
                step.add(nc.vector.tensor_scalar(selected, k.rank[:, 0, :], float(NQ), None, ALU.is_lt))
                step.add(nc.vector.tensor_scalar(k.route_w[:, 1, :], k.rank[:, 0, :], float(NQ), None, ALU.is_ge))
                step.wait()
                by_token = k.route_cols[:, 1, :, :].rearrange("p t r -> p r t")
                step.add(nc.vector.tensor_tensor(selected.rearrange("p (b t) -> p b t", t=SUB), selected.rearrange("p (b t) -> p b t", t=SUB),
                                                 by_token[:, 0:BATCH, :], ALU.mult))
                step.add(nc.vector.tensor_copy(k.route_w[:, 2, :].rearrange("p (b t) -> p b t", t=SUB), by_token[:, BATCH:2 * BATCH, :]))

            @block.scalar
            def _(act):
                act.wait_ge(s.scored, 1)
                nc.scalar.activation(k.route_exp[:, :], k.logits[:, :], ACT.Exp).then_inc(s.exped, 1)

            @block.sync
            def _(sp):
                sp.wait_ge(s.scored, 1)
                sp.dma_start(k.scratch, k.logits[0:BATCH, :]).then_inc(s.sent, 16)
                sp.wait_ge(s.sent, 16)
                sp.dma_start(w.scores_all[:, :, :].rearrange("p b n -> p (b n)"),
                             k.scratch.rearrange("b n -> (b n)").partition_broadcast(P)).then_inc(s.spread, 16)

            @block.tensor
            def _(pe):
                pe.wait_ge(s.scored, 1)
                for t in range(SUB):
                    nc.tensor.transpose(k.psum[0][:, 16 * t:16 * (t + 1)], k.logits[:, P * t:P * (t + 1)], k.ident[0:16, 0:16])
                pe.wait_ge(s.weighted, 1)
                for t in range(SUB):
                    last = nc.tensor.transpose(k.psum[0][:, 16 * (SUB + t):16 * (SUB + t + 1)], k.route_arg[:, P * t:P * (t + 1)],
                                               k.ident[0:16, 0:16])
                last.then_inc(s.turned, 1)



def taylor_attention_stage(nc, k, b, w):
    LAG = 2
    ABUF = 3
    SB, EB, OB = (0, 1), (2, 3), (4, 5)
    WIDE = SEQ + P
    with signals(nc, "x_copied", "proj_made", "query_saved", "keys_saved", "values_made", "act_values", "dve_values", "enc_made",
                 "head_query", "scores_ready", "squared", "kernel_ready", "weighed", "dve_step", "out_saved", "y_made", "y_saved",
                 "y_turned", "x_added") as s:
        with nc.Block() as block:
            @block.gpsimd
            def _(pool):
                nc.gpsimd.tensor_copy(k.xb[:, 0, 0, :], k.xnT[:, bass.ds(b * SEQ, SEQ)]).then_inc(s.x_copied, 1)
                pool.wait_ge(s.query_saved, 1)
                for h in range(HEADS):
                    nc.gpsimd.tensor_scalar(k.keys[:, h, :], k.queryT[:, h // 8, :], k.head16[:, h % 8:h % 8 + 1], None, ALU.mult)\
                        .then_inc(s.head_query, 1)

            @block.tensor
            def _(pe):
                xb = k.xb[:, 0, 0, :]
                pe.wait_ge(s.x_copied, 1)
                for i in range(2):
                    nc.tensor.matmul(k.psum[6][:, SEQ * i:SEQ * (i + 1)], w.w_q[:, P * i:P * (i + 1)], xb, start=True, stop=True)
                    last = nc.tensor.matmul(k.psum[7][:, SEQ * i:SEQ * (i + 1)], w.w_k[:, P * i:P * (i + 1)], xb, start=True, stop=True)
                last.then_inc(s.proj_made, 1)
                for i in range(2):
                    last = nc.tensor.matmul(k.psum[2][:, L1_ENC * i:L1_ENC * (i + 1)], w.w_k_enc[:, P * i:P * (i + 1)], xb[:, 0:L1_ENC],
                                            start=True, stop=True)
                last.then_inc(s.proj_made, 1)
                for i in range(2 * SUB):
                    t, half = i // 2, i % 2
                    nc.tensor.matmul(k.psum[(0, 1, 4, 5)[i]][:, :], xb[:, P * t:P * (t + 1)], w.w_v[:, CHUNK * half:CHUNK * (half + 1)],
                                     start=True, stop=True).then_inc(s.values_made, 1)
                for half in range(2):
                    if half:
                        pe.wait_ge(s.query_saved, 1)
                    nc.tensor.matmul(k.psum[(3, 6)[half]][0:L1_ENC, :], xb[:, 0:L1_ENC], w.w_v_enc[:, CHUNK * half:CHUNK * (half + 1)],
                                     start=True, stop=True).then_inc(s.enc_made, 1)
                pe.wait_ge(s.keys_saved, 2)
                pe.wait_ge(s.act_values, 4)
                pe.wait_ge(s.dve_values, 2)

                def scores(h):
                    pe.wait_ge(s.head_query, h + 1)
                    if h >= 2:
                        pe.wait_ge(s.squared, 2 * (h - 1))
                    c, q = h // 8, k.keys[:, h, :]
                    sb = k.psum[SB[h % 2]]
                    nc.tensor.matmul(sb[:, 0:SEQ], w.kT[:, c, 0:P], q, start=True, stop=True)
                    nc.tensor.matmul(sb[:, SEQ:WIDE], w.kT[:, c, P:2 * P], q[:, P:2 * P], start=True, stop=True)
                    nc.tensor.matmul(k.psum[EB[h % 2]][0:L1_ENC, 0:SEQ], w.k_encT[:, c, :], q, start=True, stop=True).then_inc(s.scores_ready, 1)

                def weigh(h):
                    pe.wait_ge(s.kernel_ready, 2 * (h + 1))
                    o = h // 2
                    if o >= 2 and h % 2 == 0:
                        pe.wait_ge(s.out_saved, o - 1)
                    rows = slice(HD * (h % 2), HD * (h % 2 + 1))
                    ob = k.psum[OB[o % 2]]
                    A, E = w.kernel[:, h % ABUF, :], w.kernel_enc[:, h % ABUF, :]
                    for col, vals in ((0, [k.values[:, 0, 0, HD * h:HD * (h + 1)], k.values[:, 0, 1, HD * h:HD * (h + 1)], w.v_enc[:, HD * h:HD * (h + 1)]]),
                                      (SEQ, [w.ones[:, :]] * 3)):
                        nc.tensor.matmul(ob[rows, col:col + SEQ], vals[0], A[:, 0:SEQ], start=True, stop=False)
                        nc.tensor.matmul(ob[rows, col + P:col + SEQ], vals[1], A[:, SEQ:WIDE], start=False, stop=False)
                        last = nc.tensor.matmul(ob[rows, col:col + SEQ], vals[2], E, start=False, stop=True)
                    last.then_inc(s.weighed, 1)

                for h in range(HEADS + LAG):
                    if h < HEADS:
                        scores(h)
                    if h >= LAG:
                        weigh(h - LAG)
                pe.wait_ge(s.out_saved, PAIRS)
                for o in range(PAIRS):
                    last = nc.tensor.matmul(k.psum[6][:, 0:SEQ], w.w_out[:, o, :], k.outT[:, 0, o, :], start=(o == 0), stop=(o == PAIRS - 1))
                last.then_inc(s.y_made, 1)
                pe.wait_ge(s.y_saved, 1)
                for t in range(SUB):
                    last = nc.tensor.transpose(k.psum[7][:, P * t:P * (t + 1)], k.yT[:, 0, P * t:P * (t + 1)], k.ident[:, :])
                last.then_inc(s.y_turned, 1)

            @block.scalar
            def _(act):
                act.wait_ge(s.proj_made, 1)
                nc.scalar.activation(k.queryT[:, 0:2, :].rearrange("p c n -> p (c n)"), k.psum[6][:, :], ACT.Copy).then_inc(s.query_saved, 1)
                for i in range(2):
                    act.wait_ge(s.values_made, i + 1)
                    nc.scalar.activation(k.values[:, 0, 0, CHUNK * i:CHUNK * (i + 1)], k.psum[i][:, :], ACT.Copy).then_inc(s.act_values, 1)
                for i in range(2):
                    act.wait_ge(s.enc_made, i + 1)
                    nc.scalar.activation(w.v_enc[0:L1_ENC, CHUNK * i:CHUNK * (i + 1)], k.psum[(3, 6)[i]][0:L1_ENC, :], ACT.Copy)\
                        .then_inc(s.act_values, 1)
                for h in range(HEADS):
                    act.wait_ge(s.scores_ready, h + 1)
                    if h >= ABUF:
                        act.wait_ge(s.weighed, h - ABUF + 1)
                    nc.scalar.activation(w.kernel[:, h % ABUF, :], k.psum[SB[h % 2]][:, 0:WIDE], ACT.Square, scale=0.25, bias=1.0)\
                        .then_inc(s.squared, 1)
                    nc.scalar.activation(w.kernel_enc[0:L1_ENC, h % ABUF, :], k.psum[EB[h % 2]][0:L1_ENC, 0:SEQ], ACT.Square, scale=0.25,
                                         bias=1.0).then_inc(s.squared, 1)
                act.wait_ge(s.y_made, 1)
                nc.scalar.activation(k.yT[:, 0, :], k.psum[6][:, 0:SEQ], ACT.Copy).then_inc(s.y_saved, 1)

            @block.vector
            def _(dve):
                step = Steps(dve, s.dve_step)
                dve.wait_ge(s.proj_made, 2)
                nc.vector.tensor_copy(w.kT[:, :, :].rearrange("p c n -> p (c n)"), k.psum[7][:, :]).then_inc(s.keys_saved, 1)
                nc.vector.tensor_copy(w.k_encT[:, :, :].rearrange("p c n -> p (c n)"), k.psum[2][:, 0:2 * L1_ENC]).then_inc(s.keys_saved, 1)
                for i in range(2):
                    dve.wait_ge(s.values_made, 3 + i)
                    nc.vector.tensor_copy(k.values[:, 0, 1, CHUNK * i:CHUNK * (i + 1)], k.psum[4 + i][:, :]).then_inc(s.dve_values, 1)

                def divide(o):
                    dve.wait_ge(s.weighed, 2 * (o + 1))
                    ob = k.psum[OB[o % 2]]
                    step.add(nc.vector.tensor_scalar(w.norm[:, o % 2, :], ob[:, SEQ:2 * SEQ], 2 * L1_EPS, None, ALU.add))
                    step.wait()
                    step.add(nc.vector.reciprocal(w.norm[:, o % 2, :], w.norm[:, o % 2, :]))
                    step.wait()
                    nc.vector.tensor_tensor(k.outT[:, 0, o, :], ob[:, 0:SEQ], w.norm[:, o % 2, :], ALU.mult).then_inc(s.out_saved, 1)

                for h in range(HEADS + LAG + 1):
                    if h < HEADS:
                        dve.wait_ge(s.squared, 2 * (h + 1))
                        A, E = w.kernel[:, h % ABUF, :], w.kernel_enc[0:L1_ENC, h % ABUF, :]
                        nc.vector.scalar_tensor_tensor(A, A, 1.0, w.causal[:, :], ALU.add, ALU.mult).then_inc(s.kernel_ready, 1)
                        nc.vector.tensor_scalar(E, E, 1.0, None, ALU.add).then_inc(s.kernel_ready, 1)
                    done = h - LAG - 1
                    if done >= 0 and done % 2:
                        divide(done // 2)
                dve.wait_ge(s.y_turned, 1)
                nc.vector.tensor_tensor(k.x[:, bass.ds(b * SUB, SUB), :], k.x[:, bass.ds(b * SUB, SUB), :],
                                        k.psum[7][:, 0:SEQ].rearrange("p (t n) -> p t n", t=SUB), ALU.add).then_inc(s.x_added, 1)



def gate_stage(nc, k, w_router, renormalise, zeros=()):
    E = 8
    with signals(nc, "logits_made", "centred", "exped", "dve_step", "gated", "turned", "saved", "pool_step") as s:
        with nc.Block() as block:
            @block.gpsimd
            def _(pool):
                nc.gpsimd.memset(k.gateT[:, :], 0.0).then_inc(s.pool_step, 1)
                for z in zeros:
                    nc.gpsimd.memset(z, 0.0)

            @block.tensor
            def _(pe):
                for t in range(TILES):
                    last = nc.tensor.matmul(k.psum[0][:, E * t:E * (t + 1)], k.xnT[:, P * t:P * (t + 1)], w_router, start=True, stop=True)
                last.then_inc(s.logits_made, 1)
                pe.wait_ge(s.gated, 1)
                for g in range(CHUNKS):
                    for j in range(CT):
                        last = nc.tensor.transpose(k.psum[1 + g][0:E, P * j:P * (j + 1)], k.gate[:, CT * g + j, :], k.ident[:, :])
                    last.then_inc(s.turned, 1)

            @block.scalar
            def _(act):
                act.wait_ge(s.centred, 1)
                nc.scalar.activation(k.gate[:, :, :], k.gate[:, :, :], ACT.Exp).then_inc(s.exped, 1)
                act.wait_ge(s.pool_step, 1)
                for g in range(CHUNKS):
                    act.wait_ge(s.turned, g + 1)
                    nc.scalar.activation(k.gateT[0:E, CHUNK * g:CHUNK * (g + 1)], k.psum[1 + g][0:E, :], ACT.Copy).then_inc(s.saved, 1)

            @block.vector
            def _(dve):
                step = Steps(dve, s.dve_step)
                logits = k.psum[0][:, 0:E * TILES].rearrange("p (t e) -> p t e", e=E)
                per_tile = k.gate_sum[:, :].unsqueeze(2).to_broadcast([P, TILES, E])
                step.add(nc.vector.memset(k.gate_cmp[:, :, :, :], 0.0))
                dve.wait_ge(s.logits_made, 1)
                step.add(nc.vector.reduce_max(k.gate_sum[:, :], logits, AXX))
                step.wait()
                nc.vector.tensor_tensor(k.gate[:, :, :], logits, per_tile, ALU.subtract).then_inc(s.centred, 1)
                dve.wait_ge(s.exped, 1)
                step.add(nc.vector.reduce_sum(k.gate_sum[:, :], k.gate[:, :, :], AXX))
                step.wait()
                step.add(nc.vector.reciprocal(k.gate_sum[:, :], k.gate_sum[:, :]))
                step.wait()
                step.add(nc.vector.tensor_tensor(k.gate[:, :, :], k.gate[:, :, :], per_tile, ALU.mult))
                step.wait()
                for j in range(E):
                    rival = k.gate[:, :, j:j + 1]
                    if j > 0:
                        step.add(nc.vector.tensor_tensor(k.gate_cmp[:, j, :, 0:j], rival.to_broadcast([P, TILES, j]), k.gate[:, :, 0:j], ALU.is_gt))
                    if j < E - 1:
                        step.add(nc.vector.tensor_tensor(k.gate_cmp[:, j, :, j + 1:E], rival.to_broadcast([P, TILES, E - 1 - j]),
                                                         k.gate[:, :, j + 1:E], ALU.is_ge))
                step.wait()
                step.add(nc.vector.reduce_sum(k.gate_rank[:, :, :].rearrange("p t e -> p (t e)"),
                                              k.gate_cmp[:, :, :, :].rearrange("p j t e -> p (t e) j"), AXX))
                step.wait()
                last = nc.vector.scalar_tensor_tensor(k.gate[:, :, :], k.gate_rank[:, :, :], 2.0, k.gate[:, :, :], ALU.is_lt, ALU.mult)
                if renormalise:
                    step.add(last)
                    step.wait()
                    step.add(nc.vector.reduce_sum(k.gate_sum[:, :], k.gate[:, :, :], AXX))
                    step.wait()
                    step.add(nc.vector.reciprocal(k.gate_sum[:, :], k.gate_sum[:, :]))
                    step.wait()
                    last = nc.vector.tensor_tensor(k.gate[:, :, :], k.gate[:, :, :], per_tile, ALU.mult)
                last.then_inc(s.gated, 1)


def finish_chunk_pe(nc, k, pe, s):
    pe.wait_ge(s.y_saved, 1)
    for j in range(CT):
        last = nc.tensor.transpose(k.psum[7][:, P * j:P * (j + 1)], k.y_chunk[:, P * j:P * (j + 1)], k.ident[:, :])
    last.then_inc(s.y_turned, 1)


def finish_chunk_dve(nc, k, dve, s, c):
    dve.wait_ge(s.y_turned, 1)
    rows = k.x[:, bass.ds(c * CT, CT), :]
    nc.vector.tensor_tensor(rows, rows, k.psum[7][:, :].rearrange("p (t n) -> p t n", t=CT), ALU.add).then_inc(s.x_added, 1)


def swiglu_experts_stage(nc, k, c, w):
    HB = 3
    with signals(nc, "up_ready", "silu_ready", "product_ready", "hidden_ready", "down_done", "y_made", "y_saved", "y_turned", "x_added") as s:
        with nc.Block() as block:
            @block.tensor
            def _(pe):
                xs, gs = k.xnT[:, bass.ds(c * CHUNK, CHUNK)], k.gateT[:, bass.ds(c * CHUNK, CHUNK)]
                for i in range(L1_HC + 1):
                    if i < L1_HC:
                        if i >= 2:
                            pe.wait_ge(s.hidden_ready, i - 1)
                        cols = slice(P * i, P * (i + 1))
                        nc.tensor.matmul(k.psum[i % 2][:, :], w.w1[:, cols], xs, start=True, stop=True)
                        nc.tensor.matmul(k.psum[2 + i % 2][:, :], w.w3[:, cols], xs, start=True, stop=True)
                        nc.tensor.matmul(k.psum[4 + i % 2][:, :], w.expert_of[:, cols], gs, start=True, stop=True).then_inc(s.up_ready, 1)
                    if i >= 1:
                        pe.wait_ge(s.hidden_ready, i)
                        last = nc.tensor.matmul(k.psum[6][:, :], w.w2[:, i - 1, :], w.hidden[:, (i - 1) % HB, :], start=(i == 1),
                                                stop=(i == L1_HC))
                        last.then_inc(s.down_done, 1)
                finish_chunk_pe(nc, k, pe, s)

            @block.scalar
            def _(act):
                for i in range(L1_HC):
                    act.wait_ge(s.up_ready, i + 1)
                    if i >= 2:
                        act.wait_ge(s.product_ready, i - 1)
                    nc.scalar.activation(w.silu[:, i % 2, :], k.psum[i % 2][:, :], ACT.Silu).then_inc(s.silu_ready, 1)
                act.wait_ge(s.down_done, L1_HC)
                nc.scalar.activation(k.y_chunk[:, :], k.psum[6][:, :], ACT.Copy).then_inc(s.y_saved, 1)

            @block.vector
            def _(dve):
                for i in range(L1_HC):
                    dve.wait_ge(s.silu_ready, i + 1)
                    if i >= HB:
                        dve.wait_ge(s.down_done, i - HB + 1)
                    hid = w.hidden[:, i % HB, :]
                    nc.vector.tensor_tensor(hid, w.silu[:, i % 2, :], k.psum[2 + i % 2][:, :], ALU.mult).then_inc(s.product_ready, 1)
                    dve.wait_ge(s.product_ready, i + 1)
                    nc.vector.tensor_tensor(hid, hid, k.psum[4 + i % 2][:, :], ALU.mult).then_inc(s.hidden_ready, 1)
                finish_chunk_dve(nc, k, dve, s, c)


def relu_experts_stage(nc, k, c, w):
    HB, UB, STEPS = 3, 4, L2_E * L2_FC
    with signals(nc, "gate_made", "gate_saved", "up_ready", "hidden_ready", "down_done", "y_saved", "y_turned", "x_added") as s:
        with nc.Block() as block:
            @block.tensor
            def _(pe):
                xs, gs = k.xnT[:, bass.ds(c * CHUNK, CHUNK)], k.gateT[:, bass.ds(c * CHUNK, CHUNK)]

                def spread(e):
                    if e >= 2:
                        pe.wait_ge(s.gate_saved, e - 1)
                    nc.tensor.matmul(k.psum[4 + e % 2][:, :], k.ident[:, e:e + 1].to_broadcast([P, P]), gs, start=True, stop=True)\
                        .then_inc(s.gate_made, 1)

                spread(0)
                for i in range(STEPS + 2):
                    if i < STEPS:
                        if i % L2_FC == 0 and i // L2_FC + 1 < L2_E:
                            spread(i // L2_FC + 1)
                        if i >= UB:
                            pe.wait_ge(s.hidden_ready, i - UB + 1)
                        nc.tensor.matmul(k.psum[i % UB][:, :], w.w1[:, P * i:P * (i + 1)], xs, start=True, stop=True).then_inc(s.up_ready, 1)
                    if i >= 2:
                        j = i - 2
                        pe.wait_ge(s.hidden_ready, j + 1)
                        nc.tensor.matmul(k.psum[6][:, :], w.w2[:, j, :], w.hidden[:, j % HB, :], start=(j == 0), stop=(j == STEPS - 1))\
                            .then_inc(s.down_done, 1)
                finish_chunk_pe(nc, k, pe, s)

            @block.scalar
            def _(act):
                for e in range(L2_E):
                    act.wait_ge(s.gate_made, e + 1)
                    if e >= 2:
                        act.wait_ge(s.hidden_ready, L2_FC * (e - 1))
                    nc.scalar.activation(w.gate_all[:, e % 2, :], k.psum[4 + e % 2][:, :], ACT.Copy).then_inc(s.gate_saved, 1)
                act.wait_ge(s.down_done, STEPS)
                nc.scalar.activation(k.y_chunk[:, :], k.psum[6][:, :], ACT.Copy).then_inc(s.y_saved, 1)

            @block.vector
            def _(dve):
                for i in range(STEPS):
                    dve.wait_ge(s.up_ready, i + 1)
                    dve.wait_ge(s.gate_saved, i // L2_FC + 1)
                    if i >= HB:
                        dve.wait_ge(s.down_done, i - HB + 1)
                    nc.vector.scalar_tensor_tensor(w.hidden[:, i % HB, :], k.psum[i % UB][:, :], 0.0, w.gate_all[:, i // L2_FC % 2, :],
                                                   ALU.max, ALU.mult).then_inc(s.hidden_ready, 1)
                finish_chunk_dve(nc, k, dve, s, c)



HALF = TOKENS // 2
HALF_SEQS = HALF // SEQ


def ssm_prepare_stage(nc, k, w):
    with signals(nc, "cleared", "in_made", "in_saved", "x_saved", "conv_made", "ssm_ready", "proj_made", "proj_saved", "dt_made", "dt_biased",
                 "dt_folded", "dt_exped", "dt_logged", "decay_exped", "dve_step", "conv_step", "lora_made", "linear_made", "linear_turned",
                 "linear_saved") as s:
        with nc.Block() as block:
            @block.gpsimd
            def _(pool):
                nc.gpsimd.memset(w.padded[:, :, :, 0:L3_CONV - 1], 0.0).then_inc(s.cleared, 1)
                nc.gpsimd.memset(w.projT[:, :], 0.0).then_inc(s.cleared, 1)
                nc.gpsimd.memset(w.decay[:, :, :, 0:1], 0.0).then_inc(s.cleared, 1)

            @block.tensor
            def _(pe):
                n = 0
                for m in range(2 * L3_DC):
                    for g in range(CHUNKS):
                        if n >= 4:
                            pe.wait_ge(s.in_saved, n - 3)
                        nc.tensor.matmul(k.psum[n % 4][:, :], w.w_in[:, P * m:P * (m + 1)], k.xnT[:, CHUNK * g:CHUNK * (g + 1)],
                                         start=True, stop=True).then_inc(s.in_made, 1)
                        n += 1
                for l in range(L3_LIN):
                    last = nc.tensor.matmul(k.psum[4 + l // 4][:, P * (l % 4):P * (l % 4 + 1)], w.lora_b[:, l, :], w.lora_a[:, l, :],
                                            start=True, stop=True)
                last.then_inc(s.lora_made, 1)
                pe.wait_ge(s.linear_made, 2)
                for l in range(L3_LIN):
                    last = nc.tensor.transpose(k.psum[6 + l // 4][:, P * (l % 4):P * (l % 4 + 1)], w.linear[:, l, :], k.ident[:, :])
                last.then_inc(s.linear_turned, 1)
                pe.wait_ge(s.ssm_ready, L3_DC)
                pe.wait_ge(s.linear_saved, 2)
                for g in range(CHUNKS):
                    for m in range(L3_DC):
                        last = nc.tensor.matmul(k.psum[g][0:2 * L3_N + 1, :], w.w_x[:, m, :], w.xs[:, m, CHUNK * g:CHUNK * (g + 1)],
                                                start=(m == 0), stop=(m == L3_DC - 1))
                    last.then_inc(s.proj_made, 1)
                pe.wait_ge(s.proj_saved, CHUNKS)
                for m in range(L3_DC):
                    for g in range(CHUNKS):
                        last = nc.tensor.matmul(k.psum[4 * m + g][:, :], w.w_dt[:, m, :], w.projT[:, CHUNK * g:CHUNK * (g + 1)], start=True, stop=True)
                    last.then_inc(s.dt_made, 1)

            @block.scalar
            def _(act):
                n = 0
                for m in range(2 * L3_DC):
                    for g in range(CHUNKS):
                        act.wait_ge(s.in_made, n + 1)
                        seqs = slice(2 * g, 2 * g + 2)
                        if m < L3_DC:
                            last = nc.scalar.activation(w.padded[:, m, seqs, L3_CONV - 1:], k.psum[n % 4][:, :].rearrange("p (b n) -> p b n", b=2), ACT.Copy)
                        else:
                            last = nc.scalar.activation(w.z[:, m - L3_DC, CHUNK * g:CHUNK * (g + 1)], k.psum[n % 4][:, :], ACT.Silu)
                        last.then_inc(s.in_saved, 1)
                        n += 1
                for m in range(L3_DC):
                    act.wait_ge(s.conv_made, m + 1)
                    nc.scalar.activation(w.xs[:, m, :], w.xs[:, m, :], ACT.Silu, bias=w.conv_b[:, m:m + 1]).then_inc(s.ssm_ready, 1)
                act.wait_ge(s.linear_turned, 1)
                for i in range(2):
                    width = (4, 2)[i]
                    nc.scalar.activation(w.linearT[:, 4 * i:4 * i + width, :].rearrange("p l n -> p (l n)"), k.psum[6 + i][:, 0:P * width], ACT.Copy)\
                        .then_inc(s.linear_saved, 1)
                act.wait_ge(s.cleared, 2)
                for g in range(CHUNKS):
                    act.wait_ge(s.proj_made, g + 1)
                    nc.scalar.activation(w.projT[0:2 * L3_N + 1, CHUNK * g:CHUNK * (g + 1)], k.psum[g][0:2 * L3_N + 1, :], ACT.Copy)\
                        .then_inc(s.proj_saved, 1)
                nc.scalar.preload_act_table_set("natural_log_exp_and_others")
                nc.scalar.activation(w.a_neg[:, :, :], w.a_neg[:, :, :], ACT.Exp).then_inc(s.decay_exped, 1)
                for m in range(L3_DC):
                    act.wait_ge(s.dt_folded, m + 1)
                    nc.scalar.activation(w.xdt[:, m, :], w.xdt[:, m, :], ACT.Exp).then_inc(s.dt_exped, 1)
                for m in range(L3_DC):
                    act.wait_ge(s.dt_exped, m + 1)
                    nc.scalar.activation(w.xdt[:, m, :], w.xdt[:, m, :], ACT.Ln, bias=1.0).then_inc(s.dt_logged, 1)

            @block.vector
            def _(dve):
                step, conv = Steps(dve, s.dve_step), Steps(dve, s.conv_step)
                step.add(nc.vector.tensor_scalar(w.linear[:, :, :], w.codes[:, :, :], 1.0 / 7.5, -1.0, ALU.mult, ALU.add))
                step.wait()
                grouped = w.linear[:, :, :].rearrange("p l (g n) -> p (l g) n", n=L3_GROUP)
                step.add(nc.vector.tensor_tensor(grouped, grouped, w.scales[:, :].unsqueeze(2).to_broadcast([P, L3_LIN * P // L3_GROUP, L3_GROUP]),
                                                 ALU.mult))
                step.wait()
                dve.wait_ge(s.lora_made, 1)
                for i in range(2):
                    width = (4, 2)[i]
                    part = w.linear[:, 4 * i:4 * i + width, :].rearrange("p l n -> p (l n)")
                    nc.vector.tensor_tensor(part, part, k.psum[4 + i][:, 0:P * width], ALU.add).then_inc(s.linear_made, 1)
                dve.wait_ge(s.cleared, 3)
                for m in range(L3_DC):
                    dve.wait_ge(s.in_saved, CHUNKS * (m + 1))
                    out = w.xs[:, m, :].rearrange("p (b n) -> p b n", b=BATCH)
                    conv.add(nc.vector.tensor_scalar(out, w.padded[:, m, :, 0:SEQ], w.conv_w[:, m, 0:1], None, ALU.mult))
                    for j in range(1, L3_CONV):
                        conv.wait()
                        last = nc.vector.scalar_tensor_tensor(out, w.padded[:, m, :, j:j + SEQ], w.conv_w[:, m, j:j + 1], out, ALU.mult, ALU.add)
                        if j < L3_CONV - 1:
                            conv.add(last)
                        else:
                            last.then_inc(s.conv_made, 1)
                for m in range(L3_DC):
                    dve.wait_ge(s.dt_made, m + 1)
                    nc.vector.tensor_scalar(w.dt[:, m, :], k.psum_all[:, 4 * CHUNK * m:4 * CHUNK * (m + 1)], w.b_dt[:, m:m + 1], None, ALU.add)\
                        .then_inc(s.dt_biased, 1)
                    dve.wait_ge(s.dt_biased, m + 1)
                    nc.vector.scalar_tensor_tensor(w.xdt[:, m, :], w.dt[:, m, :], -1.0, w.dt[:, m, :], ALU.mult, ALU.min).then_inc(s.dt_folded, 1)
                dve.wait_ge(s.decay_exped, 1)
                step.add(nc.vector.tensor_scalar(w.a_neg[:, :, :], w.a_neg[:, :, :], -1.0, None, ALU.mult))
                for m in range(L3_DC):
                    dve.wait_ge(s.dt_logged, m + 1)
                    step.add(nc.vector.scalar_tensor_tensor(w.dt[:, m, :], w.dt[:, m, :], 0.0, w.xdt[:, m, :], ALU.max, ALU.add))
                    step.wait()
                    step.add(nc.vector.tensor_tensor(w.xdt[:, m, :], w.dt[:, m, :], w.xs[:, m, :], ALU.mult))


def ssm_scan_stage(nc, k, hf, w):
    UNITS = L3_N * L3_DC
    BUF = 3
    with signals(nc, "b_spread", "c_spread", "c_saved", "decay_ready", "input_ready", "scanned", "weighted", "summed", "dve_step", "y_ready",
                 "out_made", "y_saved", "y_turned", "x_added") as s:
        with nc.Block() as block:
            @block.tensor
            def _(pe):
                def spread(n):
                    if n >= 1:
                        pe.wait_ge(s.input_ready, L3_DC * n)
                    for j in range(2):
                        last = nc.tensor.matmul(k.psum[j][:, :], k.ident[:, n:n + 1].to_broadcast([P, P]),
                                                w.projT[:, bass.ds(hf * HALF + CHUNK * j, CHUNK)], start=True, stop=True)
                    last.then_inc(s.b_spread, 1)
                    if n >= 1:
                        pe.wait_ge(s.c_saved, n)
                    for j in range(2):
                        last = nc.tensor.matmul(k.psum[2 + j][:, :], k.ident[:, L3_N + n:L3_N + n + 1].to_broadcast([P, P]),
                                                w.projT[:, bass.ds(hf * HALF + CHUNK * j, CHUNK)], start=True, stop=True)
                    last.then_inc(s.c_spread, 1)

                def accumulate(u):
                    pe.wait_ge(s.weighted, u + 1)
                    n, m = u // L3_DC, u % L3_DC
                    for j in range(2):
                        last = nc.tensor.matmul(k.psum[4 + 2 * m + j][:, :], k.ident[:, :], w.weighted[:, u % BUF, CHUNK * j:CHUNK * (j + 1)],
                                                start=(n == 0), stop=(n == L3_N - 1))
                    last.then_inc(s.summed, 1)

                spread(0)
                for n in range(L3_N):
                    if n + 1 < L3_N:
                        spread(n + 1)
                    if n >= 1:
                        for m in range(L3_DC):
                            accumulate(L3_DC * (n - 1) + m)
                for m in range(L3_DC):
                    accumulate(L3_DC * (L3_N - 1) + m)
                pe.wait_ge(s.y_ready, L3_DC)
                for j in range(2):
                    for m in range(L3_DC):
                        last = nc.tensor.matmul(k.psum[j][:, :], w.w_out[:, m, :], w.gated[:, m, CHUNK * j:CHUNK * (j + 1)],
                                                start=(m == 0), stop=(m == L3_DC - 1))
                last.then_inc(s.out_made, 1)
                for j in range(2):
                    pe.wait_ge(s.y_saved, j + 1)
                    for t in range(CT):
                        last = nc.tensor.transpose(k.psum[2 + j][:, P * t:P * (t + 1)], w.out_T[:, j, P * t:P * (t + 1)], k.ident[:, :])
                    last.then_inc(s.y_turned, 1)

            @block.scalar
            def _(act):
                for n in range(L3_N):
                    for m in range(L3_DC):
                        u = L3_DC * n + m
                        if u >= BUF:
                            act.wait_ge(s.scanned, u - BUF + 1)
                        nc.scalar.activation(w.decay[:, u % BUF, :, 1:], w.dt[:, m, bass.ds(hf * HALF, HALF)].rearrange("p (b n) -> p b n", n=SEQ)[:, :, 1:],
                                             ACT.Exp, scale=w.a_neg[:, m, n:n + 1]).then_inc(s.decay_ready, 1)
                    act.wait_ge(s.c_spread, n + 1)
                    if n >= 2:
                        act.wait_ge(s.weighted, L3_DC * (n - 1))
                    nc.scalar.activation(w.c_all[:, n % 2, :], k.psum_all[:, 2 * CHUNK:4 * CHUNK], ACT.Copy).then_inc(s.c_saved, 1)
                act.wait_ge(s.out_made, 1)
                for j in range(2):
                    nc.scalar.activation(w.out_T[:, j, :], k.psum[j][:, :], ACT.Copy).then_inc(s.y_saved, 1)

            @block.gpsimd
            def _(pool):
                for u in range(UNITS):
                    pool.wait_ge(s.scanned, u + 1)
                    pool.wait_ge(s.c_saved, u // L3_DC + 1)
                    if u >= BUF:
                        pool.wait_ge(s.summed, u - BUF + 1)
                    nc.gpsimd.tensor_tensor(w.weighted[:, u % BUF, :], w.state[:, u % BUF, :], w.c_all[:, u // L3_DC % 2, :], ALU.mult)\
                        .then_inc(s.weighted, 1)

            @block.vector
            def _(dve):
                step = Steps(dve, s.dve_step)
                for u in range(UNITS):
                    n, m = u // L3_DC, u % L3_DC
                    if m == 0:
                        dve.wait_ge(s.b_spread, n + 1)
                    nc.vector.tensor_tensor(w.inflow[:, u % 2, :], w.xdt[:, m, bass.ds(hf * HALF, HALF)], k.psum_all[:, 0:HALF], ALU.mult)\
                        .then_inc(s.input_ready, 1)
                    dve.wait_ge(s.input_ready, u + 1)
                    dve.wait_ge(s.decay_ready, u + 1)
                    if u >= BUF:
                        dve.wait_ge(s.weighted, u - BUF + 1)
                    nc.vector.tensor_tensor_scan(w.state[:, u % BUF, :], w.decay[:, u % BUF, :, :].rearrange("p b n -> p (b n)"), w.inflow[:, u % 2, :],
                                                 0.0, ALU.mult, ALU.add).then_inc(s.scanned, 1)
                dve.wait_ge(s.summed, UNITS)
                for m in range(L3_DC):
                    step.add(nc.vector.scalar_tensor_tensor(w.gated[:, m, :], w.xs[:, m, bass.ds(hf * HALF, HALF)], w.d_skip[:, m:m + 1],
                                                            k.psum_all[:, CHUNK * (4 + 2 * m):CHUNK * (6 + 2 * m)], ALU.mult, ALU.add))
                    step.wait()
                    nc.vector.tensor_tensor(w.gated[:, m, :], w.gated[:, m, :], w.z[:, m, bass.ds(hf * HALF, HALF)], ALU.mult).then_inc(s.y_ready, 1)
                for j in range(2):
                    dve.wait_ge(s.y_turned, j + 1)
                    rows = k.x[:, bass.ds(hf * (HALF // P) + CT * j, CT), :]
                    nc.vector.tensor_tensor(rows, rows, k.psum[2 + j][:, :].rearrange("p (t n) -> p t n", t=CT), ALU.add).then_inc(s.x_added, 1)


def quantised_ffn_stage(nc, k, w):
    BLOCKS = L3_LIN // 2
    with signals(nc, "first_made", "first_biased", "dve_step", "moments_ready", "rstd_ready", "normed", "turned", "gelu_ready", "second_made",
                 "h_ready", "h_turned", "x_added") as s:
        with nc.Block() as block:
            @block.tensor
            def _(pe):
                n_turn = 0
                for blk in range(BLOCKS):
                    h = k.xnT if blk == 0 else w.hT
                    for g in range(CHUNKS):
                        if blk:
                            pe.wait_ge(s.h_ready, CHUNKS * (blk - 1) + g + 1)
                            pe.wait_ge(s.first_biased, CHUNKS * (blk - 1) + g + 1)
                        for j in range(CT):
                            c = CHUNK * g + P * j
                            last = nc.tensor.matmul(k.psum[g][:, P * j:P * (j + 1)], h[:, c:c + P], w.linearT[:, 2 * blk, :], start=True, stop=True)
                        last.then_inc(s.first_made, 1)
                    for g in range(CHUNKS):
                        pe.wait_ge(s.normed, TILES * blk + CT * (g + 1))
                        if n_turn >= 2:
                            pe.wait_ge(s.gelu_ready, n_turn - 1)
                        for j in range(CT):
                            last = nc.tensor.transpose(k.psum[4 + n_turn % 2][:, P * j:P * (j + 1)], w.y[:, CT * g + j, :], k.ident[:, :])
                        last.then_inc(s.turned, 1)
                        n_turn += 1
                        pe.wait_ge(s.gelu_ready, n_turn)
                        if n_turn > 2:
                            pe.wait_ge(s.h_ready, n_turn - 2)
                        nc.tensor.matmul(k.psum[6 + n_turn % 2][:, :], w.linearT[:, 2 * blk + 1, :], w.gelu[:, (n_turn - 1) % 2, :],
                                         start=True, stop=True).then_inc(s.second_made, 1)
                for g in range(CHUNKS):
                    pe.wait_ge(s.h_ready, CHUNKS * (BLOCKS - 1) + g + 1)
                    for j in range(CT):
                        c = CHUNK * g + P * j
                        last = nc.tensor.transpose(k.psum[g][:, P * j:P * (j + 1)], w.hT[:, c:c + P], k.ident[:, :])
                    last.then_inc(s.h_turned, 1)

            @block.scalar
            def _(act):
                n = 0
                for blk in range(BLOCKS):
                    act.wait_ge(s.moments_ready, blk + 1)
                    nc.scalar.activation(k.rstd[:, :], k.rstd[:, :], ACT.Sqrt).then_inc(s.rstd_ready, 1)
                    for g in range(CHUNKS):
                        act.wait_ge(s.turned, n + 1)
                        if n >= 2:
                            act.wait_ge(s.second_made, n - 1)
                        nc.scalar.activation(w.gelu[:, n % 2, :], k.psum[4 + n % 2][:, :], ACT.Gelu, scale=w.gamma[:, blk:blk + 1],
                                             bias=w.beta[:, blk:blk + 1]).then_inc(s.gelu_ready, 1)
                        n += 1

            @block.vector
            def _(dve):
                step = Steps(dve, s.dve_step)
                for blk in range(BLOCKS):
                    for g in range(CHUNKS):
                        dve.wait_ge(s.first_made, CHUNKS * blk + g + 1)
                        if blk:
                            dve.wait_ge(s.turned, CHUNKS * blk)
                        bias = w.bias_rows[:, blk, :].unsqueeze(1).to_broadcast([P, CT, P])
                        nc.vector.tensor_tensor(w.y[:, CT * g:CT * (g + 1), :], k.psum[g][:, :].rearrange("p (t n) -> p t n", t=CT), bias, ALU.add)\
                            .then_inc(s.first_biased, 1)
                    dve.wait_ge(s.first_biased, CHUNKS * (blk + 1))
                    for t in range(TILES):
                        step.add(nc.vector.bn_stats(k.stats[:, t, :], w.y[:, t, :]))
                    step.wait()
                    for t in range(TILES):
                        step.add(nc.vector.bn_aggr(k.moments[:, t, :], k.stats[:, t, :]))
                    step.wait()
                    step.add(nc.vector.tensor_scalar(k.rstd[:, :], k.moments[:, :, 1], LN_EPS, None, ALU.add))
                    step.wait()
                    nc.vector.reciprocal(k.rstd[:, :], k.rstd[:, :]).then_inc(s.moments_ready, 1)
                    dve.wait_ge(s.rstd_ready, blk + 1)
                    for t in range(TILES):
                        nc.vector.tensor_scalar(w.y[:, t, :], w.y[:, t, :], k.moments[:, t, 0:1], k.rstd[:, t:t + 1], ALU.subtract, ALU.mult)\
                            .then_inc(s.normed, 1)
                    for g in range(CHUNKS):
                        n = CHUNKS * blk + g
                        dve.wait_ge(s.second_made, n + 1)
                        if blk:
                            dve.wait_ge(s.h_ready, CHUNKS * (blk - 1) + g + 1)
                        before = (k.xnT if blk == 0 else w.hT)[:, CHUNK * g:CHUNK * (g + 1)]
                        nc.vector.scalar_tensor_tensor(w.hT[:, CHUNK * g:CHUNK * (g + 1)], k.psum[6 + (n + 1) % 2][:, :], w.bias_cols[:, blk:blk + 1],
                                                       before, ALU.add, ALU.add).then_inc(s.h_ready, 1)
                for g in range(CHUNKS):
                    dve.wait_ge(s.h_turned, g + 1)
                    rows = k.x[:, CT * g:CT * (g + 1), :]
                    nc.vector.tensor_tensor(rows, rows, k.psum[g][:, :].rearrange("p (t n) -> p t n", t=CT), ALU.add).then_inc(s.x_added, 1)


def layer3(nc, k, d):
    with ExitStack() as held:
        def sb(name, shape, dt=F32):
            return held.enter_context(nc.sbuf_tensor(name, shape, dt))
        w = Names(
            w_in=sb("w_in", [P, 4 * P]), conv_w=sb("conv_w", [P, L3_DC, L3_CONV]), conv_b=sb("conv_b", [P, L3_DC]),
            w_x=sb("w_x", [P, L3_DC, 2 * L3_N + 1]), a_neg=sb("a_neg", [P, L3_DC, L3_N]), d_skip=sb("d_skip", [P, L3_DC]),
            w_dt=sb("w_dt", [P, L3_DC, P]), b_dt=sb("b_dt", [P, L3_DC]), w_out=sb("w_out3", [P, L3_DC, P]),
            codes=sb("codes", [P, L3_LIN, P], I32), scales=sb("scales", [P, L3_LIN * P // L3_GROUP]), linear=sb("linear", [P, L3_LIN, P]),
            linearT=sb("linearT", [P, L3_LIN, P]), lora_a=sb("lora_a", [L3_R, L3_LIN, P]), lora_b=sb("lora_b", [L3_R, L3_LIN, P]),
            gamma=sb("gamma", [P, 3]), beta=sb("beta", [P, 3]), bias_rows=sb("bias_rows", [P, 3, P]), bias_cols=sb("bias_cols", [P, 3]),
            xs=sb("xs", [P, L3_DC, TOKENS]), z=sb("z", [P, L3_DC, TOKENS]), dt=sb("dt", [P, L3_DC, TOKENS]), xdt=sb("xdt", [P, L3_DC, TOKENS]),
            projT=sb("projT", [P, TOKENS]), decay=sb("decay", [P, 3, HALF_SEQS, SEQ]))
        loads = [(w.w_in[:, :], d["w_in3"]), (w.conv_w[:, :, :], d["conv_w"]), (w.conv_b[:, :], d["conv_b"]), (w.w_x[:, :, :], d["w_x"]),
                 (w.a_neg[:, :, :], d["a_log"]), (w.d_skip[:, :], d["d_skip"]), (w.w_dt[:, :, :], d["w_dt"]), (w.b_dt[:, :], d["b_dt"]),
                 (w.w_out[:, :, :], d["w_out3"]), (w.codes[:, :, :], d["codes"]), (w.scales[:, :], d["scales"]), (w.lora_a[:, :, :], d["lora_a"]),
                 (w.lora_b[:, :, :], d["lora_b"]), (w.gamma[:, :], d["gamma"]), (w.beta[:, :], d["beta"]),
                 (w.bias_rows[:, :, :].rearrange("p l n -> p (l n)"), d["bias_rows"].partition_broadcast(P)), (w.bias_cols[:, :], d["bias_cols"])]
        layer_norm_stage(nc, k, loads)
        with nc.sbuf_tensor("padded", [P, L3_DC, BATCH, L3_CONV - 1 + SEQ], F32) as padded:
            w.padded = padded
            ssm_prepare_stage(nc, k, w)
        with ExitStack() as scan:
            def sc(name, shape):
                return scan.enter_context(nc.sbuf_tensor(name, shape, F32))
            w.c_all, w.weighted, w.state = sc("c_all", [P, 2, HALF]), sc("weighted", [P, 3, HALF]), sc("state", [P, 3, HALF])
            w.inflow = sc("inflow", [P, 2, HALF])
            w.gated, w.out_T = w.state, w.inflow[:, :, 0:CHUNK]
            with nc.Fori(0, 2) as hf:
                ssm_scan_stage(nc, k, hf, w)
        with ExitStack() as ffn:
            w.y = k.xn
            w.hT = ffn.enter_context(nc.sbuf_tensor("hT", [P, TOKENS], F32))
            w.gelu = ffn.enter_context(nc.sbuf_tensor("gelu", [P, 2, CHUNK], F32))
            quantised_ffn_stage(nc, k, w)



def layer0(nc, k, d):
    with ExitStack() as held:
        def sb(name, shape):
            return held.enter_context(nc.sbuf_tensor(name, shape, F32))
        w = Names(
            cols=sb("norm_cols", [P, 3]), inT=sb("in_T", [HD, 3, P]), fc=sb("fc", [HD, 3, HEADS * HD]), fused=sb("fused", [P, 3, HEADS * HD]),
            qbias=sb("qbias", [P, PAIRS]), kbias=sb("kbias", [P, PAIRS]), vbias=sb("vbias", [P, HEADS * HD]), obias=sb("obias", [P, 1]),
            wo=sb("wo", [P, PAIRS, P]), qkv_l=sb("qkv_l", [P, 3, 512]), qkv_h=sb("qkv_h", [P, 3, 512]), wo_l=sb("wo_l", [P, 4, P]),
            wo_h=sb("wo_h", [P, 4, P]), null_k=sb("null_k", [P, 4, 2]), null_v=sb("null_v", [P, 4, 8]), null_q=sb("null_q", [P, P]),
            route_tokens=sb("route_tokens", [P, BATCH, 16]), xlT=sb("xlT", [P, TOKENS]), xrT=sb("xrT", [P, TOKENS]),
            null_out=sb("null_out", [P, P]), earlier=k.gate_cmp[:, 0:4, :, :].rearrange("p j t e -> p (j t e)").rearrange("p (t n) -> p t n", t=SUB), compare=k.masked_scores[:, :, :, :].rearrange("p i t n -> p (i t) n"),
            scores_all=k.probs[:, :, :, :].rearrange("p i t n -> p (i t) n"))
        loads = [(w.cols[:, :], d["cols"]), (w.inT[:, :, :], d["inT"]), (w.fc[:, :, :], d["fc"]), (w.qbias[:, :], d["qbias"]),
                 (w.kbias[:, :], d["kbias"]), (w.vbias[:, :], d["vbias"].partition_broadcast(P)), (w.obias[:, :], d["obias0"]),
                 (w.wo[:, :, :], d["wo0"]), (w.qkv_l[:, :, :], d["qkv_l"]), (w.qkv_h[:, :, :], d["qkv_h"]), (w.wo_l[:, :, :], d["wo_l"]),
                 (w.wo_h[:, :, :], d["wo_h"]), (w.null_k[:, :, :], d["null_k"]), (w.null_v[:, :, :], d["null_v"]),
                 (w.null_q[:, :], d["null_q"].partition_broadcast(P)), (w.route_tokens[:, :, :], d["route_tokens"]), (k.logk[:, :], d["logk"]),
                 (k.window_mask[:, :, :], d["window_mask"]), (w.earlier[:, :, :], d["earlier"]), (k.head16[:, :], d["head16"]),
                 (k.head8[:, :], d["head8"]), (k.rot_cos[:, :, :], d["rot_cos"]), (k.rot_sin[:, :, :], d["rot_sin"])]
        layer_norm_stage(nc, k, loads, first=d["x"])
        layer0_prepare_stage(nc, k, w)
        main = Names(
            kind="l0", w=w, wq=lambda p: w.fused[:, 0, P * p:P * (p + 1)], wk=lambda p: w.fused[:, 1, P * p:P * (p + 1)],
            wv=lambda half: w.fused[:, 2, CHUNK * half:CHUNK * (half + 1)], qbias=lambda p: w.qbias[:, p:p + 1],
            query=lambda q, h, t: k.queryT[:, h // 2, P * t:P * (t + 1)], value=lambda q, h, kt: k.values[:, q % 2, kt, HD * h:HD * (h + 1)],
            wo=lambda o: w.wo[:, o, :], obias=w.obias[:, 0:1])
        with nc.Fori(0, BATCH // SEQS) as b:
            softmax_attention_stage(nc, k, b, main)
        route_stage(nc, k, w)

        def of(p, i):
            return (w.qkv_l if p < 4 else w.qkv_h)[:, i, P * (p % 4):P * (p % 4 + 1)]
        routed = Names(
            kind="l0ffn", w=w, wq=lambda p: of(p, 0), wk=lambda p: of(p, 1), wv=lambda half: (w.qkv_h if half else w.qkv_l)[:, 2, :],
            qbias=lambda p: 0.0, query=main.query, value=main.value, wo=lambda o: (w.wo_l if o < 4 else w.wo_h)[:, o % 4, :])
        with nc.Fori(0, BATCH // SEQS) as b:
            softmax_attention_stage(nc, k, b, routed)


def layer1(nc, k, d):
    with ExitStack() as held:
        def sb(name, shape):
            return held.enter_context(nc.sbuf_tensor(name, shape, F32))
        w = Names(
            w_q=sb("w_q", [P, 256]), w_k=sb("w_k", [P, 256]), w_k_enc=sb("w_k_enc", [P, 256]), w_v=sb("w_v", [P, 1024]),
            w_v_enc=sb("w_v_enc", [P, 1024]), w_out=sb("w_out", [P, PAIRS, P]), router=sb("router1", [P, L1_E]),
            w1=sb("w1", [P, L1_E * L1_H]), w3=sb("w3", [P, L1_E * L1_H]), w2=sb("w2", [P, L1_HC, P]),
            expert_of=sb("expert_of", [P, L1_E * L1_H]), causal=sb("causal", [P, SEQ + P]), ones=sb("ones", [P, HD]),
            kT=sb("kT", [P, 2, SEQ]), k_encT=sb("k_encT", [P, 2, L1_ENC]), v_enc=sb("v_enc", [P, 1024]), kernel=sb("kernel", [P, 3, SEQ + P]),
            kernel_enc=sb("kernel_enc", [P, 3, SEQ]), norm=sb("norm", [P, 2, SEQ]), silu=sb("silu", [P, 2, CHUNK]),
            hidden=sb("hidden1", [P, 3, CHUNK]))
        loads = [(dst, d[name]) for dst, name in (
            (w.w_q[:, :], "w_q1"), (w.w_k[:, :], "w_k1"), (w.w_k_enc[:, :], "w_k_enc1"), (w.w_v[:, :], "w_v1"), (w.w_v_enc[:, :], "w_v_enc1"),
            (w.w_out[:, :, :], "w_out1"), (w.router[:, :], "router1"), (w.w1[:, :], "w1_1"), (w.w3[:, :], "w3_1"), (w.w2[:, :, :], "w2_1"),
            (w.expert_of[:, :], "expert_of"), (w.causal[:, :], "causal"), (w.ones[:, :], "ones"))]
        layer_norm_stage(nc, k, loads)
        gate_stage(nc, k, w.router[:, :], False, zeros=(w.v_enc[:, :], w.kernel_enc[:, :, :]))
        with nc.Fori(0, BATCH) as b:
            taylor_attention_stage(nc, k, b, w)
        with nc.Fori(0, CHUNKS) as c:
            swiglu_experts_stage(nc, k, c, w)


def layer2(nc, k, d):
    with ExitStack() as held:
        def sb(name, shape):
            return held.enter_context(nc.sbuf_tensor(name, shape, F32))
        w = Names(
            w_rot=sb("w_rot", [P, 4, P]), w_v=sb("w_v2", [P, P]), wo=sb("wo2", [P, 4, P]), obias=sb("obias2", [P, 1]),
            router=sb("router2", [P, L2_E]), w1=sb("w1_2", [P, L2_E * L2_F]), w2=sb("w2_2", [P, L2_E * L2_FC, P]),
            padded_values=sb("padded_values", [P, 2, SUB, HEADS, 32]), hidden=sb("hidden2", [P, 3, CHUNK]), gate_all=sb("gate_all", [P, 2, CHUNK]))
        loads = [(w.w_rot[:, :, :], d["w_rot"]), (w.w_v[:, :], d["w_v2"]), (w.wo[:, :, :], d["wo2"]), (w.obias[:, :], d["obias2"]),
                 (w.router[:, :], d["router2"]), (w.w1[:, :], d["w1_2"]), (w.w2[:, :, :], d["w2_2"])]
        layer_norm_stage(nc, k, loads)
        gate_stage(nc, k, w.router[:, :], True, zeros=(w.padded_values[:, :, :, :, :],))
        narrow = Names(
            kind="l2", w=w, query=lambda q, h, t: k.rot[:, q % 2, 0, P * t:P * (t + 1)], value=lambda q, h, kt: w.padded_values[:, q % 2, kt, h, :],
            wo=lambda o: w.wo[:, o, :], obias=w.obias[:, 0:1])
        with nc.Fori(0, BATCH // SEQS) as b:
            softmax_attention_stage(nc, k, b, narrow)
        with nc.Fori(0, CHUNKS) as c:
            relu_experts_stage(nc, k, c, w)


def store_stage(nc, k, out):
    with signals(nc, "stored") as s:
        with nc.Block() as block:
            @block.sync
            def _(sp):
                sp.dma_start(out, k.x[:, :, :]).then_inc(s.stored, 16)
                sp.wait_ge(s.stored, 16)


def build(nc, d, out, layers=4):
    with ExitStack() as held:
        def sb(name, shape):
            return held.enter_context(nc.sbuf_tensor(name, shape, F32))
        k = Names(
            dram=d, scratch=nc.dram_tensor("scratch", (BATCH, SEQ), F32, kind="Internal").ap(),
            psum_all=held.enter_context(nc.psum_tensor("psum_all", [P, 8 * CHUNK], F32)),
            x=sb("x", [P, TILES, P]), xn=sb("xn", [P, TILES, P]), xnT=sb("xnT", [P, TOKENS]), ident=sb("ident", [P, P]),
            stats=sb("stats", [P, TILES, 6]), moments=sb("moments", [P, TILES, 2]), rstd=sb("rstd", [P, TILES]), rms=sb("rms", [P, TILES]),
            logits=sb("logits", [16, SEQ]), logit_max=sb("logit_max", [16, 1]), neg_a=sb("neg_a", [16, 1]), floor_m=sb("floor_m", [16, 1]),
            logk=sb("logk", [16, 1]), route_arg=sb("route_arg", [16, SEQ]), route_exp=sb("route_exp", [16, SEQ]),
            route_sum=sb("route_sum", [16, 1]), route_log=sb("route_log", [16, 1]), route_cols=sb("route_cols", [P, 2, SUB, 16]),
            rank=sb("rank", [P, 2, TILES]), route_w=sb("route_w", [P, 3, TILES]), route_b=sb("route_b", [P, 3, SEQS * SUB]),
            window_mask=sb("window_mask", [P, SUB, SEQ]), head16=sb("head16", [P, 8]), head8=sb("head8", [P, HEADS]),
            rot_cos=sb("rot_cos", [P, 2, SEQ]), rot_sin=sb("rot_sin", [P, 2, SEQ]),
            gateT=sb("gateT", [P, TOKENS]), gate=sb("gate", [P, TILES, 8]), gate_sum=sb("gate_sum", [P, TILES]),
            gate_rank=sb("gate_rank", [P, TILES, 8]), gate_cmp=sb("gate_cmp", [P, 8, TILES, 8]), y_chunk=sb("y_chunk", [P, CHUNK]))
        k.psum = [k.psum_all[:, CHUNK * i:CHUNK * (i + 1)] for i in range(8)]
        with ExitStack() as attn:
            def sa(name, shape):
                return attn.enter_context(nc.sbuf_tensor(name, shape, F32))
            k.xb = sa("xb", [P, 2, 2, SEQ])
            k.keys = sa("keys", [P, HEADS, SEQ])
            k.queryT = sa("queryT", [P, PAIRS, SEQ])
            k.values = sa("values", [P, 2, SUB, HEADS * HD])
            k.norm8 = k.values[:, 0, 0, :].rearrange("p (t n) -> p t n", n=P)
            k.probs = sa("probs", [P, PBUF, SUB, SEQ])
            k.probsT = sa("probsT", [P, 3, SUB, SEQ])
            k.outT = sa("outT", [P, 2, PAIRS, SEQ])
            k.yT = sa("yT", [P, 2, SEQ])
            k.masked_scores = sa("masked_scores", [P, 2, SUB, SEQ])
            k.negmax = sa("negmax", [P, HEADS, SUB])
            k.null_scores = sa("null_scores_sb", [P, 2, 2 * SUB])
            k.key_negmax = sa("key_negmax", [P, SUB])
            k.prob_sum = sa("prob_sum", [P, HEADS, SUB])
            k.recip = sa("recip", [P, HEADS, SUB])
            k.null_arg = sa("null_arg", [P, PAIRS, SUB])
            k.null_exp = sa("null_exp", [P, PAIRS, SUB])
            k.null_probs = sa("null_probs", [P, SUB, PAIRS])
            k.null_probsT = sa("null_probsT", [P, SEQ])
            k.mix = sa("mix", [P, SUB, P])
            k.rot = sa("rot", [P, 2, 2, SEQ])
            k.rot2 = sa("rot2", [P, 2, SEQ])
            layer0(nc, k, d)
            if layers > 1:
                layer1(nc, k, d)
            if layers > 2:
                layer2(nc, k, d)
        if layers > 3:
            layer3(nc, k, d)
        store_stage(nc, k, out)


def rows_first(a, n):
    return a.reshape(n, P, -1).transpose(1, 0, 2)


def lay_out(i):
    z = np.zeros
    f = np.float32
    a = {}
    a["x"] = i["L0_attn_z"]
    a["ident"] = np.eye(P, dtype=f)
    a["cols"] = np.stack([i["L0_ffn_ln_g"], i["L0_ffn_ln_b"], i["L0_ffn_rms_g"]], 1)
    a["inT"] = np.stack([i[f"L0_attn_{n}"].T for n in ("wq", "wk", "wv")], 1)
    a["fc"] = np.stack([i[f"L0_attn_{n}"] for n in ("fcq_w", "fck_w", "fcv_w")], 1)
    a["qbias"] = i["L0_attn_fcq_b"].reshape(PAIRS, P).T
    a["kbias"] = i["L0_attn_fck_b"].reshape(PAIRS, P).T
    a["vbias"] = i["L0_attn_fcv_b"]
    a["obias0"] = i["L0_attn_fco_b"].reshape(P, 1)
    a["wo0"] = rows_first(i["L0_attn_fco_w"], PAIRS)
    a["qkv_l"] = i["L0_ffn_w_qkv_l"].reshape(P, 3, 512)
    kv = i["L0_ffn_w_kv_h"]
    a["qkv_h"] = np.stack([i["L0_ffn_w_q_h"], kv[:, :, :HD].reshape(P, 512), kv[:, :, HD:].reshape(P, 512)], 1)
    a["wo_l"] = rows_first(i["L0_ffn_w_out_l"], 4)
    a["wo_h"] = rows_first(i["L0_ffn_w_out_h"], 4)
    nk, nv = i["L0_ffn_null_kv"]
    null_k, null_v = z((P, 4, 2), f), z((P, 4, 8), f)
    for h in range(PAIRS):
        rows = slice(HD * (h % 2), HD * (h % 2 + 1))
        null_k[rows, h // 2, h % 2] = nk[h]
        null_v[rows, h // 2, h] = nv[h]
    a["null_k"], a["null_v"] = null_k, null_v
    a["null_q"] = i["L0_ffn_null_q"]
    rt = z((P, BATCH, 16), f)
    for b in range(BATCH):
        rt[:, b, b] = i["L0_ffn_rt_q"][0]
        rt[:, b, BATCH + b] = i["L0_ffn_rt_kv"][0]
    a["route_tokens"] = rt
    a["logk"] = np.log(np.array([[KQ]] * BATCH + [[KKV]] * BATCH, f))
    token = np.arange(SEQ)
    mine = (np.arange(P)[:, None, None] + P * np.arange(SUB)[None, :, None])
    a["window_mask"] = np.where(abs(mine // 64 - token // 64) <= 1, 0.0, -3e38).astype(f)
    a["earlier"] = (token < mine).astype(f)
    r = np.arange(P)
    a["head16"] = (r[:, None] // L1_FD == np.arange(8)).astype(f)
    a["head8"] = (r[:, None] // L2_D == np.arange(HEADS)).astype(f)
    inv = (f(1.0) / f(10000.0) ** (np.arange(0, L2_D, 2, dtype=f) / f(L2_D))).astype(f)
    angle = (token.astype(f)[None, :] * inv[r % L2_D % 4][:, None]).astype(f)
    sign = np.where(r % L2_D < 4, -1.0, 1.0)[:, None]
    scale = np.array([L2_D ** -0.5, 1.0])[None, :, None]
    a["rot_cos"] = (np.cos(angle.astype(np.float64))[:, None, :] * scale).astype(f)
    a["rot_sin"] = ((sign * np.sin(angle.astype(np.float64)))[:, None, :] * scale).astype(f)
    for n, m in (("w_q1", "Wq"), ("w_k1", "Wk"), ("w_k_enc1", "Wk_enc"), ("w_v1", "Wv"), ("w_v_enc1", "Wv_enc")):
        a[n] = i[f"L1_attn_{m}"].T
    a["w_out1"] = rows_first(i["L1_attn_Wout"].T, PAIRS)
    a["router1"] = i["L1_ffn_w_router"].T
    a["w1_1"] = i["L1_ffn_w1"].transpose(1, 0, 2).reshape(P, -1)
    a["w3_1"] = i["L1_ffn_w3"].transpose(1, 0, 2).reshape(P, -1)
    a["w2_1"] = rows_first(i["L1_ffn_w2"].reshape(-1, P), L1_HC)
    a["expert_of"] = (np.arange(L1_E * L1_H)[None, :] // L1_H == r[:, None]).astype(f)
    c = np.arange(P)
    tri = (c[None, :] >= r[:, None]).astype(f)
    a["causal"] = np.concatenate([tri, np.ones((P, P), f), tri], 1)
    a["ones"] = np.ones((P, HD), f)
    w = i["L2_attn_w_qkv"].reshape(3, HEADS, L2_D, P)
    straight, swapped = [0, 2, 4, 6, 1, 3, 5, 7], [1, 3, 5, 7, 0, 2, 4, 6]
    a["w_rot"] = np.stack([w[n][:, order].reshape(P, P).T for order in (straight, swapped) for n in (0, 1)], 1)
    a["w_v2"] = w[2].reshape(P, P).T
    wo = z((4, 32, 4, P), f)
    wo[:, :L2_D] = i["L2_attn_w_proj"].T.reshape(4, 4, L2_D, P).transpose(1, 2, 0, 3)
    a["wo2"] = wo.reshape(P, 4, P)
    a["obias2"] = i["L2_attn_b_proj"].reshape(P, 1)
    a["router2"] = i["L2_ffn_Wr"]
    a["w1_2"] = i["L2_ffn_W1"].transpose(1, 0, 2).reshape(P, -1)
    a["w2_2"] = rows_first(i["L2_ffn_W2"].reshape(-1, P), L2_E * L2_FC)
    a["w_in3"] = i["L3_attn_W_in"].T
    a["conv_w"] = i["L3_attn_conv_w"].reshape(L3_DC, P, L3_CONV).transpose(1, 0, 2)
    a["w_x"] = rows_first(i["L3_attn_W_x"].T, L3_DC)
    a["a_log"] = rows_first(i["L3_attn_A_log"], L3_DC)
    w_dt = z((P, L3_DC, P), f)
    w_dt[2 * L3_N] = i["L3_attn_W_dt"].reshape(L3_DC, P)
    a["w_dt"] = w_dt
    for n, m in (("conv_b", "conv_b"), ("d_skip", "D_param"), ("b_dt", "b_dt")):
        a[n] = i[f"L3_attn_{m}"].reshape(L3_DC, P).T
    a["w_out3"] = rows_first(i["L3_attn_W_out"].T, L3_DC)
    a["codes"] = i["L3_ffn_qweights"].transpose(1, 0, 2)
    a["scales"] = i["L3_ffn_scales"].transpose(1, 0, 2).reshape(P, -1)
    a["lora_a"] = i["L3_ffn_lora_a"].transpose(1, 0, 2)
    a["lora_b"] = i["L3_ffn_lora_b"].transpose(2, 0, 1)
    a["gamma"], a["beta"] = i["L3_ffn_ln_gamma"].T, i["L3_ffn_ln_beta"].T
    a["bias_rows"] = i["L3_ffn_biases"][0::2].reshape(-1)
    a["bias_cols"] = i["L3_ffn_biases"][1::2].T
    return {n: np.ascontiguousarray(v) for n, v in a.items()}


def kernel(**inputs):
    import concourse.bacc as bacc
    from concourse.bass_utils import run_bass_kernel_spmd

    nc = bacc.Bacc("TRN2", target_bir_lowering=False, num_devices=1)
    arrays = lay_out({n: np.asarray(v) for n, v in inputs.items()})
    d = {n: nc.dram_tensor(n + "_dram", v.shape, mybir.dt.from_np(v.dtype), kind="ExternalInput").ap() for n, v in arrays.items()}
    d["x"] = d["x"].rearrange("b (s p) n -> p (b s) n", p=P)
    out = nc.dram_tensor("out_dram", (BATCH, SEQ, DIM), F32, kind="ExternalOutput").ap()
    build(nc, d, out.rearrange("b (s p) n -> p (b s) n", p=P))
    r = run_bass_kernel_spmd(nc, [{n + "_dram": v for n, v in arrays.items()}], core_ids=[0])
    return r.results[0]["out_dram"]
```

```python
from contextlib import ExitStack, contextmanager

import numpy as np
import concourse.bass as bass
from concourse import mybir

F32 = mybir.dt.float32
I32 = mybir.dt.int32
BF16 = mybir.dt.bfloat16
ALU = mybir.AluOpType
ACT = mybir.ActivationFunctionType
AXX = mybir.AxisListType.X

BATCH, SEQ, DIM = 8, 256, 128
P = 128
TOKENS = BATCH * SEQ
TILES = TOKENS // P
SUB = SEQ // P
CHUNK = 512
CHUNKS = TOKENS // CHUNK
CT = CHUNK // P
LN_EPS = 1e-5

HEADS = 16
HD = 64
PAIRS = HEADS // 2
DESCENTS = 50
NQ, NKV = 128, 256
KQ, KKV = NQ * 9.0 / 8.0, NKV * 9.0 / 8.0
DESCENTS_PER_SEQ = 6

L1_FD = 16
L1_ENC = 64
L1_EPS = 1e-12
L1_E, L1_H = 8, 176
L1_HC = L1_E * L1_H // P
L2_D = 8
L2_E, L2_F = 8, 512
L2_FC = L2_F // P
L3_IN, L3_N, L3_CONV = 256, 16, 4
L3_DC = L3_IN // P
L3_R, L3_GROUP, L3_LIN = 32, 16, 6
PARTS, PART_ROWS = 3, 32
SPREAD_K = PARTS * PART_ROWS



class Names(dict):

    def __getattr__(self, name):
        return self[name]


@contextmanager
def signals(nc, *names):
    with ExitStack() as held:
        sems = {n: held.enter_context(nc.semaphore(n)) for n in names}
        yield Names(**sems)
        for s in sems.values():
            nc.sync.sem_clear(s)
        nc.all_engine_barrier()


class Steps:

    def __init__(self, engine, sem):
        self.engine, self.sem, self.n = engine, sem, 0

    def add(self, instruction):
        instruction.then_inc(self.sem, 1)
        self.n += 1
        return self.n

    def wait(self):
        self.engine.wait_ge(self.sem, self.n)


def bank(k, i):
    return k.psum[i]



def layer_norm_stage(nc, k, loads=(), first=None):
    with signals(nc, "x_loaded", "weights_loaded", "dve_step", "moments_ready", "rstd_ready", "tile_normed", "group_turned", "group_saved") as s:
        with nc.Block() as block:
            @block.sync
            def _(sp):
                if first is not None:
                    sp.dma_start(k.x[:, :, :], first).then_inc(s.x_loaded, 16)
                    sp.dma_start(k.ident[:, :], k.dram["ident"]).then_inc(s.x_loaded, 16)
                for dst, src in loads:
                    sp.dma_start(dst, src).then_inc(s.weights_loaded, 16)
                if loads:
                    sp.wait_ge(s.weights_loaded, 16 * len(loads))

            @block.vector
            def _(dve):
                step = Steps(dve, s.dve_step)
                if first is not None:
                    dve.wait_ge(s.x_loaded, 32)
                for t in range(TILES):
                    step.add(nc.vector.bn_stats(k.stats[:, t, :], k.x[:, t, :]))
                step.wait()
                for t in range(TILES):
                    step.add(nc.vector.bn_aggr(k.moments[:, t, :], k.stats[:, t, :]))
                step.wait()
                step.add(nc.vector.tensor_scalar(k.rstd[:, :], k.moments[:, :, 1], LN_EPS, None, ALU.add))
                step.wait()
                nc.vector.reciprocal(k.rstd[:, :], k.rstd[:, :]).then_inc(s.moments_ready, 1)
                dve.wait_ge(s.rstd_ready, 1)
                for t in range(TILES):
                    nc.vector.tensor_scalar(k.xn[:, t, :], k.x[:, t, :], k.moments[:, t, 0:1], k.rstd[:, t:t + 1],
                                            ALU.subtract, ALU.mult).then_inc(s.tile_normed, 1)


            @block.tensor
            def _(pe):
                if first is not None:
                    pe.wait_ge(s.x_loaded, 32)
                for g in range(CHUNKS):
                    pe.wait_ge(s.tile_normed, CT * (g + 1))
                    if g >= 2:
                        pe.wait_ge(s.group_saved, g - 1)
                    for j in range(CT):
                        last = nc.tensor.transpose(bank(k, g % 2)[:, P * j:P * (j + 1)], k.xn[:, CT * g + j, :], k.ident[:, :])
                    last.then_inc(s.group_turned, 1)

            @block.scalar
            def _(act):
                act.wait_ge(s.moments_ready, 1)
                nc.scalar.activation(k.rstd[:, :], k.rstd[:, :], ACT.Sqrt).then_inc(s.rstd_ready, 1)
                for g in range(CHUNKS):
                    act.wait_ge(s.group_turned, g + 1)
                    nc.scalar.activation(k.xnT[:, CHUNK * g:CHUNK * (g + 1)], bank(k, g % 2)[:, :], ACT.Copy).then_inc(s.group_saved, 1)


def layer0_prepare_stage(nc, k, w):
    with signals(nc, "dve_step", "moments_ready", "factors_ready", "light_normed", "rms_normed", "turned", "saved", "logits_made", "logits_saved", "route_dve", "route_act",
                 "fused_made", "fused_saved", "nullw_made", "act_step", "pool_step") as s:
        with nc.Block() as block:
            @block.vector
            def _(dve):
                step = Steps(dve, s.dve_step)
                for t in range(TILES):
                    step.add(nc.vector.bn_stats(k.stats[:, t, :], k.xn[:, t, :]))
                step.wait()
                for t in range(TILES):
                    step.add(nc.vector.bn_aggr(k.moments[:, t, :], k.stats[:, t, :]))
                step.wait()
                step.add(nc.vector.tensor_tensor(k.rms[:, :], k.moments[:, :, 0], k.moments[:, :, 0], ALU.mult))
                step.wait()
                step.add(nc.vector.tensor_tensor(k.rms[:, :], k.rms[:, :], k.moments[:, :, 1], ALU.add))
                step.wait()
                step.add(nc.vector.tensor_scalar(k.rms[:, :], k.rms[:, :], float(DIM), 1e-24, ALU.mult, ALU.max))
                step.add(nc.vector.tensor_scalar(k.rstd[:, :], k.moments[:, :, 1], LN_EPS, None, ALU.add))
                step.wait()
                nc.vector.reciprocal(k.rms[:, :], k.rms[:, :]).then_inc(s.moments_ready, 1)
                nc.vector.reciprocal(k.rstd[:, :], k.rstd[:, :]).then_inc(s.moments_ready, 1)
                dve.wait_ge(s.factors_ready, 2)
                for t in range(TILES):
                    if t >= 8:
                        dve.wait_ge(s.turned, (t - 8) // CT + 1)
                    nc.vector.tensor_scalar(k.norm8[:, t % 8, :], k.xn[:, t, :], k.moments[:, t, 0:1], k.rstd[:, t:t + 1],
                                            ALU.subtract, ALU.mult).then_inc(s.light_normed, 1)
                for t in range(TILES):
                    dve.wait_ge(s.turned, (t + 8) // CT + 1)
                    nc.vector.tensor_scalar(k.norm8[:, t % 8, :], k.xn[:, t, :], k.rms[:, t:t + 1], None, ALU.mult).then_inc(s.rms_normed, 1)
                dve.wait_ge(s.logits_made, 1)
                step.add(nc.vector.tensor_copy(k.logits[:, :], bank(k, 7)[0:16, 0:SEQ]))
                step.wait()
                step.add(nc.vector.reduce_max(k.logit_max[:, :], k.logits[:, :], AXX))
                step.add(nc.vector.tensor_scalar(k.neg_a[:, :], k.logk[:, :], -1.0, float(np.log(np.float32(SEQ))), ALU.mult, ALU.add))
                step.wait()
                step.add(nc.vector.tensor_scalar(k.floor_m[:, :], k.neg_a[:, :], k.logit_max[:, :], None, ALU.min))
                for i in range(1, DESCENTS - BATCH * DESCENTS_PER_SEQ):
                    step.wait()
                    descend_dve_first(nc, k).then_inc(s.route_dve, 1)
                    dve.wait_ge(s.route_act, i)
                    step.add(descend_dve_a(nc, k))
                    step.wait()
                    step.add(descend_dve_m(nc, k))

            @block.scalar
            def _(act):
                act.wait_ge(s.moments_ready, 2)
                nc.scalar.activation(k.rstd[:, :], k.rstd[:, :], ACT.Sqrt).then_inc(s.factors_ready, 1)
                nc.scalar.activation(k.rms[:, :], k.rms[:, :], ACT.Sqrt, scale=float(DIM)).then_inc(s.factors_ready, 1)
                for g in range(2 * CHUNKS):
                    light = g < CHUNKS
                    act.wait_ge(s.turned, g + 1)
                    dst = (w.xlT if light else w.xrT)[:, CHUNK * (g % CHUNKS):CHUNK * (g % CHUNKS + 1)]
                    if light:
                        ins = nc.scalar.activation(dst, bank(k, g % 2)[:, :], ACT.Identity, scale=w.cols[:, 0:1], bias=w.cols[:, 1:2])
                    else:
                        ins = nc.scalar.activation(dst, bank(k, g % 2)[:, :], ACT.Copy, scale=w.cols[:, 2:3])
                    ins.then_inc(s.saved, 1)
                for i in range(6):
                    act.wait_ge(s.fused_made, i + 1)
                    nc.scalar.activation(w.fused[:, i // 2, CHUNK * (i % 2):CHUNK * (i % 2 + 1)], bank(k, 2 + i % 2)[:, :], ACT.Copy)\
                        .then_inc(s.fused_saved, 1)
                act.wait_ge(s.nullw_made, 1)
                act.wait_ge(s.pool_step, 2)
                nc.scalar.activation(w.null_out[0:8, :], bank(k, 4)[0:8, 0:P], ACT.Copy).then_inc(s.act_step, 1)
                nc.scalar.activation(w.qbias[:, :], w.qbias[:, :], ACT.Copy, scale=HD ** -0.5).then_inc(s.act_step, 1)
                nc.scalar.preload_act_table_set("natural_log_exp_and_others")
                for i in range(1, DESCENTS - BATCH * DESCENTS_PER_SEQ):
                    act.wait_ge(s.route_dve, i)
                    nc.scalar.activation(k.route_exp[:, :], k.route_arg[:, :], ACT.Exp, accum_out=k.route_sum[:, :]).then_inc(s.act_step, 1)
                    act.wait_ge(s.act_step, 2 + i)
                    nc.scalar.activation(k.route_log[:, :], k.route_sum[:, :], ACT.Ln).then_inc(s.route_act, 1)

            @block.gpsimd
            def _(pool):
                nc.gpsimd.memset(w.null_out[:, :], 0.0).then_inc(s.pool_step, 1)
                nc.gpsimd.memset(k.null_probsT[:, :], 0.0).then_inc(s.pool_step, 1)
                nc.gpsimd.memset(k.keys[:, :, :], 0.0).then_inc(s.pool_step, 1)

            @block.tensor
            def _(pe):
                for g in range(2 * CHUNKS):
                    light = g < CHUNKS
                    if light:
                        pe.wait_ge(s.light_normed, CT * (g + 1))
                    else:
                        pe.wait_ge(s.rms_normed, CT * (g - CHUNKS + 1))
                    if g >= 2:
                        pe.wait_ge(s.saved, g - 1)
                    for j in range(CT):
                        last = nc.tensor.transpose(bank(k, g % 2)[:, P * j:P * (j + 1)], k.norm8[:, (CT * g + j) % 8, :], k.ident[:, :])
                    last.then_inc(s.turned, 1)
                for b in range(BATCH):
                    last = nc.tensor.matmul(bank(k, 7)[0:16, 0:SEQ], w.route_tokens[:, b, :], k.xnT[:, SEQ * b:SEQ * (b + 1)],
                                            start=(b == 0), stop=(b == BATCH - 1))
                last.then_inc(s.logits_made, 1)
                for i in range(6):
                    if i >= 2:
                        pe.wait_ge(s.fused_saved, i - 1)
                    nc.tensor.matmul(bank(k, 2 + i % 2)[:, :], w.inT[:, i // 2, :], w.fc[:, i // 2, CHUNK * (i % 2):CHUNK * (i % 2 + 1)],
                                     start=True, stop=True).then_inc(s.fused_made, 1)
                for c in range(4):
                    last = nc.tensor.matmul(bank(k, 4)[0:8, 0:P], w.null_v[:, c, :], w.wo_h[:, c, :], start=(c == 0), stop=(c == 3))
                last.then_inc(s.nullw_made, 1)


def descend_dve_first(nc, k):
    return nc.vector.tensor_scalar(k.route_arg[:, :], k.logits[:, :], k.neg_a[:, :], k.floor_m[:, :], ALU.min, ALU.subtract)


def descend_dve_a(nc, k):
    return nc.vector.tensor_scalar(k.neg_a[:, :], k.route_log[:, :], k.floor_m[:, :], k.logk[:, :], ALU.add, ALU.subtract)


def descend_dve_m(nc, k):
    return nc.vector.tensor_scalar(k.floor_m[:, :], k.neg_a[:, :], k.logit_max[:, :], None, ALU.min)



PT_LAG, PV_LAG = 2, 3
PBUF = 4
SEQS = 4


def attention_jobs(kind):
    before, at = [], [[] for _ in range(SEQS * HEADS + 6)]
    for q in range(SEQS):
        if kind == "l2":
            first = [("straight", q, 0), ("swapped", q, 0), ("narrow_values", q, 0)]
        else:
            first = [("pair", q, 0)] + [("values", q, i) for i in range(2 * SUB)]
        if q == 0:
            before += first
        elif kind == "l2":
            for i, job in enumerate(first):
                at[HEADS * (q - 1) + 5 + 2 * i].append(job)
        else:
            for i, job in enumerate(first[1:]):
                at[HEADS * (q - 1) + 5 + 2 * i].append(job)
            at[HEADS * q - 2].append(first[0])
        if kind != "l2":
            for p in range(1, PAIRS):
                at[HEADS * q + 2 * (p - 1)].append(("pair", q, p))
        if kind == "l0ffn":
            at[HEADS * (q + 1) + 3].append(("null_probs", q, 0))
        at[HEADS * (q + 1) + 4].append(("output", q, 0))
        at[HEADS * (q + 1) + 5].append(("output_turned", q, 0))
    return before, at


def softmax_attention_stage(nc, k, b, c):
    l0, ffn, l2 = c.kind == "l0", c.kind == "l0ffn", c.kind == "l2"
    per_out = 4 if l2 else 2
    outs = HEADS // per_out
    mcols = P // per_out
    SB, TB, OB, JB = (0, 1), (3, 4), (5, 6), (7, 2)
    N = SEQS * HEADS
    before, at = attention_jobs(c.kind)
    order = before + [job for jobs in at for job in jobs]
    number = {job: i for i, job in enumerate(order)}
    steps = range(N + 6)

    def job_bank(job):
        return k.psum[JB[number[job] % 2]]

    def saver(job):
        what, _, i = job
        if what in ("null_probs", "output") or (ffn and what == "values" and i % 2):
            return "act"
        return "dve"

    def saved_count(job):
        return sum(saver(j) == saver(job) for j in order[:number[job] + 1])

    def last_input_job(q):
        return [job for job in order if job[1] == q and not job[0].startswith(("null", "output"))][-1]

    def masked(g):
        return ffn and g % HEADS < PAIRS

    def nulled(g):
        return ffn and g % HEADS >= PAIRS

    def null_pairs(g):
        return 4 * (g // HEADS) + g % HEADS // 2 - 3

    def null_heads(g):
        return PAIRS * (g // HEADS) + g % HEADS - PAIRS + 1

    def by_act(g):
        return g % 2 == 1 or not l2

    with signals(nc, "x_copied", "job_made", "query_saved", "act_saved_job", "dve_saved_job", "head_keys", "scores_ready",
                 "masked_ready", "negmax_ready", "probs_ready", "recip_ready", "probs_normed", "turned", "dve_turned", "act_turned",
                 "values_weighed", "out_saved", "null_scores", "null_taken", "null_args", "null_exps", "null_weights", "weights_picked",
                 "route_dve", "route_act", "act_step", "dve_step") as s:

        def wait_saved(engine, job):
            engine.wait_ge(s.act_saved_job if saver(job) == "act" else s.dve_saved_job, saved_count(job))

        def wait_made(engine, job):
            engine.wait_ge(s.job_made, number[job] + 1)

        with nc.Block() as block:

            @block.gpsimd
            def _(pool):
                def copy_inputs(q):
                    if q >= 2:
                        wait_made(pool, last_input_job(q - 2))
                    cols = bass.ds((b * SEQS + q) * SEQ, SEQ)
                    for i, src in enumerate((c.w.xlT, c.w.xrT) if ffn else (k.xnT,)):
                        nc.gpsimd.tensor_copy(k.xb[:, q % 2, i, :], src[:, cols]).then_inc(s.x_copied, 1)

                for q in range(2):
                    copy_inputs(q)
                for q in range(SEQS):
                    if q >= 2 and not l2:
                        copy_inputs(q)
                    if l2:
                        pool.wait_ge(s.query_saved, q + 1)
                        for h in range(HEADS):
                            if q:
                                pool.wait_ge(s.scores_ready, HEADS * (q - 1) + h + 1)
                            nc.gpsimd.tensor_scalar(k.keys[:, h, :], k.rot[:, q % 2, 1, :], k.head8[:, h:h + 1], None, ALU.mult).then_inc(s.head_keys, 1)
                        if q + 2 < SEQS:
                            copy_inputs(q + 2)

            @block.tensor
            def _(pe):
                def do(job):
                    what, q, i = job
                    n = number[job]
                    if n >= 2:
                        wait_saved(pe, order[n - 2])
                    jb = job_bank(job)
                    xb = k.xb[:, q % 2]
                    if what in ("pair", "values", "straight"):
                        pe.wait_ge(s.x_copied, (2 if ffn else 1) * (q + 1))
                    if what == "pair":
                        src = xb[:, 1 if ffn and i >= 4 else 0, :]
                        nc.tensor.matmul(jb[:, 0:SEQ], c.wq(i), src, start=True, stop=True)
                        last = nc.tensor.matmul(jb[:, SEQ:2 * SEQ], c.wk(i), src, start=True, stop=True)
                    elif what == "values":
                        t, half = i // 2, i % 2
                        last = nc.tensor.matmul(jb[:, :], xb[:, 1 if ffn and half else 0, P * t:P * (t + 1)], c.wv(half), start=True, stop=True)
                    elif what in ("straight", "swapped"):
                        for j in range(2):
                            last = nc.tensor.matmul(jb[:, SEQ * j:SEQ * (j + 1)], c.w.w_rot[:, (what == "swapped") * 2 + j, :], xb[:, 0, :],
                                                    start=True, stop=True)
                    elif what == "narrow_values":
                        for t in range(SUB):
                            last = nc.tensor.matmul(jb[:, P * t:P * (t + 1)], xb[:, 0, P * t:P * (t + 1)], c.w.w_v[:, :], start=True, stop=True)
                    elif what == "null_probs":
                        pe.wait_ge(s.null_weights, PAIRS * (q + 1))
                        for t in range(SUB):
                            last = nc.tensor.transpose(jb[0:8, P * t:P * (t + 1)], k.null_probs[:, t, :], k.ident[:, :])
                    elif what == "output":
                        pe.wait_ge(s.out_saved, outs * (q + 1))
                        for g, (o0, o1) in enumerate([(0, 4), (4, 8)] if ffn else [(0, outs)]):
                            for o in range(o0, o1):
                                last = nc.tensor.matmul(jb[:, SEQ * g:SEQ * (g + 1)], c.wo(o), k.outT[:, q % 2, o, :],
                                                        start=(o == o0), stop=(o == o1 - 1 and g == 0))
                            if g == 1:
                                wait_saved(pe, ("null_probs", q, 0))
                                last = nc.tensor.matmul(jb[:, SEQ:2 * SEQ], c.w.null_out[:, :], k.null_probsT[:, :], start=False, stop=True)
                    else:
                        wait_saved(pe, ("output", q, 0))
                        for g in range(2 if ffn else 1):
                            for t in range(SUB):
                                last = nc.tensor.transpose(jb[:, SEQ * g + P * t:SEQ * g + P * (t + 1)], k.yT[:, g, P * t:P * (t + 1)], k.ident[:, :])
                    last.then_inc(s.job_made, 1)

                def scores(g):
                    q, h = g // HEADS, g % HEADS
                    if l2:
                        pe.wait_ge(s.query_saved, q + 1)
                        pe.wait_ge(s.head_keys, g + 1)
                    else:
                        wait_saved(pe, ("pair", q, h // 2))
                    if g >= 2:
                        if masked(g - 2):
                            pe.wait_ge(s.masked_ready, PAIRS * ((g - 2) // HEADS) + (g - 2) % HEADS + 1)
                        else:
                            pe.wait_ge(s.probs_ready, 2 * (g - 1))
                    sb = k.psum[SB[g % 2]]
                    for t in range(SUB):
                        last = nc.tensor.matmul(sb[:, SEQ * t:SEQ * (t + 1)], c.query(q, h, t), k.keys[:, h, :], start=True, stop=True)
                    last.then_inc(s.scores_ready, 1)

                def null_scores(g):
                    q, p = g // HEADS, g % HEADS // 2
                    jb = job_bank(("pair", q, p))
                    for t in range(SUB):
                        last = nc.tensor.matmul(jb[:, 2 * t:2 * t + 2], c.query(q, 2 * p, t), c.w.null_k[:, p - 4, :], start=True, stop=True)
                    last.then_inc(s.null_scores, 1)

                def wait_turned(g):
                    mine = sum(by_act(i) == by_act(g) for i in range(g + 1))
                    pe.wait_ge(s.act_turned if by_act(g) else s.dve_turned, mine)

                def turn(g):
                    pe.wait_ge(s.probs_normed, 2 * (g + 1))
                    if g >= 2:
                        wait_turned(g - 2)
                    tb = k.psum[TB[g % 2]]
                    for kt in range(SUB):
                        for t in range(SUB):
                            last = nc.tensor.transpose(tb[:, SEQ * kt + P * t:SEQ * kt + P * (t + 1)],
                                                       k.probs[:, g % PBUF, t, P * kt:P * (kt + 1)], k.ident[:, :])
                    last.then_inc(s.turned, 1)

                def weigh_values(g):
                    wait_turned(g)
                    q, h = g // HEADS, g % HEADS
                    o = g // per_out
                    if h == 0:
                        for job in [("narrow_values", q, 0)] if l2 else [("values", q, 2), ("values", q, 3)]:
                            wait_saved(pe, job)
                    if o >= 2 and g % per_out == 0:
                        pe.wait_ge(s.out_saved, o - 1)
                    r = mcols * (g % per_out)
                    for kt in range(SUB):
                        last = nc.tensor.matmul(k.psum[OB[o % 2]][r:r + mcols, 0:SEQ], c.value(q, h, kt), k.probsT[:, g % 3, kt, :],
                                                start=(kt == 0), stop=(kt == SUB - 1))
                    last.then_inc(s.values_weighed, 1)

                for job in before:
                    do(job)
                for g in steps:
                    if g < N:
                        scores(g)
                        if nulled(g) and g % 2 == 0:
                            null_scores(g)
                            pe.wait_ge(s.null_taken, null_pairs(g))
                    for job in at[g]:
                        do(job)
                    if 0 <= g - PT_LAG < N:
                        turn(g - PT_LAG)
                    if 0 <= g - PV_LAG < N:
                        weigh_values(g - PV_LAG)

            @block.scalar
            def _(act):
                def do(job):
                    what, q, i = job
                    jb = job_bank(job)
                    if what == "pair":
                        wait_made(act, job)
                        nc.scalar.activation(k.queryT[:, i, :], jb[:, 0:SEQ], ACT.Identity, scale=HD ** -0.5, bias=c.qbias(i)).then_inc(s.query_saved, 1)
                    elif saver(job) == "act":
                        wait_made(act, job)
                        if what == "values":
                            act.wait_ge(s.weights_picked, 1)
                            ins = nc.scalar.activation(k.values[:, q % 2, i // 2, CHUNK:2 * CHUNK], jb[:, :], ACT.Copy, scale=k.route_b[:, 2, SUB * q + i // 2:SUB * q + i // 2 + 1])
                        elif what == "null_probs":
                            ins = nc.scalar.activation(k.null_probsT[0:8, :], jb[0:8, 0:SEQ], ACT.Copy)
                        elif ffn:
                            ins = nc.scalar.activation(k.yT[:, :, :].rearrange("p g n -> p (g n)"), jb[:, :], ACT.Copy)
                        else:
                            ins = nc.scalar.activation(k.yT[:, 0, :], jb[:, 0:SEQ], ACT.Identity, bias=c.obias)
                        ins.then_inc(s.act_saved_job, 1)

                def exponentials(g):
                    act.wait_ge(s.negmax_ready, g + 1)
                    if g >= PBUF:
                        act.wait_ge(s.turned, g - PBUF + 1)
                    for t in range(SUB):
                        src = k.masked_scores[:, g % 2, t, :] if masked(g) else k.psum[SB[g % 2]][:, SEQ * t:SEQ * (t + 1)]
                        nc.scalar.activation(k.probs[:, g % PBUF, t, :], src, ACT.Exp, bias=k.negmax[:, g % HEADS, t:t + 1],
                                             accum_out=k.prob_sum[:, g % HEADS, t:t + 1]).then_inc(s.probs_ready, 1)
                    if nulled(g):
                        act.wait_ge(s.null_args, null_heads(g))
                        i = g % HEADS - PAIRS
                        nc.scalar.activation(k.null_exp[:, i, :], k.null_arg[:, i, :], ACT.Exp).then_inc(s.null_exps, 1)

                def save_out(o):
                    act.wait_ge(s.values_weighed, per_out * (o + 1))
                    nc.scalar.activation(k.outT[:, o // outs % 2, o % outs, :], k.psum[OB[o % 2]][:, 0:SEQ], ACT.Copy).then_inc(s.out_saved, 1)

                def save_turned(g):
                    act.wait_ge(s.turned, g + 1)
                    if g >= 3:
                        act.wait_ge(s.values_weighed, g - 2)
                    nc.scalar.activation(k.probsT[:, g % 3, :, :].rearrange("p a n -> p (a n)"), k.psum[TB[g % 2]][:, :], ACT.Copy)\
                        .then_inc(s.act_turned, 1)

                def descend(i):
                    act.wait_ge(s.route_dve, i + 1)
                    nc.scalar.activation(k.route_exp[:, :], k.route_arg[:, :], ACT.Exp, accum_out=k.route_sum[:, :]).then_inc(s.act_step, 1)
                    act.wait_ge(s.act_step, i + 1)
                    nc.scalar.activation(k.route_log[:, :], k.route_sum[:, :], ACT.Ln).then_inc(s.route_act, 1)

                for job in before:
                    do(job)
                for g in steps:
                    for job in at[g]:
                        do(job)
                    if 0 <= g - PT_LAG < N and by_act(g - PT_LAG):
                        save_turned(g - PT_LAG)
                    if g < N:
                        exponentials(g)
                    if l0 and g % 2 == 1 and g // 2 < SEQS * DESCENTS_PER_SEQ:
                        descend(g // 2)
                    done = g - PV_LAG
                    if 0 <= done < N and done % per_out == per_out - 1:
                        save_out(done // per_out)

            @block.vector
            def _(dve):
                step = Steps(dve, s.dve_step)

                def add_output(job):
                    _, q, _ = job
                    jb = job_bank(job)
                    tile = (b * SEQS + q) * SUB
                    rows = k.x[:, bass.ds(tile, SUB), :]
                    if not ffn:
                        return nc.vector.tensor_tensor(rows, rows, jb[:, 0:SEQ].rearrange("p (t n) -> p t n", t=SUB), ALU.add)
                    for t in range(SUB):
                        i = SUB * q + t
                        step.add(nc.vector.scalar_tensor_tensor(k.mix[:, t, :], jb[:, SEQ + P * t:SEQ + P * (t + 1)], k.route_b[:, 0, i:i + 1],
                                                                k.x[:, bass.ds(tile + t, 1), :].rearrange("p a n -> p (a n)"),
                                                                ALU.mult, ALU.add))
                    step.wait()
                    for t in range(SUB):
                        i = SUB * q + t
                        step.add(nc.vector.scalar_tensor_tensor(k.mix[:, t, :], c.w.null_q[:, :], k.route_b[:, 1, i:i + 1], k.mix[:, t, :],
                                                                ALU.mult, ALU.add))
                    step.wait()
                    return nc.vector.tensor_tensor(rows, k.mix[:, :, :], jb[:, 0:SEQ].rearrange("p (t n) -> p t n", t=SUB), ALU.add)

                def do(job):
                    what, q, i = job
                    jb = job_bank(job)
                    if saver(job) != "dve":
                        return
                    wait_made(dve, job)
                    if what == "pair":
                        dve.wait_ge(s.query_saved, PAIRS * q + i + 1)
                        for j in range(2):
                            rows = slice(HD * j, HD * (j + 1))
                            dst, src = k.keys[rows, 2 * i + j, :], jb[rows, SEQ:2 * SEQ]
                            if l0:
                                ins = nc.vector.tensor_scalar(dst, src, c.w.kbias[rows, i:i + 1], None, ALU.add)
                            else:
                                ins = nc.vector.tensor_copy(dst, src)
                    elif what == "values":
                        t, half = i // 2, i % 2
                        dst = k.values[:, q % 2, t, CHUNK * half:CHUNK * (half + 1)]
                        if l0:
                            ins = nc.vector.tensor_tensor(dst, jb[:, :], c.w.vbias[:, CHUNK * half:CHUNK * (half + 1)], ALU.add)
                        else:
                            ins = nc.vector.tensor_copy(dst, jb[:, :])
                    elif what == "straight":
                        ins = nc.vector.tensor_tensor(k.rot[:, q % 2, :, :], jb[:, :].rearrange("p (i n) -> p i n", i=2), k.rot_cos[:, :, :], ALU.mult)
                    elif what == "swapped":
                        ins = nc.vector.tensor_tensor(k.rot2[:, :, :], jb[:, :].rearrange("p (i n) -> p i n", i=2), k.rot_sin[:, :, :], ALU.mult)
                        ins.then_inc(s.dve_saved_job, 1)
                        wait_saved(dve, job)
                        nc.vector.tensor_tensor(k.rot[:, q % 2, :, :], k.rot[:, q % 2, :, :], k.rot2[:, :, :], ALU.add).then_inc(s.query_saved, 1)
                        return
                    elif what == "narrow_values":
                        ins = nc.vector.tensor_copy(c.w.padded_values[:, q % 2, :, :, 0:L2_D],
                                                    jb[:, 0:SEQ].rearrange("p (t h d) -> p t h d", t=SUB, d=L2_D))
                    else:
                        ins = add_output(job)
                    ins.then_inc(s.dve_saved_job, 1)

                def negmax(g):
                    dve.wait_ge(s.scores_ready, g + 1)
                    h = g % HEADS
                    sb = k.psum[SB[g % 2]][:, :].rearrange("p (t n) -> p t n", t=SUB)
                    if masked(g):
                        n = PAIRS * (g // HEADS) + h + 1
                        if g >= 2:
                            dve.wait_ge(s.probs_ready, 2 * (g - 1))
                        nc.vector.tensor_tensor(k.masked_scores[:, g % 2, :, :], sb, k.window_mask[:, :, :], ALU.add).then_inc(s.masked_ready, 1)
                        dve.wait_ge(s.masked_ready, n)
                        sb = k.masked_scores[:, g % 2, :, :]
                    if not nulled(g):
                        nc.vector.reduce_max(k.negmax[:, h, :], sb, AXX, negate=True).then_inc(s.negmax_ready, 1)
                        return
                    p, j = h // 2, h % 2
                    if j == 0:
                        dve.wait_ge(s.null_scores, null_pairs(g))
                        nc.vector.tensor_copy(k.null_scores[:, p % 2, :], job_bank(("pair", g // HEADS, p))[:, 0:2 * SUB]).then_inc(s.null_taken, 1)
                    step.add(nc.vector.reduce_max(k.key_negmax[:, :], sb, AXX, negate=True))
                    step.wait()
                    dve.wait_ge(s.null_taken, null_pairs(g))
                    null = k.null_scores[:, p % 2, :].rearrange("p (t j) -> p t j", j=2)[:, :, j]
                    nc.vector.scalar_tensor_tensor(k.negmax[:, h, :], null, -1.0, k.key_negmax[:, :], ALU.mult, ALU.min).then_inc(s.negmax_ready, 1)
                    dve.wait_ge(s.negmax_ready, g + 1)
                    nc.vector.tensor_tensor(k.null_arg[:, h - PAIRS, :], null, k.negmax[:, h, :], ALU.add).then_inc(s.null_args, 1)

                def reciprocal(g):
                    h = g % HEADS
                    dve.wait_ge(s.probs_ready, 2 * (g + 1))
                    if nulled(g):
                        dve.wait_ge(s.null_exps, null_heads(g))
                        step.add(nc.vector.tensor_tensor(k.prob_sum[:, h, :], k.prob_sum[:, h, :], k.null_exp[:, h - PAIRS, :], ALU.add))
                        step.wait()
                    nc.vector.reciprocal(k.recip[:, h, :], k.prob_sum[:, h, :]).then_inc(s.recip_ready, 1)
                    dve.wait_ge(s.recip_ready, g + 1)
                    if nulled(g):
                        nc.vector.tensor_tensor(k.null_probs[:, :, h - PAIRS], k.null_exp[:, h - PAIRS, :], k.recip[:, h, :], ALU.mult)\
                            .then_inc(s.null_weights, 1)

                def normalise(g):
                    for t in range(SUB):
                        piece = k.probs[:, g % PBUF, t, :]
                        nc.vector.tensor_scalar(piece, piece, k.recip[:, g % HEADS, t:t + 1], None, ALU.mult).then_inc(s.probs_normed, 1)

                def save_turned(g):
                    dve.wait_ge(s.turned, g + 1)
                    if g >= 3:
                        dve.wait_ge(s.values_weighed, g - 2)
                    nc.vector.tensor_copy(k.probsT[:, g % 3, :, :].rearrange("p a n -> p (a n)"), k.psum[TB[g % 2]][:, :]).then_inc(s.dve_turned, 1)

                def descend(i):
                    if i >= 1:
                        dve.wait_ge(s.route_act, i)
                        step.add(descend_dve_a(nc, k))
                        step.wait()
                        step.add(descend_dve_m(nc, k))
                        step.wait()
                    if i < SEQS * DESCENTS_PER_SEQ:
                        descend_dve_first(nc, k).then_inc(s.route_dve, 1)

                if ffn:
                    nc.vector.tensor_copy(k.route_b[:, :, :], k.route_w[:, :, bass.ds(b * SEQS * SUB, SEQS * SUB)]).then_inc(s.weights_picked, 1)
                    dve.wait_ge(s.weights_picked, 1)
                for job in before:
                    do(job)
                for g in steps:
                    for job in at[g - 1] if g else []:
                        do(job)
                    if g < N:
                        negmax(g)
                    if 1 <= g <= N:
                        reciprocal(g - 1)
                        normalise(g - 1)
                    if l0 and g % 2 == 0 and g // 2 <= SEQS * DESCENTS_PER_SEQ:
                        descend(g // 2)
                    if 0 <= g - PT_LAG < N and not by_act(g - PT_LAG):
                        save_turned(g - PT_LAG)
                for job in at[steps[-1]]:
                    do(job)


def route_stage(nc, k, w):
    with signals(nc, "dve_step", "scored", "exped", "weighted", "sent", "spread", "turned", "cols_saved") as s:
        with nc.Block() as block:
            @block.vector
            def _(dve):
                step = Steps(dve, s.dve_step)
                step.add(nc.vector.tensor_scalar(k.logits[:, :], k.logits[:, :], k.neg_a[:, :], 0.0, ALU.subtract, ALU.min))
                step.wait()
                nc.vector.tensor_scalar(k.logits[:, :], k.logits[:, :], -103.0, None, ALU.max).then_inc(s.scored, 1)
                dve.wait_ge(s.exped, 1)
                step.add(nc.vector.tensor_scalar(k.route_arg[:, :], k.route_exp[:, :], -1.0, 1.0, ALU.mult, ALU.add))
                step.wait()
                nc.vector.tensor_tensor(k.route_arg[:, :], k.route_arg[:, :], k.route_exp[:, :], ALU.add).then_inc(s.weighted, 1)
                dve.wait_ge(s.turned, 1)
                nc.vector.tensor_copy(k.route_cols[:, :, :, :].rearrange("p a t r -> p (a t r)"), k.psum[0][:, 0:4 * 16]).then_inc(s.cols_saved, 1)
                dve.wait_ge(s.cols_saved, 1)
                dve.wait_ge(s.spread, 16)
                n = 0
                for b in range(BATCH):
                    for t in range(SUB):
                        mine = k.route_cols[:, 0, t, b:b + 1]
                        i = SUB * b + t
                        if n >= 2:
                            dve.wait_ge(s.dve_step, step.n - 2)
                        step.add(nc.vector.tensor_scalar(w.compare[:, n % 2, :], w.scores_all[:, b, :], mine, 0.0, ALU.is_gt, ALU.add,
                                                         accum_out=k.rank[:, 0, i:i + 1]))
                        step.add(nc.vector.scalar_tensor_tensor(w.compare[:, 2 + n % 2, :], w.scores_all[:, b, :], mine, w.earlier[:, t, :],
                                                                ALU.is_equal, ALU.mult, accum_out=k.rank[:, 1, i:i + 1]))
                        n += 1
                step.wait()
                step.add(nc.vector.tensor_tensor(k.rank[:, 0, :], k.rank[:, 0, :], k.rank[:, 1, :], ALU.add))
                step.wait()
                selected = k.route_w[:, 0, :]
                step.add(nc.vector.tensor_scalar(selected, k.rank[:, 0, :], float(NQ), None, ALU.is_lt))
                step.add(nc.vector.tensor_scalar(k.route_w[:, 1, :], k.rank[:, 0, :], float(NQ), None, ALU.is_ge))
                step.wait()
                by_token = k.route_cols[:, 1, :, :].rearrange("p t r -> p r t")
                step.add(nc.vector.tensor_tensor(selected.rearrange("p (b t) -> p b t", t=SUB), selected.rearrange("p (b t) -> p b t", t=SUB),
                                                 by_token[:, 0:BATCH, :], ALU.mult))
                step.add(nc.vector.tensor_copy(k.route_w[:, 2, :].rearrange("p (b t) -> p b t", t=SUB), by_token[:, BATCH:2 * BATCH, :]))

            @block.scalar
            def _(act):
                act.wait_ge(s.scored, 1)
                nc.scalar.activation(k.route_exp[:, :], k.logits[:, :], ACT.Exp).then_inc(s.exped, 1)

            @block.sync
            def _(sp):
                sp.wait_ge(s.scored, 1)
                sp.dma_start(k.scratch, k.logits[0:BATCH, :]).then_inc(s.sent, 16)
                sp.wait_ge(s.sent, 16)
                sp.dma_start(w.scores_all[:, :, :].rearrange("p b n -> p (b n)"),
                             k.scratch.rearrange("b n -> (b n)").partition_broadcast(P)).then_inc(s.spread, 16)

            @block.tensor
            def _(pe):
                pe.wait_ge(s.scored, 1)
                for t in range(SUB):
                    nc.tensor.transpose(k.psum[0][:, 16 * t:16 * (t + 1)], k.logits[:, P * t:P * (t + 1)], k.ident[0:16, 0:16])
                pe.wait_ge(s.weighted, 1)
                for t in range(SUB):
                    last = nc.tensor.transpose(k.psum[0][:, 16 * (SUB + t):16 * (SUB + t + 1)], k.route_arg[:, P * t:P * (t + 1)],
                                               k.ident[0:16, 0:16])
                last.then_inc(s.turned, 1)



def taylor_jobs():
    before, at = [], [[] for _ in range(SEQS * HEADS + 6)]
    for q in range(SEQS):
        g = HEADS * q
        first = [("query", q, 0), ("keys", q, 0), ("enc_keys", q, 0)]
        values = [("values", q, 0), ("values", q, 2), ("enc_values", q, 0)]
        if q == 0:
            before += first
            at[0] += values[:2]
            at[1] += values[2:]
        else:
            for i, job in enumerate(first + values):
                at[g - 8 + i].append(job)
        for i, job in enumerate([("values", q, 1), ("values", q, 3), ("enc_values", q, 1)]):
            at[g + 4 + i].append(job)
        at[g + HEADS + 4].append(("output", q, 0))
        at[g + HEADS + 5].append(("output_turned", q, 0))
    return before, at


def taylor_attention_stage(nc, k, b, w):
    LAG = 2
    ABUF = 3
    AHEAD = 3
    SB, EB, OB, JB = (0, 1), (2, 3), (4, 5), (6, 7)
    WIDE = SEQ + P
    N = SEQS * HEADS
    before, at = taylor_jobs()
    order = before + [job for jobs in at for job in jobs]
    number = {job: i for i, job in enumerate(order)}
    steps = range(N + 6)

    def job_bank(job):
        return k.psum[JB[number[job] % 2]]

    def saver(job):
        return "dve" if job[0] in ("keys", "enc_keys", "output_turned") else "act"

    def saved_count(job):
        return sum(saver(j) == saver(job) for j in order[:number[job] + 1])

    with signals(nc, "x_copied", "job_made", "act_saved_job", "dve_saved_job", "head_query", "scores_ready", "squared", "kernel_ready",
                 "sum_begun", "kernel_summed", "weighed", "dve_step", "out_saved") as s:

        def wait_saved(engine, job):
            engine.wait_ge(s.act_saved_job if saver(job) == "act" else s.dve_saved_job, saved_count(job))

        def wait_made(engine, job):
            engine.wait_ge(s.job_made, number[job] + 1)

        with nc.Block() as block:
            @block.gpsimd
            def _(pool):
                def copy_input(q):
                    if q >= 2:
                        wait_made(pool, ("enc_values", q - 2, 1))
                    nc.gpsimd.tensor_copy(k.xb[:, q % 2, 0, :], k.xnT[:, bass.ds((b * SEQS + q) * SEQ, SEQ)]).then_inc(s.x_copied, 1)

                def lay_query(g):
                    q, h = g // HEADS, g % HEADS
                    if h == 0:
                        wait_saved(pool, ("query", q, 0))
                    if q:
                        pool.wait_ge(s.scores_ready, g - HEADS + 1)
                    nc.gpsimd.tensor_scalar(k.keys[:, h, :], k.queryT[:, 2 * (q % 2) + h // 8, :], k.head16[:, h % 8:h % 8 + 1], None, ALU.mult)\
                        .then_inc(s.head_query, 1)

                def sum_kernel(g):
                    pool.wait_ge(s.kernel_ready, 2 * (g + 1))
                    if g >= ABUF:
                        pool.wait_ge(s.weighed, g - ABUF + 1)
                    A, total = w.kernel[:, g % ABUF, :], w.kernel_sum[:, g % ABUF, :]
                    nc.gpsimd.tensor_tensor(total, A[:, 0:SEQ], w.kernel_enc[:, g % ABUF, :], ALU.add).then_inc(s.sum_begun, 1)
                    pool.wait_ge(s.sum_begun, g + 1)
                    nc.gpsimd.tensor_tensor(total[:, P:SEQ], total[:, P:SEQ], A[:, SEQ:WIDE], ALU.add).then_inc(s.kernel_summed, 1)

                copy_input(0)
                copy_input(1)
                for g in range(N + AHEAD):
                    if g % HEADS == 2 and 2 <= g // HEADS + 1 < SEQS:
                        copy_input(g // HEADS + 1)
                    if g < N:
                        lay_query(g)
                    if g >= AHEAD:
                        sum_kernel(g - AHEAD)

            @block.tensor
            def _(pe):
                def do(job):
                    what, q, i = job
                    n = number[job]
                    if n >= 2:
                        wait_saved(pe, order[n - 2])
                    jb, xb = job_bank(job), k.xb[:, q % 2, 0, :]
                    if n == 0 or what == "query":
                        pe.wait_ge(s.x_copied, q + 1)
                    if what in ("query", "keys"):
                        weight = w.w_q if what == "query" else w.w_k
                        for j in range(2):
                            last = nc.tensor.matmul(jb[:, SEQ * j:SEQ * (j + 1)], weight[:, P * j:P * (j + 1)], xb, start=True, stop=True)
                    elif what == "enc_keys":
                        for j in range(2):
                            last = nc.tensor.matmul(jb[:, L1_ENC * j:L1_ENC * (j + 1)], w.w_k_enc[:, P * j:P * (j + 1)], xb[:, 0:L1_ENC],
                                                    start=True, stop=True)
                    elif what == "values":
                        t, half = i // 2, i % 2
                        last = nc.tensor.matmul(jb[:, :], xb[:, P * t:P * (t + 1)], w.w_v[:, CHUNK * half:CHUNK * (half + 1)],
                                                start=True, stop=True)
                    elif what == "enc_values":
                        last = nc.tensor.matmul(jb[0:L1_ENC, :], xb[:, 0:L1_ENC], w.w_v_enc[:, CHUNK * i:CHUNK * (i + 1)],
                                                start=True, stop=True)
                    elif what == "output":
                        pe.wait_ge(s.out_saved, PAIRS * (q + 1))
                        for o in range(PAIRS):
                            last = nc.tensor.matmul(jb[:, 0:SEQ], w.w_out[:, o, :], k.outT[:, q % 2, o, :], start=(o == 0), stop=(o == PAIRS - 1))
                    else:
                        wait_saved(pe, ("output", q, 0))
                        for t in range(SUB):
                            last = nc.tensor.transpose(jb[:, P * t:P * (t + 1)], k.yT[:, q % 2, P * t:P * (t + 1)], k.ident[:, :])
                    last.then_inc(s.job_made, 1)

                def scores(g):
                    q, h = g // HEADS, g % HEADS
                    if h == 0:
                        wait_saved(pe, ("enc_keys", q, 0))
                    pe.wait_ge(s.head_query, g + 1)
                    if g >= 2:
                        pe.wait_ge(s.squared, 2 * (g - 1))
                    c, query = h // 8, k.keys[:, h, :]
                    sb = k.psum[SB[g % 2]]
                    nc.tensor.matmul(sb[:, 0:SEQ], w.kT[:, q % 2, c, 0:P], query, start=True, stop=True)
                    nc.tensor.matmul(sb[:, SEQ:WIDE], w.kT[:, q % 2, c, P:2 * P], query[:, P:2 * P], start=True, stop=True)
                    nc.tensor.matmul(k.psum[EB[g % 2]][0:L1_ENC, 0:SEQ], w.k_encT[:, q % 2, c, :], query, start=True, stop=True)\
                        .then_inc(s.scores_ready, 1)

                def weigh(g):
                    q, h = g // HEADS, g % HEADS
                    if h % 8 == 0:
                        wait_saved(pe, ("enc_values", q, h // 8))
                    pe.wait_ge(s.kernel_ready, 2 * (g + 1))
                    o = g // 2
                    if o >= 2 and h % 2 == 0:
                        pe.wait_ge(s.out_saved, o - 1)
                    rows, cols = slice(HD * (h % 2), HD * (h % 2 + 1)), slice(HD * h, HD * (h + 1))
                    ob = k.psum[OB[o % 2]]
                    A, E = w.kernel[:, g % ABUF, :], w.kernel_enc[:, g % ABUF, :]
                    nc.tensor.matmul(ob[rows, 0:SEQ], k.values[:, q % 2, 0, cols], A[:, 0:SEQ], start=True, stop=False)
                    nc.tensor.matmul(ob[rows, P:SEQ], k.values[:, q % 2, 1, cols], A[:, SEQ:WIDE], start=False, stop=False)
                    nc.tensor.matmul(ob[rows, 0:SEQ], w.v_enc[:, q % 2, cols], E, start=False, stop=True)
                    pe.wait_ge(s.kernel_summed, g + 1)
                    nc.tensor.matmul(ob[rows, SEQ:2 * SEQ], w.ones[:, :], w.kernel_sum[:, g % ABUF, :], start=True, stop=True)\
                        .then_inc(s.weighed, 1)

                for job in before:
                    do(job)
                for g in steps:
                    if g < N:
                        scores(g)
                    for job in at[g]:
                        do(job)
                    if 0 <= g - LAG < N:
                        weigh(g - LAG)

            @block.scalar
            def _(act):
                def do(job):
                    what, q, i = job
                    if saver(job) != "act":
                        return
                    wait_made(act, job)
                    jb = job_bank(job)
                    if what == "query":
                        dst, src = k.queryT[:, 2 * (q % 2):2 * (q % 2) + 2, :].rearrange("p c n -> p (c n)"), jb[:, :]
                    elif what == "values":
                        dst, src = k.values[:, q % 2, i // 2, CHUNK * (i % 2):CHUNK * (i % 2 + 1)], jb[:, :]
                    elif what == "enc_values":
                        dst, src = w.v_enc[0:L1_ENC, q % 2, CHUNK * i:CHUNK * (i + 1)], jb[0:L1_ENC, :]
                    else:
                        dst, src = k.yT[:, q % 2, :], jb[:, 0:SEQ]
                    nc.scalar.activation(dst, src, ACT.Copy).then_inc(s.act_saved_job, 1)

                for job in before:
                    do(job)
                for g in steps:
                    if g < N:
                        act.wait_ge(s.scores_ready, g + 1)
                        if g >= ABUF:
                            act.wait_ge(s.weighed, g - ABUF + 1)
                        nc.scalar.activation(w.kernel[:, g % ABUF, :], k.psum[SB[g % 2]][:, 0:WIDE], ACT.Square, scale=0.25, bias=1.0)\
                            .then_inc(s.squared, 1)
                        nc.scalar.activation(w.kernel_enc[0:L1_ENC, g % ABUF, :], k.psum[EB[g % 2]][0:L1_ENC, 0:SEQ], ACT.Square, scale=0.25,
                                             bias=1.0).then_inc(s.squared, 1)
                    for job in at[g]:
                        do(job)

            @block.vector
            def _(dve):
                step = Steps(dve, s.dve_step)

                def do(job):
                    what, q, _ = job
                    if saver(job) != "dve":
                        return
                    wait_made(dve, job)
                    jb = job_bank(job)
                    if what == "keys":
                        ins = nc.vector.tensor_copy(w.kT[:, q % 2, :, :].rearrange("p c n -> p (c n)"), jb[:, :])
                    elif what == "enc_keys":
                        ins = nc.vector.tensor_copy(w.k_encT[:, q % 2, :, :].rearrange("p c n -> p (c n)"), jb[:, 0:2 * L1_ENC])
                    else:
                        rows = k.x[:, bass.ds((b * SEQS + q) * SUB, SUB), :]
                        ins = nc.vector.tensor_tensor(rows, rows, jb[:, 0:SEQ].rearrange("p (t n) -> p t n", t=SUB), ALU.add)
                    ins.then_inc(s.dve_saved_job, 1)

                def divide(o):
                    dve.wait_ge(s.weighed, 2 * (o + 1))
                    ob = k.psum[OB[o % 2]]
                    step.add(nc.vector.tensor_scalar(w.norm[:, o % 2, :], ob[:, SEQ:2 * SEQ], 2 * L1_EPS, None, ALU.add))
                    step.wait()
                    step.add(nc.vector.reciprocal(w.norm[:, o % 2, :], w.norm[:, o % 2, :]))
                    step.wait()
                    nc.vector.tensor_tensor(k.outT[:, o // PAIRS % 2, o % PAIRS, :], ob[:, 0:SEQ], w.norm[:, o % 2, :], ALU.mult)\
                        .then_inc(s.out_saved, 1)

                for job in before:
                    do(job)
                for g in steps:
                    if g < N:
                        dve.wait_ge(s.squared, 2 * (g + 1))
                        A, E = w.kernel[:, g % ABUF, :], w.kernel_enc[0:L1_ENC, g % ABUF, :]
                        nc.vector.scalar_tensor_tensor(A, A, 1.0, w.causal[:, :], ALU.add, ALU.mult).then_inc(s.kernel_ready, 1)
                        nc.vector.tensor_scalar(E, E, 1.0, None, ALU.add).then_inc(s.kernel_ready, 1)
                    for job in at[g]:
                        do(job)
                    done = g - LAG - 1
                    if 0 <= done < N and done % 2:
                        divide(done // 2)



def gate_stage(nc, k, w_router, renormalise, zeros=(), picks=None):
    E = 8
    with signals(nc, "logits_made", "centred", "exped", "dve_step", "gated", "turned", "saved", "picks_made", "pool_step") as s:
        with nc.Block() as block:
            @block.gpsimd
            def _(pool):
                nc.gpsimd.memset(k.gate_split[:, :, :, :], 0.0).then_inc(s.pool_step, 1)
                for z in zeros:
                    nc.gpsimd.memset(z, 0.0)
                if picks is not None:
                    nc.gpsimd.tensor_copy(picks[0], picks[1])

            @block.tensor
            def _(pe):
                for t in range(TILES):
                    last = nc.tensor.matmul(k.psum[0][:, E * t:E * (t + 1)], k.xnT[:, P * t:P * (t + 1)], w_router, start=True, stop=True)
                last.then_inc(s.logits_made, 1)
                pe.wait_ge(s.gated, 1)
                for g in range(CHUNKS):
                    for j in range(CT):
                        last = nc.tensor.transpose(k.psum[1 + g][0:SPREAD_K, P * j:P * (j + 1)],
                                                   k.gate_split[:, CT * g + j, :, :].rearrange("p a e -> p (a e)"), k.ident[:, :])
                    last.then_inc(s.turned, 1)

            @block.scalar
            def _(act):
                act.wait_ge(s.centred, 1)
                nc.scalar.activation(k.gate[:, :, :], k.gate[:, :, :], ACT.Exp).then_inc(s.exped, 1)
                for g in range(CHUNKS):
                    act.wait_ge(s.turned, g + 1)
                    nc.scalar.activation(k.row_parts[:, CHUNK * g:CHUNK * (g + 1)], k.psum[1 + g][0:SPREAD_K, :], ACT.Copy).then_inc(s.saved, 1)

            @block.vector
            def _(dve):
                step = Steps(dve, s.dve_step)
                logits = k.psum[0][:, 0:E * TILES].rearrange("p (t e) -> p t e", e=E)
                per_tile = k.gate_sum[:, :].unsqueeze(2).to_broadcast([P, TILES, E])
                step.add(nc.vector.memset(k.gate_cmp[:, :, :, :], 0.0))
                dve.wait_ge(s.logits_made, 1)
                step.add(nc.vector.reduce_max(k.gate_sum[:, :], logits, AXX))
                step.wait()
                nc.vector.tensor_tensor(k.gate[:, :, :], logits, per_tile, ALU.subtract).then_inc(s.centred, 1)
                dve.wait_ge(s.exped, 1)
                step.add(nc.vector.reduce_sum(k.gate_sum[:, :], k.gate[:, :, :], AXX))
                step.wait()
                step.add(nc.vector.reciprocal(k.gate_sum[:, :], k.gate_sum[:, :]))
                step.wait()
                step.add(nc.vector.tensor_tensor(k.gate[:, :, :], k.gate[:, :, :], per_tile, ALU.mult))
                step.wait()
                for j in range(E):
                    rival = k.gate[:, :, j:j + 1]
                    if j > 0:
                        step.add(nc.vector.tensor_tensor(k.gate_cmp[:, j, :, 0:j], rival.to_broadcast([P, TILES, j]), k.gate[:, :, 0:j], ALU.is_gt))
                    if j < E - 1:
                        step.add(nc.vector.tensor_tensor(k.gate_cmp[:, j, :, j + 1:E], rival.to_broadcast([P, TILES, E - 1 - j]),
                                                         k.gate[:, :, j + 1:E], ALU.is_ge))
                step.wait()
                step.add(nc.vector.reduce_sum(k.gate_rank[:, :, :].rearrange("p t e -> p (t e)"),
                                              k.gate_cmp[:, :, :, :].rearrange("p j t e -> p (t e) j"), AXX))
                step.wait()
                last = nc.vector.scalar_tensor_tensor(k.gate[:, :, :], k.gate_rank[:, :, :], 2.0, k.gate[:, :, :], ALU.is_lt, ALU.mult)
                if renormalise:
                    step.add(last)
                    step.wait()
                    step.add(nc.vector.reduce_sum(k.gate_sum[:, :], k.gate[:, :, :], AXX))
                    step.wait()
                    step.add(nc.vector.reciprocal(k.gate_sum[:, :], k.gate_sum[:, :]))
                    step.wait()
                    last = nc.vector.tensor_tensor(k.gate[:, :, :], k.gate[:, :, :], per_tile, ALU.mult)
                step.add(last)
                step.wait()
                dve.wait_ge(s.pool_step, 1)
                for i in range(PARTS):
                    part = k.gate_split[:, :, i, 0:E]
                    step.add(nc.vector.tensor_copy(k.gate_rounded[:, :, :], k.gate[:, :, :]))
                    step.wait()
                    last = nc.vector.tensor_copy(part, k.gate_rounded[:, :, :])
                    if i < PARTS - 1:
                        step.add(nc.vector.tensor_tensor(k.gate[:, :, :], k.gate[:, :, :], k.gate_rounded[:, :, :], ALU.subtract))
                        step.wait()
                last.then_inc(s.gated, 1)


def finish_chunk_pe(nc, k, pe, s):
    pe.wait_ge(s.y_saved, 1)
    for j in range(CT):
        last = nc.tensor.transpose(k.psum[7][:, P * j:P * (j + 1)], k.y_chunk[:, P * j:P * (j + 1)], k.ident[:, :])
    last.then_inc(s.y_turned, 1)


def finish_chunk_dve(nc, k, dve, s, c):
    dve.wait_ge(s.y_turned, 1)
    rows = k.x[:, bass.ds(c * CT, CT), :]
    nc.vector.tensor_tensor(rows, rows, k.psum[7][:, :].rearrange("p (t n) -> p t n", t=CT), ALU.add).then_inc(s.x_added, 1)


def swiglu_experts_stage(nc, k, c, w):
    HB = 3
    with signals(nc, "up_ready", "silu_ready", "product_ready", "hidden_ready", "down_done", "y_made", "y_saved", "y_turned", "x_added") as s:
        with nc.Block() as block:
            @block.tensor
            def _(pe):
                xs, gs = k.xnT[:, bass.ds(c * CHUNK, CHUNK)], k.row_parts[:, bass.ds(c * CHUNK, CHUNK)]
                for i in range(L1_HC + 1):
                    if i < L1_HC:
                        if i >= 2:
                            pe.wait_ge(s.hidden_ready, i - 1)
                        cols = slice(P * i, P * (i + 1))
                        nc.tensor.matmul(k.psum[i % 2][:, :], w.w1[:, cols], xs, start=True, stop=True)
                        nc.tensor.matmul(k.psum[2 + i % 2][:, :], w.w3[:, cols], xs, start=True, stop=True)
                        nc.tensor.matmul(k.psum[4 + i % 2][:, :], w.expert_of[:, cols], gs, start=True, stop=True).then_inc(s.up_ready, 1)
                    if i >= 1:
                        pe.wait_ge(s.hidden_ready, i)
                        last = nc.tensor.matmul(k.psum[6][:, :], w.w2[:, i - 1, :], w.hidden[:, (i - 1) % HB, :], start=(i == 1),
                                                stop=(i == L1_HC))
                        last.then_inc(s.down_done, 1)
                finish_chunk_pe(nc, k, pe, s)

            @block.scalar
            def _(act):
                for i in range(L1_HC):
                    act.wait_ge(s.up_ready, i + 1)
                    if i >= 2:
                        act.wait_ge(s.product_ready, i - 1)
                    nc.scalar.activation(w.silu[:, i % 2, :], k.psum[i % 2][:, :], ACT.Silu).then_inc(s.silu_ready, 1)
                act.wait_ge(s.down_done, L1_HC)
                nc.scalar.activation(k.y_chunk[:, :], k.psum[6][:, :], ACT.Copy).then_inc(s.y_saved, 1)

            @block.vector
            def _(dve):
                for i in range(L1_HC):
                    dve.wait_ge(s.silu_ready, i + 1)
                    if i >= HB:
                        dve.wait_ge(s.down_done, i - HB + 1)
                    hid = w.hidden[:, i % HB, :]
                    nc.vector.tensor_tensor(hid, w.silu[:, i % 2, :], k.psum[2 + i % 2][:, :], ALU.mult).then_inc(s.product_ready, 1)
                    dve.wait_ge(s.product_ready, i + 1)
                    nc.vector.tensor_tensor(hid, hid, k.psum[4 + i % 2][:, :], ALU.mult).then_inc(s.hidden_ready, 1)
                finish_chunk_dve(nc, k, dve, s, c)


def relu_experts_stage(nc, k, c, w):
    HB, UB, STEPS = 3, 4, L2_E * L2_FC
    with signals(nc, "gate_made", "gate_saved", "up_ready", "hidden_ready", "down_done", "y_saved", "y_turned", "x_added") as s:
        with nc.Block() as block:
            @block.tensor
            def _(pe):
                xs, gs = k.xnT[:, bass.ds(c * CHUNK, CHUNK)], k.row_parts[:, bass.ds(c * CHUNK, CHUNK)]

                def spread(e):
                    if e >= 2:
                        pe.wait_ge(s.gate_saved, e - 1)
                    nc.tensor.matmul(k.psum[4 + e % 2][:, :], k.pick_row[0:SPREAD_K, e:e + 1].to_broadcast([SPREAD_K, P]), gs, start=True, stop=True)\
                        .then_inc(s.gate_made, 1)

                spread(0)
                for i in range(STEPS + 2):
                    if i < STEPS:
                        if i % L2_FC == 0 and i // L2_FC + 1 < L2_E:
                            spread(i // L2_FC + 1)
                        if i >= UB:
                            pe.wait_ge(s.hidden_ready, i - UB + 1)
                        nc.tensor.matmul(k.psum[i % UB][:, :], w.w1[:, P * i:P * (i + 1)], xs, start=True, stop=True).then_inc(s.up_ready, 1)
                    if i >= 2:
                        j = i - 2
                        pe.wait_ge(s.hidden_ready, j + 1)
                        nc.tensor.matmul(k.psum[6][:, :], w.w2[:, j, :], w.hidden[:, j % HB, :], start=(j == 0), stop=(j == STEPS - 1))\
                            .then_inc(s.down_done, 1)
                finish_chunk_pe(nc, k, pe, s)

            @block.scalar
            def _(act):
                for e in range(L2_E):
                    act.wait_ge(s.gate_made, e + 1)
                    if e >= 2:
                        act.wait_ge(s.hidden_ready, L2_FC * (e - 1))
                    nc.scalar.activation(w.gate_all[:, e % 2, :], k.psum[4 + e % 2][:, :], ACT.Copy).then_inc(s.gate_saved, 1)
                act.wait_ge(s.down_done, STEPS)
                nc.scalar.activation(k.y_chunk[:, :], k.psum[6][:, :], ACT.Copy).then_inc(s.y_saved, 1)

            @block.vector
            def _(dve):
                for i in range(STEPS):
                    dve.wait_ge(s.up_ready, i + 1)
                    dve.wait_ge(s.gate_saved, i // L2_FC + 1)
                    if i >= HB:
                        dve.wait_ge(s.down_done, i - HB + 1)
                    nc.vector.scalar_tensor_tensor(w.hidden[:, i % HB, :], k.psum[i % UB][:, :], 0.0, w.gate_all[:, i // L2_FC % 2, :],
                                                   ALU.max, ALU.mult).then_inc(s.hidden_ready, 1)
                finish_chunk_dve(nc, k, dve, s, c)



HALF = TOKENS // 2
HALF_SEQS = HALF // SEQ


def ssm_prepare_stage(nc, k, w):
    with signals(nc, "cleared", "in_made", "in_saved", "x_saved", "conv_made", "ssm_ready", "proj_made", "proj_saved", "dt_made", "dt_biased",
                 "dt_folded", "dt_exped", "dt_logged", "decay_exped", "dve_step", "parts_cut", "rest_left", "conv_step", "lora_made", "linear_made", "linear_turned",
                 "linear_saved") as s:
        rest = w.padded[:, :, :, :].rearrange("p m b n -> p (m b n)")[0:SPREAD_K, 0:TOKENS]
        second, third = slice(PART_ROWS, 2 * PART_ROWS), slice(2 * PART_ROWS, SPREAD_K)
        with nc.Block() as block:
            @block.gpsimd
            def _(pool):
                nc.gpsimd.memset(w.padded[:, :, :, 0:L3_CONV - 1], 0.0).then_inc(s.cleared, 1)
                nc.gpsimd.memset(w.projT[:, :], 0.0).then_inc(s.cleared, 1)
                nc.gpsimd.memset(w.decay[:, :, :, 0:1], 0.0).then_inc(s.cleared, 1)

            @block.tensor
            def _(pe):
                n = 0
                for m in range(2 * L3_DC):
                    for g in range(CHUNKS):
                        if n >= 4:
                            pe.wait_ge(s.in_saved, n - 3)
                        nc.tensor.matmul(k.psum[n % 4][:, :], w.w_in[:, P * m:P * (m + 1)], k.xnT[:, CHUNK * g:CHUNK * (g + 1)],
                                         start=True, stop=True).then_inc(s.in_made, 1)
                        n += 1
                for l in range(L3_LIN):
                    last = nc.tensor.matmul(k.psum[4 + l // 4][:, P * (l % 4):P * (l % 4 + 1)], w.lora_b[:, l, :], w.lora_a[:, l, :],
                                            start=True, stop=True)
                last.then_inc(s.lora_made, 1)
                pe.wait_ge(s.linear_made, 2)
                for l in range(L3_LIN):
                    last = nc.tensor.transpose(k.psum[6 + l // 4][:, P * (l % 4):P * (l % 4 + 1)], w.linear[:, l, :], k.ident[:, :])
                last.then_inc(s.linear_turned, 1)
                pe.wait_ge(s.ssm_ready, L3_DC)
                pe.wait_ge(s.linear_saved, 2)
                for g in range(CHUNKS):
                    for m in range(L3_DC):
                        last = nc.tensor.matmul(k.psum[g][0:SPREAD_K + 1, :], w.w_x[:, m, :], w.xs[:, m, CHUNK * g:CHUNK * (g + 1)],
                                                start=(m == 0), stop=(m == L3_DC - 1))
                    last.then_inc(s.proj_made, 1)
                pe.wait_ge(s.proj_saved, CHUNKS)
                for m in range(L3_DC):
                    if m == 1:
                        pe.wait_ge(s.parts_cut, CHUNKS)
                    for g in range(CHUNKS):
                        last = nc.tensor.matmul(k.psum[4 * (1 - m) + g][:, :], w.w_dt[:, m, :], w.projT[:, CHUNK * g:CHUNK * (g + 1)], start=True, stop=True)
                    last.then_inc(s.dt_made, 1)

            @block.scalar
            def _(act):
                n = 0
                for m in range(2 * L3_DC):
                    for g in range(CHUNKS):
                        act.wait_ge(s.in_made, n + 1)
                        seqs = slice(2 * g, 2 * g + 2)
                        if m < L3_DC:
                            last = nc.scalar.activation(w.padded[:, m, seqs, L3_CONV - 1:], k.psum[n % 4][:, :].rearrange("p (b n) -> p b n", b=2), ACT.Copy)
                        else:
                            last = nc.scalar.activation(w.z[:, m - L3_DC, CHUNK * g:CHUNK * (g + 1)], k.psum[n % 4][:, :], ACT.Silu)
                        last.then_inc(s.in_saved, 1)
                        n += 1
                for m in range(L3_DC):
                    act.wait_ge(s.conv_made, m + 1)
                    nc.scalar.activation(w.xs[:, m, :], w.xs[:, m, :], ACT.Silu, bias=w.conv_b[:, m:m + 1]).then_inc(s.ssm_ready, 1)
                act.wait_ge(s.linear_turned, 1)
                for i in range(2):
                    width = (4, 2)[i]
                    nc.scalar.activation(w.linearT[:, 4 * i:4 * i + width, :].rearrange("p l n -> p (l n)"), k.psum[6 + i][:, 0:P * width], ACT.Copy)\
                        .then_inc(s.linear_saved, 1)
                act.wait_ge(s.cleared, 2)
                for g in range(CHUNKS):
                    act.wait_ge(s.proj_made, g + 1)
                    nc.scalar.activation(w.projT[0:SPREAD_K + 1, CHUNK * g:CHUNK * (g + 1)], k.psum[g][0:SPREAD_K + 1, :], ACT.Copy)\
                        .then_inc(s.proj_saved, 1)
                    nc.scalar.activation(k.row_parts[:, CHUNK * g:CHUNK * (g + 1)], k.psum[g][0:SPREAD_K, :], ACT.Copy).then_inc(s.parts_cut, 1)
                act.wait_ge(s.rest_left, 1)
                for part in (second, third):
                    nc.scalar.activation(k.row_parts[part, :], rest[part, :], ACT.Copy).then_inc(s.parts_cut, 1)
                nc.scalar.preload_act_table_set("natural_log_exp_and_others")
                nc.scalar.activation(w.a_neg[:, :, :], w.a_neg[:, :, :], ACT.Exp).then_inc(s.decay_exped, 1)
                for m in range(L3_DC):
                    act.wait_ge(s.dt_folded, m + 1)
                    nc.scalar.activation(w.xdt[:, m, :], w.xdt[:, m, :], ACT.Exp).then_inc(s.dt_exped, 1)
                for m in range(L3_DC):
                    act.wait_ge(s.dt_exped, m + 1)
                    nc.scalar.activation(w.xdt[:, m, :], w.xdt[:, m, :], ACT.Ln, bias=1.0).then_inc(s.dt_logged, 1)

            @block.vector
            def _(dve):
                step, conv = Steps(dve, s.dve_step), Steps(dve, s.conv_step)
                step.add(nc.vector.tensor_scalar(w.linear[:, :, :], w.codes[:, :, :], 1.0 / 7.5, -1.0, ALU.mult, ALU.add))
                step.wait()
                grouped = w.linear[:, :, :].rearrange("p l (g n) -> p (l g) n", n=L3_GROUP)
                step.add(nc.vector.tensor_tensor(grouped, grouped, w.scales[:, :].unsqueeze(2).to_broadcast([P, L3_LIN * P // L3_GROUP, L3_GROUP]),
                                                 ALU.mult))
                step.wait()
                dve.wait_ge(s.lora_made, 1)
                for i in range(2):
                    width = (4, 2)[i]
                    part = w.linear[:, 4 * i:4 * i + width, :].rearrange("p l n -> p (l n)")
                    nc.vector.tensor_tensor(part, part, k.psum[4 + i][:, 0:P * width], ALU.add).then_inc(s.linear_made, 1)
                dve.wait_ge(s.cleared, 3)
                for m in range(L3_DC):
                    dve.wait_ge(s.in_saved, CHUNKS * (m + 1))
                    out = w.xs[:, m, :].rearrange("p (b n) -> p b n", b=BATCH)
                    conv.add(nc.vector.tensor_scalar(out, w.padded[:, m, :, 0:SEQ], w.conv_w[:, m, 0:1], None, ALU.mult))
                    for j in range(1, L3_CONV):
                        conv.wait()
                        last = nc.vector.scalar_tensor_tensor(out, w.padded[:, m, :, j:j + SEQ], w.conv_w[:, m, j:j + 1], out, ALU.mult, ALU.add)
                        if j < L3_CONV - 1:
                            conv.add(last)
                        else:
                            last.then_inc(s.conv_made, 1)
                dve.wait_ge(s.parts_cut, CHUNKS)
                nc.vector.tensor_tensor(rest, w.projT[0:SPREAD_K, :], k.row_parts[:, :], ALU.subtract).then_inc(s.rest_left, 1)
                for m in range(L3_DC):
                    dve.wait_ge(s.dt_made, m + 1)
                    nc.vector.tensor_scalar(w.dt[:, m, :], k.psum_all[:, 4 * CHUNK * (1 - m):4 * CHUNK * (2 - m)], w.b_dt[:, m:m + 1], None, ALU.add)\
                        .then_inc(s.dt_biased, 1)
                    dve.wait_ge(s.dt_biased, m + 1)
                    nc.vector.scalar_tensor_tensor(w.xdt[:, m, :], w.dt[:, m, :], -1.0, w.dt[:, m, :], ALU.mult, ALU.min).then_inc(s.dt_folded, 1)
                dve.wait_ge(s.parts_cut, CHUNKS + 2)
                nc.vector.tensor_tensor(k.row_parts[third, :], rest[third, :], k.row_parts[third, :], ALU.subtract)
                dve.wait_ge(s.decay_exped, 1)
                step.add(nc.vector.tensor_scalar(w.a_neg[:, :, :], w.a_neg[:, :, :], -1.0, None, ALU.mult))
                for m in range(L3_DC):
                    dve.wait_ge(s.dt_logged, m + 1)
                    step.add(nc.vector.scalar_tensor_tensor(w.dt[:, m, :], w.dt[:, m, :], 0.0, w.xdt[:, m, :], ALU.max, ALU.add))
                    step.wait()
                    step.add(nc.vector.tensor_tensor(w.xdt[:, m, :], w.dt[:, m, :], w.xs[:, m, :], ALU.mult))


def ssm_scan_stage(nc, k, hf, w):
    UNITS = L3_N * L3_DC
    BUF = 3
    with signals(nc, "b_spread", "c_spread", "c_saved", "decay_ready", "input_ready", "scanned", "weighted", "summed", "dve_step", "y_ready",
                 "out_made", "y_saved", "y_turned", "x_added") as s:
        with nc.Block() as block:
            @block.tensor
            def _(pe):
                def spread(n):
                    if n >= 1:
                        pe.wait_ge(s.input_ready, L3_DC * n)
                    for j in range(2):
                        last = nc.tensor.matmul(k.psum[j][:, :], k.pick_row[0:SPREAD_K, n:n + 1].to_broadcast([SPREAD_K, P]),
                                                k.row_parts[:, bass.ds(hf * HALF + CHUNK * j, CHUNK)], start=True, stop=True)
                    last.then_inc(s.b_spread, 1)
                    if n >= 1:
                        pe.wait_ge(s.c_saved, n)
                    for j in range(2):
                        last = nc.tensor.matmul(k.psum[2 + j][:, :], k.pick_row[0:SPREAD_K, L3_N + n:L3_N + n + 1].to_broadcast([SPREAD_K, P]),
                                                k.row_parts[:, bass.ds(hf * HALF + CHUNK * j, CHUNK)], start=True, stop=True)
                    last.then_inc(s.c_spread, 1)

                def accumulate(u):
                    pe.wait_ge(s.weighted, u + 1)
                    n, m = u // L3_DC, u % L3_DC
                    for j in range(2):
                        last = nc.tensor.matmul(k.psum[4 + 2 * m + j][:, :], k.ident[:, :], w.weighted[:, u % BUF, CHUNK * j:CHUNK * (j + 1)],
                                                start=(n == 0), stop=(n == L3_N - 1))
                    last.then_inc(s.summed, 1)

                spread(0)
                for n in range(L3_N):
                    if n + 1 < L3_N:
                        spread(n + 1)
                    if n >= 1:
                        for m in range(L3_DC):
                            accumulate(L3_DC * (n - 1) + m)
                for m in range(L3_DC):
                    accumulate(L3_DC * (L3_N - 1) + m)
                pe.wait_ge(s.y_ready, L3_DC)
                for j in range(2):
                    for m in range(L3_DC):
                        last = nc.tensor.matmul(k.psum[j][:, :], w.w_out[:, m, :], w.gated[:, m, CHUNK * j:CHUNK * (j + 1)],
                                                start=(m == 0), stop=(m == L3_DC - 1))
                last.then_inc(s.out_made, 1)
                for j in range(2):
                    pe.wait_ge(s.y_saved, j + 1)
                    for t in range(CT):
                        last = nc.tensor.transpose(k.psum[2 + j][:, P * t:P * (t + 1)], w.out_T[:, j, P * t:P * (t + 1)], k.ident[:, :])
                    last.then_inc(s.y_turned, 1)

            @block.scalar
            def _(act):
                for n in range(L3_N):
                    for m in range(L3_DC):
                        u = L3_DC * n + m
                        if u >= BUF:
                            act.wait_ge(s.scanned, u - BUF + 1)
                        nc.scalar.activation(w.decay[:, u % BUF, :, 1:], w.dt[:, m, bass.ds(hf * HALF, HALF)].rearrange("p (b n) -> p b n", n=SEQ)[:, :, 1:],
                                             ACT.Exp, scale=w.a_neg[:, m, n:n + 1]).then_inc(s.decay_ready, 1)
                    act.wait_ge(s.c_spread, n + 1)
                    if n >= 2:
                        act.wait_ge(s.weighted, L3_DC * (n - 1))
                    nc.scalar.activation(w.c_all[:, n % 2, :], k.psum_all[:, 2 * CHUNK:4 * CHUNK], ACT.Copy).then_inc(s.c_saved, 1)
                act.wait_ge(s.out_made, 1)
                for j in range(2):
                    nc.scalar.activation(w.out_T[:, j, :], k.psum[j][:, :], ACT.Copy).then_inc(s.y_saved, 1)

            @block.gpsimd
            def _(pool):
                for u in range(UNITS):
                    pool.wait_ge(s.scanned, u + 1)
                    pool.wait_ge(s.c_saved, u // L3_DC + 1)
                    if u >= BUF:
                        pool.wait_ge(s.summed, u - BUF + 1)
                    nc.gpsimd.tensor_tensor(w.weighted[:, u % BUF, :], w.state[:, u % BUF, :], w.c_all[:, u // L3_DC % 2, :], ALU.mult)\
                        .then_inc(s.weighted, 1)

            @block.vector
            def _(dve):
                step = Steps(dve, s.dve_step)
                for u in range(UNITS):
                    n, m = u // L3_DC, u % L3_DC
                    if m == 0:
                        dve.wait_ge(s.b_spread, n + 1)
                    nc.vector.tensor_tensor(w.inflow[:, u % 2, :], w.xdt[:, m, bass.ds(hf * HALF, HALF)], k.psum_all[:, 0:HALF], ALU.mult)\
                        .then_inc(s.input_ready, 1)
                    dve.wait_ge(s.input_ready, u + 1)
                    dve.wait_ge(s.decay_ready, u + 1)
                    if u >= BUF:
                        dve.wait_ge(s.weighted, u - BUF + 1)
                    nc.vector.tensor_tensor_scan(w.state[:, u % BUF, :], w.decay[:, u % BUF, :, :].rearrange("p b n -> p (b n)"), w.inflow[:, u % 2, :],
                                                 0.0, ALU.mult, ALU.add).then_inc(s.scanned, 1)
                dve.wait_ge(s.summed, UNITS)
                for m in range(L3_DC):
                    step.add(nc.vector.scalar_tensor_tensor(w.gated[:, m, :], w.xs[:, m, bass.ds(hf * HALF, HALF)], w.d_skip[:, m:m + 1],
                                                            k.psum_all[:, CHUNK * (4 + 2 * m):CHUNK * (6 + 2 * m)], ALU.mult, ALU.add))
                    step.wait()
                    nc.vector.tensor_tensor(w.gated[:, m, :], w.gated[:, m, :], w.z[:, m, bass.ds(hf * HALF, HALF)], ALU.mult).then_inc(s.y_ready, 1)
                for j in range(2):
                    dve.wait_ge(s.y_turned, j + 1)
                    rows = k.x[:, bass.ds(hf * (HALF // P) + CT * j, CT), :]
                    nc.vector.tensor_tensor(rows, rows, k.psum[2 + j][:, :].rearrange("p (t n) -> p t n", t=CT), ALU.add).then_inc(s.x_added, 1)


def quantised_ffn_stage(nc, k, w):
    BLOCKS = L3_LIN // 2
    with signals(nc, "first_made", "first_biased", "dve_step", "moments_ready", "rstd_ready", "normed", "turned", "gelu_ready", "second_made",
                 "h_ready", "h_turned", "x_added") as s:
        with nc.Block() as block:
            @block.tensor
            def _(pe):
                n_turn = 0
                for blk in range(BLOCKS):
                    h = k.xnT if blk == 0 else w.hT
                    for g in range(CHUNKS):
                        if blk:
                            pe.wait_ge(s.h_ready, CHUNKS * (blk - 1) + g + 1)
                            pe.wait_ge(s.first_biased, CHUNKS * (blk - 1) + g + 1)
                        for j in range(CT):
                            c = CHUNK * g + P * j
                            last = nc.tensor.matmul(k.psum[g][:, P * j:P * (j + 1)], h[:, c:c + P], w.linearT[:, 2 * blk, :], start=True, stop=True)
                        last.then_inc(s.first_made, 1)
                    for g in range(CHUNKS):
                        pe.wait_ge(s.normed, TILES * blk + CT * (g + 1))
                        if n_turn >= 2:
                            pe.wait_ge(s.gelu_ready, n_turn - 1)
                        for j in range(CT):
                            last = nc.tensor.transpose(k.psum[4 + n_turn % 2][:, P * j:P * (j + 1)], w.y[:, CT * g + j, :], k.ident[:, :])
                        last.then_inc(s.turned, 1)
                        n_turn += 1
                        pe.wait_ge(s.gelu_ready, n_turn)
                        if n_turn > 2:
                            pe.wait_ge(s.h_ready, n_turn - 2)
                        nc.tensor.matmul(k.psum[6 + n_turn % 2][:, :], w.linearT[:, 2 * blk + 1, :], w.gelu[:, (n_turn - 1) % 2, :],
                                         start=True, stop=True).then_inc(s.second_made, 1)
                for g in range(CHUNKS):
                    pe.wait_ge(s.h_ready, CHUNKS * (BLOCKS - 1) + g + 1)
                    for j in range(CT):
                        c = CHUNK * g + P * j
                        last = nc.tensor.transpose(k.psum[g][:, P * j:P * (j + 1)], w.hT[:, c:c + P], k.ident[:, :])
                    last.then_inc(s.h_turned, 1)

            @block.scalar
            def _(act):
                n = 0
                for blk in range(BLOCKS):
                    act.wait_ge(s.moments_ready, blk + 1)
                    nc.scalar.activation(k.rstd[:, :], k.rstd[:, :], ACT.Sqrt).then_inc(s.rstd_ready, 1)
                    for g in range(CHUNKS):
                        act.wait_ge(s.turned, n + 1)
                        if n >= 2:
                            act.wait_ge(s.second_made, n - 1)
                        nc.scalar.activation(w.gelu[:, n % 2, :], k.psum[4 + n % 2][:, :], ACT.Gelu, scale=w.gamma[:, blk:blk + 1],
                                             bias=w.beta[:, blk:blk + 1]).then_inc(s.gelu_ready, 1)
                        n += 1

            @block.vector
            def _(dve):
                step = Steps(dve, s.dve_step)
                for blk in range(BLOCKS):
                    for g in range(CHUNKS):
                        dve.wait_ge(s.first_made, CHUNKS * blk + g + 1)
                        if blk:
                            dve.wait_ge(s.turned, CHUNKS * blk)
                        bias = w.bias_rows[:, blk, :].unsqueeze(1).to_broadcast([P, CT, P])
                        nc.vector.tensor_tensor(w.y[:, CT * g:CT * (g + 1), :], k.psum[g][:, :].rearrange("p (t n) -> p t n", t=CT), bias, ALU.add)\
                            .then_inc(s.first_biased, 1)
                    dve.wait_ge(s.first_biased, CHUNKS * (blk + 1))
                    for t in range(TILES):
                        step.add(nc.vector.bn_stats(k.stats[:, t, :], w.y[:, t, :]))
                    step.wait()
                    for t in range(TILES):
                        step.add(nc.vector.bn_aggr(k.moments[:, t, :], k.stats[:, t, :]))
                    step.wait()
                    step.add(nc.vector.tensor_scalar(k.rstd[:, :], k.moments[:, :, 1], LN_EPS, None, ALU.add))
                    step.wait()
                    nc.vector.reciprocal(k.rstd[:, :], k.rstd[:, :]).then_inc(s.moments_ready, 1)
                    dve.wait_ge(s.rstd_ready, blk + 1)
                    for t in range(TILES):
                        nc.vector.tensor_scalar(w.y[:, t, :], w.y[:, t, :], k.moments[:, t, 0:1], k.rstd[:, t:t + 1], ALU.subtract, ALU.mult)\
                            .then_inc(s.normed, 1)
                    for g in range(CHUNKS):
                        n = CHUNKS * blk + g
                        dve.wait_ge(s.second_made, n + 1)
                        if blk:
                            dve.wait_ge(s.h_ready, CHUNKS * (blk - 1) + g + 1)
                        before = (k.xnT if blk == 0 else w.hT)[:, CHUNK * g:CHUNK * (g + 1)]
                        nc.vector.scalar_tensor_tensor(w.hT[:, CHUNK * g:CHUNK * (g + 1)], k.psum[6 + (n + 1) % 2][:, :], w.bias_cols[:, blk:blk + 1],
                                                       before, ALU.add, ALU.add).then_inc(s.h_ready, 1)
                for g in range(CHUNKS):
                    dve.wait_ge(s.h_turned, g + 1)
                    rows = k.x[:, CT * g:CT * (g + 1), :]
                    nc.vector.tensor_tensor(rows, rows, k.psum[g][:, :].rearrange("p (t n) -> p t n", t=CT), ALU.add).then_inc(s.x_added, 1)


def layer3(nc, k, d):
    with ExitStack() as held:
        def sb(name, shape, dt=F32):
            return held.enter_context(nc.sbuf_tensor(name, shape, dt))
        w = Names(
            w_in=sb("w_in", [P, 4 * P]), conv_w=sb("conv_w", [P, L3_DC, L3_CONV]), conv_b=sb("conv_b", [P, L3_DC]),
            w_x=sb("w_x", [P, L3_DC, SPREAD_K + 1]), a_neg=sb("a_neg", [P, L3_DC, L3_N]), d_skip=sb("d_skip", [P, L3_DC]),
            w_dt=sb("w_dt", [P, L3_DC, P]), b_dt=sb("b_dt", [P, L3_DC]), w_out=sb("w_out3", [P, L3_DC, P]),
            codes=sb("codes", [P, L3_LIN, P], I32), scales=sb("scales", [P, L3_LIN * P // L3_GROUP]), linear=sb("linear", [P, L3_LIN, P]),
            linearT=sb("linearT", [P, L3_LIN, P]), lora_a=sb("lora_a", [L3_R, L3_LIN, P]), lora_b=sb("lora_b", [L3_R, L3_LIN, P]),
            gamma=sb("gamma", [P, 3]), beta=sb("beta", [P, 3]), bias_rows=sb("bias_rows", [P, 3, P]), bias_cols=sb("bias_cols", [P, 3]),
            xs=sb("xs", [P, L3_DC, TOKENS]), z=sb("z", [P, L3_DC, TOKENS]), dt=sb("dt", [P, L3_DC, TOKENS]), xdt=sb("xdt", [P, L3_DC, TOKENS]),
            projT=sb("projT", [P, TOKENS]), decay=sb("decay", [P, 3, HALF_SEQS, SEQ]))
        loads = [(w.w_in[:, :], d["w_in3"]), (w.conv_w[:, :, :], d["conv_w"]), (w.conv_b[:, :], d["conv_b"]), (w.w_x[:, :, :], d["w_x"]),
                 (w.a_neg[:, :, :], d["a_log"]), (w.d_skip[:, :], d["d_skip"]), (w.w_dt[:, :, :], d["w_dt"]), (w.b_dt[:, :], d["b_dt"]),
                 (w.w_out[:, :, :], d["w_out3"]), (w.codes[:, :, :], d["codes"]), (w.scales[:, :], d["scales"]), (w.lora_a[:, :, :], d["lora_a"]),
                 (w.lora_b[:, :, :], d["lora_b"]), (w.gamma[:, :], d["gamma"]), (w.beta[:, :], d["beta"]),
                 (w.bias_rows[:, :, :].rearrange("p l n -> p (l n)"), d["bias_rows"].partition_broadcast(P)), (w.bias_cols[:, :], d["bias_cols"])]
        layer_norm_stage(nc, k, loads)
        with nc.sbuf_tensor("padded", [P, L3_DC, BATCH, L3_CONV - 1 + SEQ], F32) as padded:
            w.padded = padded
            ssm_prepare_stage(nc, k, w)
        with ExitStack() as scan:
            def sc(name, shape):
                return scan.enter_context(nc.sbuf_tensor(name, shape, F32))
            w.c_all, w.weighted, w.state = sc("c_all", [P, 2, HALF]), sc("weighted", [P, 3, HALF]), sc("state", [P, 3, HALF])
            w.inflow = sc("inflow", [P, 2, HALF])
            w.gated, w.out_T = w.state, w.inflow[:, :, 0:CHUNK]
            with nc.Fori(0, 2) as hf:
                ssm_scan_stage(nc, k, hf, w)
        with ExitStack() as ffn:
            w.y = k.xn
            w.hT = ffn.enter_context(nc.sbuf_tensor("hT", [P, TOKENS], F32))
            w.gelu = ffn.enter_context(nc.sbuf_tensor("gelu", [P, 2, CHUNK], F32))
            quantised_ffn_stage(nc, k, w)



def layer0(nc, k, d):
    with ExitStack() as held:
        def sb(name, shape):
            return held.enter_context(nc.sbuf_tensor(name, shape, F32))
        w = Names(
            cols=sb("norm_cols", [P, 3]), inT=sb("in_T", [HD, 3, P]), fc=sb("fc", [HD, 3, HEADS * HD]), fused=sb("fused", [P, 3, HEADS * HD]),
            qbias=sb("qbias", [P, PAIRS]), kbias=sb("kbias", [P, PAIRS]), vbias=sb("vbias", [P, HEADS * HD]), obias=sb("obias", [P, 1]),
            wo=sb("wo", [P, PAIRS, P]), qkv_l=sb("qkv_l", [P, 3, 512]), qkv_h=sb("qkv_h", [P, 3, 512]), wo_l=sb("wo_l", [P, 4, P]),
            wo_h=sb("wo_h", [P, 4, P]), null_k=sb("null_k", [P, 4, 2]), null_v=sb("null_v", [P, 4, 8]), null_q=sb("null_q", [P, P]),
            route_tokens=sb("route_tokens", [P, BATCH, 16]), xlT=sb("xlT", [P, TOKENS]), xrT=sb("xrT", [P, TOKENS]),
            null_out=sb("null_out", [P, P]), earlier=k.gate_cmp[:, 0:4, :, :].rearrange("p j t e -> p (j t e)").rearrange("p (t n) -> p t n", t=SUB), compare=k.masked_scores[:, :, :, :].rearrange("p i t n -> p (i t) n"),
            scores_all=k.probs[:, :, :, :].rearrange("p i t n -> p (i t) n"))
        loads = [(w.cols[:, :], d["cols"]), (w.inT[:, :, :], d["inT"]), (w.fc[:, :, :], d["fc"]), (w.qbias[:, :], d["qbias"]),
                 (w.kbias[:, :], d["kbias"]), (w.vbias[:, :], d["vbias"].partition_broadcast(P)), (w.obias[:, :], d["obias0"]),
                 (w.wo[:, :, :], d["wo0"]), (w.qkv_l[:, :, :], d["qkv_l"]), (w.qkv_h[:, :, :], d["qkv_h"]), (w.wo_l[:, :, :], d["wo_l"]),
                 (w.wo_h[:, :, :], d["wo_h"]), (w.null_k[:, :, :], d["null_k"]), (w.null_v[:, :, :], d["null_v"]),
                 (w.null_q[:, :], d["null_q"].partition_broadcast(P)), (w.route_tokens[:, :, :], d["route_tokens"]), (k.logk[:, :], d["logk"]),
                 (k.window_mask[:, :, :], d["window_mask"]), (w.earlier[:, :, :], d["earlier"]), (k.head16[:, :], d["head16"]),
                 (k.head8[:, :], d["head8"]), (k.rot_cos[:, :, :], d["rot_cos"]), (k.rot_sin[:, :, :], d["rot_sin"])]
        layer_norm_stage(nc, k, loads, first=d["x"])
        layer0_prepare_stage(nc, k, w)
        main = Names(
            kind="l0", w=w, wq=lambda p: w.fused[:, 0, P * p:P * (p + 1)], wk=lambda p: w.fused[:, 1, P * p:P * (p + 1)],
            wv=lambda half: w.fused[:, 2, CHUNK * half:CHUNK * (half + 1)], qbias=lambda p: w.qbias[:, p:p + 1],
            query=lambda q, h, t: k.queryT[:, h // 2, P * t:P * (t + 1)], value=lambda q, h, kt: k.values[:, q % 2, kt, HD * h:HD * (h + 1)],
            wo=lambda o: w.wo[:, o, :], obias=w.obias[:, 0:1])
        with nc.Fori(0, BATCH // SEQS) as b:
            softmax_attention_stage(nc, k, b, main)
        route_stage(nc, k, w)

        def of(p, i):
            return (w.qkv_l if p < 4 else w.qkv_h)[:, i, P * (p % 4):P * (p % 4 + 1)]
        routed = Names(
            kind="l0ffn", w=w, wq=lambda p: of(p, 0), wk=lambda p: of(p, 1), wv=lambda half: (w.qkv_h if half else w.qkv_l)[:, 2, :],
            qbias=lambda p: 0.0, query=main.query, value=main.value, wo=lambda o: (w.wo_l if o < 4 else w.wo_h)[:, o % 4, :])
        with nc.Fori(0, BATCH // SEQS) as b:
            softmax_attention_stage(nc, k, b, routed)


def layer1(nc, k, d):
    with ExitStack() as held:
        def sb(name, shape):
            return held.enter_context(nc.sbuf_tensor(name, shape, F32))
        w = Names(
            w_q=sb("w_q", [P, 256]), w_k=sb("w_k", [P, 256]), w_k_enc=sb("w_k_enc", [P, 256]), w_v=sb("w_v", [P, 1024]),
            w_v_enc=sb("w_v_enc", [P, 1024]), w_out=sb("w_out", [P, PAIRS, P]), router=sb("router1", [P, L1_E]),
            w1=sb("w1", [P, L1_E * L1_H]), w3=sb("w3", [P, L1_E * L1_H]), w2=sb("w2", [P, L1_HC, P]),
            expert_of=held.enter_context(nc.sbuf_tensor("expert_of", [SPREAD_K, L1_E * L1_H], BF16)), causal=sb("causal", [P, SEQ + P]), ones=sb("ones", [P, HD]),
            kT=sb("kT", [P, 2, 2, SEQ]), k_encT=sb("k_encT", [P, 2, 2, L1_ENC]), v_enc=sb("v_enc", [P, 2, 1024]),
            kernel_sum=sb("kernel_sum", [P, 3, SEQ]), kernel=sb("kernel", [P, 3, SEQ + P]),
            kernel_enc=sb("kernel_enc", [P, 3, SEQ]), norm=sb("norm", [P, 2, SEQ]), silu=k.masked_scores[:, :, :, :].rearrange("p i t n -> p i (t n)"),
            hidden=k.queryT[:, 0:6, :].rearrange("p (i a) n -> p i (a n)", i=3))
        expert_of = k.probs[:, :, :, :].rearrange("p i t n -> p (i t n)")[0:SPREAD_K, 0:L1_E * L1_H]
        loads = [(dst, d[name]) for dst, name in (
            (w.w_q[:, :], "w_q1"), (w.w_k[:, :], "w_k1"), (w.w_k_enc[:, :], "w_k_enc1"), (w.w_v[:, :], "w_v1"), (w.w_v_enc[:, :], "w_v_enc1"),
            (w.w_out[:, :, :], "w_out1"), (w.router[:, :], "router1"), (w.w1[:, :], "w1_1"), (w.w3[:, :], "w3_1"), (w.w2[:, :, :], "w2_1"),
            (expert_of, "expert_of"), (w.causal[:, :], "causal"), (w.ones[:, :], "ones"))]
        layer_norm_stage(nc, k, loads)
        gate_stage(nc, k, w.router[:, :], False, zeros=(w.v_enc[:, :, :], w.kernel_enc[:, :, :]), picks=(w.expert_of[:, :], expert_of))
        with nc.Fori(0, BATCH // SEQS) as b:
            taylor_attention_stage(nc, k, b, w)
        with nc.Fori(0, CHUNKS) as c:
            swiglu_experts_stage(nc, k, c, w)


def layer2(nc, k, d):
    with ExitStack() as held:
        def sb(name, shape):
            return held.enter_context(nc.sbuf_tensor(name, shape, F32))
        w = Names(
            w_rot=sb("w_rot", [P, 4, P]), w_v=sb("w_v2", [P, P]), wo=sb("wo2", [P, 4, P]), obias=sb("obias2", [P, 1]),
            router=sb("router2", [P, L2_E]), w1=sb("w1_2", [P, L2_E * L2_F]), w2=sb("w2_2", [P, L2_E * L2_FC, P]),
            padded_values=sb("padded_values", [P, 2, SUB, HEADS, 32]), hidden=sb("hidden2", [P, 3, CHUNK]), gate_all=sb("gate_all", [P, 2, CHUNK]))
        pick_row = k.probs[:, 0, 0, 0:PART_ROWS]
        loads = [(pick_row, d["pick_row"]), (w.w_rot[:, :, :], d["w_rot"]), (w.w_v[:, :], d["w_v2"]), (w.wo[:, :, :], d["wo2"]), (w.obias[:, :], d["obias2"]),
                 (w.router[:, :], d["router2"]), (w.w1[:, :], d["w1_2"]), (w.w2[:, :, :], d["w2_2"])]
        layer_norm_stage(nc, k, loads)
        gate_stage(nc, k, w.router[:, :], True, zeros=(w.padded_values[:, :, :, :, :],), picks=(k.pick_row[:, :], pick_row))
        narrow = Names(
            kind="l2", w=w, query=lambda q, h, t: k.rot[:, q % 2, 0, P * t:P * (t + 1)], value=lambda q, h, kt: w.padded_values[:, q % 2, kt, h, :],
            wo=lambda o: w.wo[:, o, :], obias=w.obias[:, 0:1])
        with nc.Fori(0, BATCH // SEQS) as b:
            softmax_attention_stage(nc, k, b, narrow)
        with nc.Fori(0, CHUNKS) as c:
            relu_experts_stage(nc, k, c, w)


def store_stage(nc, k, out):
    with signals(nc, "stored") as s:
        with nc.Block() as block:
            @block.sync
            def _(sp):
                sp.dma_start(out, k.x[:, :, :]).then_inc(s.stored, 16)
                sp.wait_ge(s.stored, 16)


def build(nc, d, out, layers=4):
    with ExitStack() as held:
        def sb(name, shape, dt=F32):
            return held.enter_context(nc.sbuf_tensor(name, shape, dt))
        k = Names(
            dram=d, scratch=nc.dram_tensor("scratch", (BATCH, SEQ), F32, kind="Internal").ap(),
            psum_all=held.enter_context(nc.psum_tensor("psum_all", [P, 8 * CHUNK], F32)),
            x=sb("x", [P, TILES, P]), xn=sb("xn", [P, TILES, P]), xnT=sb("xnT", [P, TOKENS]), ident=sb("ident", [P, P]),
            stats=sb("stats", [P, TILES, 6]), moments=sb("moments", [P, TILES, 2]), rstd=sb("rstd", [P, TILES]), rms=sb("rms", [P, TILES]),
            logits=sb("logits", [16, SEQ]), logit_max=sb("logit_max", [16, 1]), neg_a=sb("neg_a", [16, 1]), floor_m=sb("floor_m", [16, 1]),
            logk=sb("logk", [16, 1]), route_arg=sb("route_arg", [16, SEQ]), route_exp=sb("route_exp", [16, SEQ]),
            route_sum=sb("route_sum", [16, 1]), route_log=sb("route_log", [16, 1]), route_cols=sb("route_cols", [P, 2, SUB, 16]),
            rank=sb("rank", [P, 2, TILES]), route_w=sb("route_w", [P, 3, TILES]), route_b=sb("route_b", [P, 3, SEQS * SUB]),
            window_mask=sb("window_mask", [P, SUB, SEQ]), head16=sb("head16", [P, 8]), head8=sb("head8", [P, HEADS]),
            rot_cos=sb("rot_cos", [P, 2, SEQ]), rot_sin=sb("rot_sin", [P, 2, SEQ]),
            row_parts=sb("row_parts", [SPREAD_K, TOKENS], BF16), pick_row=sb("pick_row", [P, PART_ROWS], BF16),
            gate_rounded=sb("gate_rounded", [P, TILES, 8], BF16), gate=sb("gate", [P, TILES, 8]), gate_sum=sb("gate_sum", [P, TILES]),
            gate_rank=sb("gate_rank", [P, TILES, 8]), gate_cmp=sb("gate_cmp", [P, 8, TILES, 8]), y_chunk=sb("y_chunk", [P, CHUNK]))
        k.psum = [k.psum_all[:, CHUNK * i:CHUNK * (i + 1)] for i in range(8)]
        with ExitStack() as attn:
            def sa(name, shape):
                return attn.enter_context(nc.sbuf_tensor(name, shape, F32))
            k.xb = sa("xb", [P, 2, 2, SEQ])
            k.keys = sa("keys", [P, HEADS, SEQ])
            k.gate_split = k.keys[:, 0:TILES * SPREAD_K // SEQ, :].rearrange("p h n -> p (h n)")\
                .rearrange("p (t a e) -> p t a e", t=TILES, a=PARTS)
            k.queryT = sa("queryT", [P, PAIRS, SEQ])
            k.values = sa("values", [P, 2, SUB, HEADS * HD])
            k.norm8 = k.values[:, 0, 0, :].rearrange("p (t n) -> p t n", n=P)
            k.probs = sa("probs", [P, PBUF, SUB, SEQ])
            k.probsT = sa("probsT", [P, 3, SUB, SEQ])
            k.outT = sa("outT", [P, 2, PAIRS, SEQ])
            k.yT = sa("yT", [P, 2, SEQ])
            k.masked_scores = sa("masked_scores", [P, 2, SUB, SEQ])
            k.negmax = sa("negmax", [P, HEADS, SUB])
            k.null_scores = sa("null_scores_sb", [P, 2, 2 * SUB])
            k.key_negmax = sa("key_negmax", [P, SUB])
            k.prob_sum = sa("prob_sum", [P, HEADS, SUB])
            k.recip = sa("recip", [P, HEADS, SUB])
            k.null_arg = sa("null_arg", [P, PAIRS, SUB])
            k.null_exp = sa("null_exp", [P, PAIRS, SUB])
            k.null_probs = sa("null_probs", [P, SUB, PAIRS])
            k.null_probsT = sa("null_probsT", [P, SEQ])
            k.mix = sa("mix", [P, SUB, P])
            k.rot = sa("rot", [P, 2, 2, SEQ])
            k.rot2 = sa("rot2", [P, 2, SEQ])
            layer0(nc, k, d)
            if layers > 1:
                layer1(nc, k, d)
            if layers > 2:
                layer2(nc, k, d)
        if layers > 3:
            layer3(nc, k, d)
        store_stage(nc, k, out)


def rows_first(a, n):
    return a.reshape(n, P, -1).transpose(1, 0, 2)


def lay_out(i):
    z = np.zeros
    f = np.float32
    a = {}
    a["x"] = i["L0_attn_z"]
    a["ident"] = np.eye(P, dtype=f)
    a["cols"] = np.stack([i["L0_ffn_ln_g"], i["L0_ffn_ln_b"], i["L0_ffn_rms_g"]], 1)
    a["inT"] = np.stack([i[f"L0_attn_{n}"].T for n in ("wq", "wk", "wv")], 1)
    a["fc"] = np.stack([i[f"L0_attn_{n}"] for n in ("fcq_w", "fck_w", "fcv_w")], 1)
    a["qbias"] = i["L0_attn_fcq_b"].reshape(PAIRS, P).T
    a["kbias"] = i["L0_attn_fck_b"].reshape(PAIRS, P).T
    a["vbias"] = i["L0_attn_fcv_b"]
    a["obias0"] = i["L0_attn_fco_b"].reshape(P, 1)
    a["wo0"] = rows_first(i["L0_attn_fco_w"], PAIRS)
    a["qkv_l"] = i["L0_ffn_w_qkv_l"].reshape(P, 3, 512)
    kv = i["L0_ffn_w_kv_h"]
    a["qkv_h"] = np.stack([i["L0_ffn_w_q_h"], kv[:, :, :HD].reshape(P, 512), kv[:, :, HD:].reshape(P, 512)], 1)
    a["wo_l"] = rows_first(i["L0_ffn_w_out_l"], 4)
    a["wo_h"] = rows_first(i["L0_ffn_w_out_h"], 4)
    nk, nv = i["L0_ffn_null_kv"]
    null_k, null_v = z((P, 4, 2), f), z((P, 4, 8), f)
    for h in range(PAIRS):
        rows = slice(HD * (h % 2), HD * (h % 2 + 1))
        null_k[rows, h // 2, h % 2] = nk[h]
        null_v[rows, h // 2, h] = nv[h]
    a["null_k"], a["null_v"] = null_k, null_v
    a["null_q"] = i["L0_ffn_null_q"]
    rt = z((P, BATCH, 16), f)
    for b in range(BATCH):
        rt[:, b, b] = i["L0_ffn_rt_q"][0]
        rt[:, b, BATCH + b] = i["L0_ffn_rt_kv"][0]
    a["route_tokens"] = rt
    a["logk"] = np.log(np.array([[KQ]] * BATCH + [[KKV]] * BATCH, f))
    token = np.arange(SEQ)
    mine = (np.arange(P)[:, None, None] + P * np.arange(SUB)[None, :, None])
    a["window_mask"] = np.where(abs(mine // 64 - token // 64) <= 1, 0.0, -3e38).astype(f)
    a["earlier"] = (token < mine).astype(f)
    r = np.arange(P)
    a["head16"] = (r[:, None] // L1_FD == np.arange(8)).astype(f)
    a["head8"] = (r[:, None] // L2_D == np.arange(HEADS)).astype(f)
    inv = (f(1.0) / f(10000.0) ** (np.arange(0, L2_D, 2, dtype=f) / f(L2_D))).astype(f)
    angle = (token.astype(f)[None, :] * inv[r % L2_D % 4][:, None]).astype(f)
    sign = np.where(r % L2_D < 4, -1.0, 1.0)[:, None]
    scale = np.array([L2_D ** -0.5, 1.0])[None, :, None]
    a["rot_cos"] = (np.cos(angle.astype(np.float64))[:, None, :] * scale).astype(f)
    a["rot_sin"] = ((sign * np.sin(angle.astype(np.float64)))[:, None, :] * scale).astype(f)
    for n, m in (("w_q1", "Wq"), ("w_k1", "Wk"), ("w_k_enc1", "Wk_enc"), ("w_v1", "Wv"), ("w_v_enc1", "Wv_enc")):
        a[n] = i[f"L1_attn_{m}"].T
    a["w_out1"] = rows_first(i["L1_attn_Wout"].T, PAIRS)
    a["router1"] = i["L1_ffn_w_router"].T
    a["w1_1"] = i["L1_ffn_w1"].transpose(1, 0, 2).reshape(P, -1)
    a["w3_1"] = i["L1_ffn_w3"].transpose(1, 0, 2).reshape(P, -1)
    a["w2_1"] = rows_first(i["L1_ffn_w2"].reshape(-1, P), L1_HC)
    a["expert_of"] = (np.arange(L1_E * L1_H)[None, :] // L1_H == r[:SPREAD_K, None] % PART_ROWS).astype(f)
    a["pick_row"] = (np.arange(PART_ROWS)[None, :] == r[:, None] % PART_ROWS).astype(f)
    c = np.arange(P)
    tri = (c[None, :] >= r[:, None]).astype(f)
    a["causal"] = np.concatenate([tri, np.ones((P, P), f), tri], 1)
    a["ones"] = np.ones((P, HD), f)
    w = i["L2_attn_w_qkv"].reshape(3, HEADS, L2_D, P)
    straight, swapped = [0, 2, 4, 6, 1, 3, 5, 7], [1, 3, 5, 7, 0, 2, 4, 6]
    a["w_rot"] = np.stack([w[n][:, order].reshape(P, P).T for order in (straight, swapped) for n in (0, 1)], 1)
    a["w_v2"] = w[2].reshape(P, P).T
    wo = z((4, 32, 4, P), f)
    wo[:, :L2_D] = i["L2_attn_w_proj"].T.reshape(4, 4, L2_D, P).transpose(1, 2, 0, 3)
    a["wo2"] = wo.reshape(P, 4, P)
    a["obias2"] = i["L2_attn_b_proj"].reshape(P, 1)
    a["router2"] = i["L2_ffn_Wr"]
    a["w1_2"] = i["L2_ffn_W1"].transpose(1, 0, 2).reshape(P, -1)
    a["w2_2"] = rows_first(i["L2_ffn_W2"].reshape(-1, P), L2_E * L2_FC)
    a["w_in3"] = i["L3_attn_W_in"].T
    a["conv_w"] = i["L3_attn_conv_w"].reshape(L3_DC, P, L3_CONV).transpose(1, 0, 2)
    w_x = rows_first(i["L3_attn_W_x"].T, L3_DC)
    a["w_x"] = np.concatenate([w_x[:, :, :2 * L3_N]] * PARTS + [w_x[:, :, 2 * L3_N:]], 2)
    a["a_log"] = rows_first(i["L3_attn_A_log"], L3_DC)
    w_dt = z((P, L3_DC, P), f)
    w_dt[SPREAD_K] = i["L3_attn_W_dt"].reshape(L3_DC, P)
    a["w_dt"] = w_dt
    for n, m in (("conv_b", "conv_b"), ("d_skip", "D_param"), ("b_dt", "b_dt")):
        a[n] = i[f"L3_attn_{m}"].reshape(L3_DC, P).T
    a["w_out3"] = rows_first(i["L3_attn_W_out"].T, L3_DC)
    a["codes"] = i["L3_ffn_qweights"].transpose(1, 0, 2)
    a["scales"] = i["L3_ffn_scales"].transpose(1, 0, 2).reshape(P, -1)
    a["lora_a"] = i["L3_ffn_lora_a"].transpose(1, 0, 2)
    a["lora_b"] = i["L3_ffn_lora_b"].transpose(2, 0, 1)
    a["gamma"], a["beta"] = i["L3_ffn_ln_gamma"].T, i["L3_ffn_ln_beta"].T
    a["bias_rows"] = i["L3_ffn_biases"][0::2].reshape(-1)
    a["bias_cols"] = i["L3_ffn_biases"][1::2].T
    return {n: np.ascontiguousarray(v) for n, v in a.items()}


def kernel(**inputs):
    import concourse.bacc as bacc
    from concourse.bass_utils import run_bass_kernel_spmd

    nc = bacc.Bacc("TRN2", target_bir_lowering=False, num_devices=1)
    arrays = lay_out({n: np.asarray(v) for n, v in inputs.items()})
    d = {n: nc.dram_tensor(n + "_dram", v.shape, mybir.dt.from_np(v.dtype), kind="ExternalInput").ap() for n, v in arrays.items()}
    d["x"] = d["x"].rearrange("b (s p) n -> p (b s) n", p=P)
    out = nc.dram_tensor("out_dram", (BATCH, SEQ, DIM), F32, kind="ExternalOutput").ap()
    build(nc, d, out.rearrange("b (s p) n -> p (b s) n", p=P))
    r = run_bass_kernel_spmd(nc, [{n + "_dram": v for n, v in arrays.items()}], core_ids=[0])
    return r.results[0]["out_dram"]
```
